# Optimizing a Trainium2 kernel written in Bass

```python
import numpy as np
import jax
import jax.numpy as jnp

def _softmax(x, axis=-1):
    return jax.nn.softmax(x, axis=axis)

def _gelu(x):
    return jax.nn.gelu(x, approximate=True)

def _silu(x):
    return jax.nn.silu(x)

def _sigmoid(x):
    return jax.nn.sigmoid(x)

def _layernorm(x, axis=-1, eps=1e-05):
    m = jnp.mean(x, axis=axis, keepdims=True)
    v = jnp.var(x, axis=axis, keepdims=True)
    return (x - m) / jnp.sqrt(v + eps)

def _scatter_add(tgt, idx, src, axis=0):
    return tgt.at[idx].add(src)

def _segment_sum(src, seg, n):
    return jax.ops.segment_sum(src, seg, n)
kernel_name = 'mk_gnn_ffn_d2_gnn_r16_3b7cc6'

def setup_inputs(seed: int=0):
    np.random.seed(seed)
    _w = jnp.asarray

    def _rec_inputs():
        import jax
        import jax.numpy as jnp
        _gk = jax.random.key(seed)
        x = -0.0003713 + 1 * jax.random.normal(jax.random.fold_in(_gk, 1), (6250, 256), jnp.float32)
        src = jax.random.randint(jax.random.fold_in(_gk, 2), (100000,), 0, 6250, jnp.int32)
        dst = jax.random.randint(jax.random.fold_in(_gk, 3), (100000,), 0, 6250, jnp.int32)
        _o = jnp.argsort(dst, stable=True)
        src = src[_o]
        dst = dst[_o]
        edge_type_16 = jax.random.randint(jax.random.fold_in(_gk, 13), (100000,), 0, 16, jnp.int32)
        edge_weight1 = jax.random.uniform(jax.random.fold_in(_gk, 14), (100000, 1), jnp.float32, 0.0, 0.999998)
        return (x, src, dst, edge_type_16, edge_weight1)
    x, src, dst, edge_type_16, edge_weight1 = _rec_inputs()

    def _L0_gnn_setup():
        import jax, jax.numpy as jnp
        import numpy as np
        N_NODES = 3125
        N_EDGES = 100000
        H_SIZE = 256
        HEADS = 8
        HEAD_DIM = H_SIZE // HEADS
        NEG_SLOPE = 0.2
        key = jax.random.key(seed)
        k_x, k_e, k_w, k_as, k_ad, k_b = jax.random.split(key, 6)
        x = jax.random.normal(k_x, (N_NODES, H_SIZE), dtype=jnp.float32)
        edge_index = jax.random.randint(k_e, (2, N_EDGES), 0, N_NODES, dtype=jnp.int64)
        scale = 1.0 / np.sqrt(H_SIZE)
        W = jax.random.normal(k_w, (H_SIZE, HEADS, HEAD_DIM), dtype=jnp.float32) * scale
        att_src = jax.random.normal(k_as, (HEADS, HEAD_DIM), dtype=jnp.float32) * scale
        att_dst = jax.random.normal(k_ad, (HEADS, HEAD_DIM), dtype=jnp.float32) * scale
        bias = jnp.zeros((H_SIZE,), dtype=jnp.float32)
        return {'x': x, 'edge_index': edge_index, 'W': W, 'att_src': att_src, 'att_dst': att_dst, 'bias': bias}
    _L0_gnn_all = _L0_gnn_setup()
    _L0_gnn_in = {k: v for k, v in _L0_gnn_all.items() if k in ('W', 'att_src', 'att_dst', 'bias')}
    del _L0_gnn_all

    def _L0_ffn_setup():
        import jax, jax.numpy as jnp
        import numpy as np
        B, K, D = (512, 16, 256)
        E = 32
        H = int(D * 0.25)
        key = jax.random.key(seed)
        ks = jax.random.split(key, 7)
        d_rs = D ** (-0.5)
        h_rs = H ** (-0.5)
        x = jax.random.normal(ks[0], (B, K, D), dtype=jnp.float32)
        router_w = jax.random.uniform(ks[1], (E, D), jnp.float32, -d_rs, d_rs)
        router_b = jax.random.uniform(ks[2], (E,), jnp.float32, -d_rs, d_rs)
        W1 = jax.random.uniform(ks[3], (E, D, H), jnp.float32, -h_rs, h_rs)
        b1 = jax.random.uniform(ks[4], (E, H), jnp.float32, -h_rs, h_rs)
        W2 = jax.random.uniform(ks[5], (E, H, D), jnp.float32, -d_rs, d_rs)
        b2 = jax.random.uniform(ks[6], (E, D), jnp.float32, -d_rs, d_rs)
        return {'x': x, 'router_w': router_w, 'router_b': router_b, 'W1': W1, 'b1': b1, 'W2': W2, 'b2': b2}
    _L0_ffn_all = _L0_ffn_setup()
    _L0_ffn_in = {k: v for k, v in _L0_ffn_all.items() if k in ('router_w', 'router_b', 'W1', 'b1', 'W2', 'b2')}
    del _L0_ffn_all

    def _L1_gnn_setup():
        import jax, jax.numpy as jnp
        import numpy as np
        N_NODES = 1250
        N_EDGES = 20000
        NUM_RELS = 16
        IN_FEAT = 256
        OUT_FEAT = 256
        key = jax.random.key(seed)
        k_h, k_w, k_n, k_s, k_d, k_r = jax.random.split(key, 6)
        h = jax.random.normal(k_h, (N_NODES, IN_FEAT), dtype=jnp.float32)
        weight = jax.random.normal(k_w, (NUM_RELS, IN_FEAT, OUT_FEAT), dtype=jnp.float32)
        norm = jax.random.uniform(k_n, (N_EDGES, 1), dtype=jnp.float32)
        src = jax.random.randint(k_s, (N_EDGES,), 0, N_NODES, dtype=jnp.int32)
        dst = jax.random.randint(k_d, (N_EDGES,), 0, N_NODES, dtype=jnp.int32)
        rel_type = jax.random.randint(k_r, (N_EDGES,), 0, NUM_RELS, dtype=jnp.int32)
        return {'h': h, 'weight': weight, 'norm': norm, 'src': src, 'dst': dst, 'rel_type': rel_type}
    _L1_gnn_all = _L1_gnn_setup()
    _L1_gnn_in = {k: v for k, v in _L1_gnn_all.items() if k in ('weight',)}
    del _L1_gnn_all

    def _L1_ffn_setup():
        import math
        import jax, jax.numpy as jnp
        import numpy as np
        CAPACITY_FACTOR = 1.25
        TOP_K = 2
        LN_EPS = 1e-05

        def _layer_norm(x, gamma, beta):
            mu = jnp.mean(x, axis=-1, keepdims=True)
            var = jnp.var(x, axis=-1, keepdims=True)
            return (x - mu) * jax.lax.rsqrt(var + LN_EPS) * gamma + beta
        key = jax.random.key(seed)
        ks = jax.random.split(key, 4)
        B, S, D, F, E = (8, 256, 256, 512, 8)
        x = jax.random.normal(ks[0], (B, S, D), dtype=jnp.float32)
        Wr = jax.random.normal(ks[1], (D, E), dtype=jnp.float32) / np.sqrt(D)
        br = jnp.zeros((E,), jnp.float32)
        W1 = jax.random.normal(ks[2], (E, D, F), dtype=jnp.float32) / np.sqrt(D)
        b1 = jnp.zeros((E, F), jnp.float32)
        W2 = jax.random.normal(ks[3], (E, F, D), dtype=jnp.float32) / np.sqrt(F)
        b2 = jnp.zeros((E, D), jnp.float32)
        gamma = jnp.ones((D,), jnp.float32)
        beta = jnp.zeros((D,), jnp.float32)
        return {'x': x, 'Wr': Wr, 'br': br, 'W1': W1, 'b1': b1, 'W2': W2, 'b2': b2, 'gamma': gamma, 'beta': beta}
    _L1_ffn_all = _L1_ffn_setup()
    _L1_ffn_in = {k: v for k, v in _L1_ffn_all.items() if k in ('Wr', 'br', 'W1', 'b1', 'W2', 'b2', 'gamma', 'beta')}
    del _L1_ffn_all
    return {'x': x, 'src': src, 'dst': dst, 'edge_type_16': edge_type_16, 'edge_weight1': edge_weight1, 'L0_gnn_W': _L0_gnn_in['W'], 'L0_gnn_att_src': _L0_gnn_in['att_src'], 'L0_gnn_att_dst': _L0_gnn_in['att_dst'], 'L0_gnn_bias': _L0_gnn_in['bias'], 'L0_ffn_router_w': _L0_ffn_in['router_w'], 'L0_ffn_router_b': _L0_ffn_in['router_b'], 'L0_ffn_W1': _L0_ffn_in['W1'], 'L0_ffn_b1': _L0_ffn_in['b1'], 'L0_ffn_W2': _L0_ffn_in['W2'], 'L0_ffn_b2': _L0_ffn_in['b2'], 'L1_gnn_weight': _L1_gnn_in['weight'], 'L1_ffn_Wr': _L1_ffn_in['Wr'], 'L1_ffn_br': _L1_ffn_in['br'], 'L1_ffn_W1': _L1_ffn_in['W1'], 'L1_ffn_b1': _L1_ffn_in['b1'], 'L1_ffn_W2': _L1_ffn_in['W2'], 'L1_ffn_b2': _L1_ffn_in['b2'], 'L1_ffn_gamma': _L1_ffn_in['gamma'], 'L1_ffn_beta': _L1_ffn_in['beta']}

def reference(x, src, dst, edge_type_16, edge_weight1, L0_gnn_W, L0_gnn_att_src, L0_gnn_att_dst, L0_gnn_bias, L0_ffn_router_w, L0_ffn_router_b, L0_ffn_W1, L0_ffn_b1, L0_ffn_W2, L0_ffn_b2, L1_gnn_weight, L1_ffn_Wr, L1_ffn_br, L1_ffn_W1, L1_ffn_b1, L1_ffn_W2, L1_ffn_b2, L1_ffn_gamma, L1_ffn_beta):
    import jax
    import jax.numpy as jnp

    def _L0_gnn_ref(x, edge_index, W, att_src, att_dst, bias):
        import jax, jax.numpy as jnp
        import numpy as np
        N_NODES = 3125
        N_EDGES = 100000
        H_SIZE = 256
        HEADS = 8
        HEAD_DIM = H_SIZE // HEADS
        NEG_SLOPE = 0.2
        'GATConv (concat heads) -> relu -> dropout(eval=identity).\n\n            x: [N, F]; edge_index: [2, E] with (src=row0, dst=row1) meaning message j->i.\n            '
        N = x.shape[0]
        h = jnp.einsum('nf,fhd->nhd', x, W)
        a_src = jnp.sum(h * att_src, axis=-1)
        a_dst = jnp.sum(h * att_dst, axis=-1)
        src = edge_index[0]
        dst = edge_index[1]
        e = jax.nn.leaky_relu(a_src[src] + a_dst[dst], NEG_SLOPE)
        e_max = jax.ops.segment_max(e, dst, num_segments=N)
        e_exp = jnp.exp(e - e_max[dst])
        denom = jax.ops.segment_sum(e_exp, dst, num_segments=N)
        alpha = e_exp / (denom[dst] + 1e-16)
        msg = h[src] * alpha[:, :, None]
        out = jax.ops.segment_sum(msg, dst, num_segments=N)
        out = out.reshape(N, -1) + bias
        return jax.nn.relu(out)

    def _L0_ffn_ref(x, router_w, router_b, W1, b1, W2, b2):
        import jax, jax.numpy as jnp
        import numpy as np
        B, K, D = (512, 16, 256)
        E = 32
        H = int(D * 0.25)
        xf = x.reshape(-1, D)
        logits = xf @ router_w.T + router_b
        idx = jnp.argmax(logits, axis=-1)
        w1t = jnp.take(W1, idx, axis=0)
        h = jnp.einsum('nd,ndh->nh', xf, w1t) + jnp.take(b1, idx, axis=0)
        h = jax.nn.relu(h)
        w2t = jnp.take(W2, idx, axis=0)
        out = jnp.einsum('nh,nhd->nd', h, w2t) + jnp.take(b2, idx, axis=0)
        out = jax.nn.relu(out)
        return out.reshape(x.shape)

    def _L1_gnn_ref(h, weight, norm, src, dst, rel_type):
        import jax, jax.numpy as jnp
        import numpy as np
        N_NODES = 1250
        N_EDGES = 20000
        NUM_RELS = 16
        IN_FEAT = 256
        OUT_FEAT = 256
        transformed = jnp.einsum('ni,rio->rno', h, weight)
        msg = transformed[rel_type, src] * norm
        out = jax.ops.segment_sum(msg, dst, num_segments=h.shape[0])
        return out

    def _L1_ffn_ref(x, Wr, br, W1, b1, W2, b2, gamma, beta):
        import math
        import jax, jax.numpy as jnp
        import numpy as np
        CAPACITY_FACTOR = 1.25
        TOP_K = 2
        LN_EPS = 1e-05

        def _layer_norm(x, gamma, beta):
            mu = jnp.mean(x, axis=-1, keepdims=True)
            var = jnp.var(x, axis=-1, keepdims=True)
            return (x - mu) * jax.lax.rsqrt(var + LN_EPS) * gamma + beta
        B, S, D = x.shape
        E = Wr.shape[1]
        N = B * S
        K = TOP_K
        logits = jnp.mean(x, axis=1) @ Wr + br
        routing_weights = jax.nn.softmax(logits, axis=-1)
        capacity = float(math.ceil(N * CAPACITY_FACTOR / E))
        expected_loads = routing_weights.sum(axis=0) * (N / B)
        scale = jnp.where(expected_loads > capacity, capacity / expected_loads, 1.0)
        routing_weights = jax.nn.softmax(routing_weights * scale, axis=-1)
        rw_tok = jnp.broadcast_to(routing_weights[:, None, :], (B, S, E)).reshape(N, E)
        top_w, top_i = jax.lax.top_k(rw_tok, K)
        top_w = jax.nn.softmax(top_w, axis=-1)
        xf = x.reshape(N, D)
        h = jax.nn.gelu(jnp.einsum('nd,edf->enf', xf, W1) + b1[:, None, :], approximate=False)
        y = jnp.einsum('enf,efd->end', h, W2) + b2[:, None, :]
        w_dense = jnp.zeros((N, E), x.dtype).at[jnp.arange(N)[:, None], top_i].add(top_w)
        out = jnp.einsum('ne,end->nd', w_dense, y).reshape(B, S, D)
        out = _layer_norm(out + x, gamma, beta)
        return out
    edge_index = jnp.stack([src, dst])
    x = x + _L0_gnn_ref(_layernorm(x, axis=-1), edge_index, L0_gnn_W, L0_gnn_att_src, L0_gnn_att_dst, L0_gnn_bias)
    x = x + _L0_ffn_ref(_layernorm(x, axis=-1)[None], L0_ffn_router_w, L0_ffn_router_b, L0_ffn_W1, L0_ffn_b1, L0_ffn_W2, L0_ffn_b2)[0]
    x = x + _L1_gnn_ref(_layernorm(x, axis=-1), L1_gnn_weight, edge_weight1, src, dst, edge_type_16)
    x = x + _L1_ffn_ref(_layernorm(x, axis=-1)[None], L1_ffn_Wr, L1_ffn_br, L1_ffn_W1, L1_ffn_b1, L1_ffn_W2, L1_ffn_b2, L1_ffn_gamma, L1_ffn_beta)[0]
    return x

_drawn_inputs = setup_inputs


def setup_inputs(seed=0):
    import zlib

    import numpy as np

    out = dict(_drawn_inputs(seed))
    spreads = {'L0_gnn_bias': (0.0, 0.1),
     'L1_ffn_br': (0.0, 0.493),
     'L1_ffn_b1': (0.0, 2.0),
     'L1_ffn_b2': (0.0, 2.0),
     'L1_ffn_gamma': (1.0, 0.6),
     'L1_ffn_beta': (0.0, 2.0)}
    factors = {'L0_ffn_b1': 5.785, 'L1_ffn_Wr': 4.835, 'L1_ffn_W1': 5.496, 'L1_ffn_W2': 4.943}
    for name, (base, spread) in spreads.items():
        noise = np.random.default_rng([zlib.crc32(name.encode()), seed]).standard_normal(out[name].shape)
        drawn = base * np.exp(spread * noise) if base else spread * noise
        out[name] = jnp.asarray(drawn.astype(out[name].dtype))
    for name, factor in factors.items():
        out[name] = (out[name] * factor).astype(out[name].dtype)
    return out
```

```python
from contextlib import ExitStack, contextmanager

import concourse.bass as bass
import concourse.mybir as mybir

F32 = mybir.dt.float32
BF16 = mybir.dt.bfloat16
I32 = mybir.dt.int32
U32 = mybir.dt.uint32
ALU = mybir.AluOpType
ACT = mybir.ActivationFunctionType
AX = mybir.AxisListType.X

P = 128
N_NODES, N_EDGES, D = 6250, 100000, 256
NT = -(-N_NODES // P)
NP = NT * P
HEADS, HEAD_DIM = 8, 32
HW = HEAD_DIM + 1
HROW = HEADS * HW
RELS = 16
KD = D // P
EPS = 1e-5
C_ADST, C_START, C_DEG, C_ID, REC = D, D + HEADS, D + HEADS + 1, D + HEADS + 2, D + HEADS + 4
CHUNKS = -(-N_EDGES // P)
CG = -(-CHUNKS // P)
STRIP = CHUNKS
EP = P * STRIP
WIN = 32
SLICE = 23
SLICES = STRIP // SLICE
JCOL = 4
SLOTS = WIN // JCOL
DBINS = 64
E0, H0 = 32, 64
XCH = NT + E0 - 1
E1, H1 = 8, 512
CAPACITY = float(-(-N_NODES * 5 // (4 * E1)))
NEVER = -3e38
LOWEST = -1e38
U = 7
assert U * U == NT and SLICES * SLICE == STRIP


class Chain:

    def __init__(self, p, eng, sem):
        self.p, self.eng, self.sem, self.base, self.n = p, eng, sem, 0, 0

    def at(self, base):
        self.base, self.n = base, 0

    def total(self):
        return self.base + self.n

    def __call__(self, ins, alone=False):
        ins.then_inc(self.sem, 1)
        self.n += 1
        self.eng.wait_ge(self.sem, self.base + self.n)
        if alone:
            self.p.alone(self.eng)


def spread(ap, axis, shape):
    return ap.unsqueeze(axis).broadcast_to(shape)


class Program:
    def __init__(self, nc, ctx, a):
        self.nc, self.ctx, self.a = nc, ctx, a
        self.in_use = []
        self.bank = [ctx.enter_context(nc.psum_tensor(f"bank{i}", [P, 512], F32)) for i in range(8)]
        self.ident = self.keep("ident", [P, P], F32)
        self.ones = self.keep("ones", [P, P], F32)
        self.earlier = self.keep("earlier", [P, P], BF16)
        self.onesb = self.keep("onesb", [P, P], BF16)
        self.count = self.keep("count", [P, DBINS], F32)
        self.node = self.keep("node", [P, NT + 1], F32)
        self.rec = self.keep("rec", [P, NT, REC], F32)
        self.eps = self.keep("eps", [P, 1], F32)
        self.win = self.keep("win", [P, NT, 2 * WIN], F32)
        self.start_i = self.keep("start_i", [P, NT], I32)
        self.id_i = self.keep("id_i", [P, NT], I32)
        self.items = self.keep("items", [1, NT], I32)
        self.tails = self.keep("tails", [1, NT], I32)
        self.place_i = self.keep("place_i", [P, NT], I32)
        self.chunk_e_i = self.keep("chunk_e_i", [1, XCH], I32)
        self.two_i = self.keep("two_i", [1, 2], I32)
        self.two_w = self.keep("two_w", [P, 2], F32)
        self.passed = self.sem("passed")
        self.ready = self.sem("ready")
        self.h_table = nc.dram_tensor("h_table", (NP, HROW), F32, kind="Internal").ap()
        self.windows = nc.dram_tensor("windows", (EP, 2 * WIN), F32, kind="Internal").ap()
        self.records = nc.dram_tensor("records", (NP, REC), F32, kind="Internal").ap()
        self.x_grouped = nc.dram_tensor("x_grouped", (XCH * P, REC), F32, kind="Internal").ap()
        self.y_grouped = nc.dram_tensor("y_grouped", (XCH * P, D), F32, kind="Internal").ap()
        self.transformed = nc.dram_tensor("transformed", (NP * RELS, D), F32, kind="Internal").ap()

    def alone(self, eng):
        eng.sem_inc(self.passed, 1)

    def keep(self, name, shape, dt):
        return self.ctx.enter_context(self.nc.sbuf_tensor(name, shape, dt))

    def sem(self, name):
        self.in_use.append(self.nc.alloc_semaphore(name))
        return self.in_use[-1]

    @contextmanager
    def phase(self):
        kept, self.in_use = self.in_use, []
        with ExitStack() as ctx:
            yield ctx
        self.nc.all_engine_barrier()
        self.nc.clear_and_free_semaphores(self.in_use)
        self.nc.all_engine_barrier()
        self.in_use = kept


class Front:

    def __init__(self, p, ctx, name):
        nc = p.nc
        self.p = p
        self.xn = [ctx.enter_context(nc.sbuf_tensor(f"{name}_xn{u}", [P, D], F32)) for u in range(U)]
        self.xt = [ctx.enter_context(nc.sbuf_tensor(f"{name}_xt{u}", [P, D], F32)) for u in range(U)]
        self.stats = ctx.enter_context(nc.sbuf_tensor(f"{name}_stats", [P, U, 6], F32))
        self.ms = ctx.enter_context(nc.sbuf_tensor(f"{name}_ms", [P, U, 4], F32))
        self.varied, self.rooted, self.normed, self.turned, self.copied = (
            p.sem(f"{name}_{x}") for x in ("varied", "rooted", "normed", "turned", "copied"))

    def moments(self, dve, chain, x, g, u):
        chain(dve.bn_stats(self.stats[:, u, :], x), True)
        dve.bn_aggr(self.ms[:, u, 0:2], self.stats[:, u, :]).then_inc(self.varied, 1)

    def root(self, act, g, u):
        act.wait_ge(self.varied, done(g))
        act.activation(self.ms[:, u, 2:3], self.ms[:, u, 1:2], ACT.Sqrt, bias=self.p.eps[:, 0:1]).then_inc(self.rooted, 1)

    def norm(self, dve, chain, x, g, u, out=None):
        dve.wait_ge(self.rooted, done(g))
        chain(dve.reciprocal(self.ms[:, u, 3:4], self.ms[:, u, 2:3]))
        dve.wait_ge(self.turned, done(g - U))
        dve.tensor_scalar(self.xn[u][:] if out is None else out, x, self.ms[:, u, 0:1], self.ms[:, u, 3:4],
                          ALU.subtract, ALU.mult).then_inc(self.normed, 1)

    STEPS = 2

    def turn(self, pe, g, u):
        pe.wait_ge(self.normed, done(g))
        pe.wait_ge(self.copied, done(g - 3))
        for k in range(KD):
            ins = pe.transpose(self.p.bank[u % 4][:, k * P:(k + 1) * P], self.xn[u][:, k * P:(k + 1) * P], self.p.ident[:])
        ins.then_inc(self.turned, 1)

    def copy(self, act, g, u, used):
        if used is not None:
            act.wait_ge(used, done(g - U))
        act.wait_ge(self.turned, done(g))
        act.activation(self.xt[u][:], self.p.bank[u % 4][:, 0:D], ACT.Copy).then_inc(self.copied, 1)

    def start(self, eng, *sems):
        for s in sems:
            eng.sem_inc(s, U)

    def scalar_loop(self, act, used):
        self.start(act, self.rooted, self.copied)
        with act.Fori(0, U) as i:
            self.root(act, i * U, 0)
            for u in range(U):
                if u + 1 < U:
                    self.root(act, i * U + (u + 1), u + 1)
                self.copy(act, i * U + u, u, used)


def done(g):
    return g + (1 + U)


def rank_steps(dve, chain, hot, within, total, cum, base, tmp, rank, nb, align=None):
    chain(dve.memset(cum[:, 0, :], 0.0))
    for t in range(NT):
        chain(dve.tensor_tensor(cum[:, t + 1, :], cum[:, t, :], total[:, t, :], ALU.add))
    size, ends, part = base[:, 0, :], base[:, 1, :], base[:, 2, :]
    if align is not None:
        bits = P.bit_length() - 1
        chain(dve.tensor_scalar(align, cum[:, NT, :], float(P - 1), None, ALU.add))
        chain(dve.tensor_scalar(align, align, bits, bits, ALU.arith_shift_right, ALU.logical_shift_left))
        chain(dve.tensor_copy(size, align))
    else:
        chain(dve.tensor_copy(size, cum[:, NT, :]))
    chain(dve.memset(part, 0.0))
    chain(dve.tensor_tensor_scan(ends, size, part, 0.0, ALU.add, ALU.add))
    chain(dve.tensor_tensor(part, ends, size, ALU.subtract))
    chain(dve.tensor_tensor(tmp, within, cum[:, 0:NT, :], ALU.add))
    chain(dve.tensor_tensor(tmp, tmp, spread(part, 1, [P, NT, nb]), ALU.add))
    chain(dve.tensor_tensor(tmp, tmp, hot, ALU.mult))
    chain(dve.tensor_reduce(rank, tmp, AX, ALU.add))


def search_and_project(p: Program):
    nc, a = p.nc, p.a
    with p.phase() as ctx:
        def sb(n, s, d):
            return ctx.enter_context(nc.sbuf_tensor(n, s, d))

        xa = sb("xa", [P, NT, REC], F32)
        dst_rows = sb("dst_rows", [P, CG, P], I32)
        first = sb("first", [P, CG], F32)
        diag = sb("diag", [P, 2, P], F32)
        pivots = sb("pivots", [P, CG * P], F32)
        less = sb("less", [P, CG * P], BF16)
        chunks_below = sb("chunks_below", [P, NT + 1], F32)
        chunk = sb("chunk", [P, NT + 1], F32)
        chunk_i = sb("chunk_i", [P, NT + 1], I32)
        found = sb("found", [P, NT + 1, P], I32)
        start = sb("start", [P, NT + 1], F32)
        bin_ = sb("bin_", [P, NT], F32)
        hot = sb("hot", [P, NT, DBINS], BF16)
        scratch = p.rec[:].rearrange("q t c -> q (t c)")
        within, total, cum = (scratch[:, n * NT * DBINS:(n * NT + m) * DBINS].rearrange("q (t b) -> q t b", b=DBINS)
                              for n, m in ((0, NT), (1, NT), (2, NT + 1)))
        cmp = scratch[:, (3 * NT + 1) * DBINS:(3 * NT + 1) * DBINS + (NT + 1) * P // 2].bitcast(BF16)\
            .rearrange("q (t e) -> q t e", e=P)
        base = sb("base", [P, 3, DBINS], F32)
        rank = sb("rank", [P, NT], F32)
        rank_i = sb("rank_i", [P, NT], I32)
        shift = sb("shift", [P, 2, P], F32)
        s_src = sb("s_src", [P, STRIP + WIN], I32)
        s_typ = sb("s_typ", [P, STRIP + WIN], I32)
        s_key = sb("s_key", [P, STRIP + WIN], F32)
        s_wgt = sb("s_wgt", [P, STRIP + WIN], F32)
        w = SLICE * 2 * WIN
        wide = [p.win[:].rearrange("q t c -> q (t c)")[:, i * w:(i + 1) * w].rearrange("q (e c) -> q e c", c=2 * WIN) for i in range(2)]
        wa = sb("wa", [P, KD, HROW + HEADS], F32)
        att = sb("att", [P, 2, D], F32)
        prod = sb("prod", [P, D], F32)
        front = Front(p, ctx, "gat")
        hrow = [sb(f"hrow{i}", [P, HROW], F32) for i in range(U)]

        dst_in, x_in, w_in, att_in, edge_in = (p.sem(x) for x in ("dst_in", "x_in", "w_in", "att_in", "edge_in"))
        first_ready, pivots_ready, chunks_ready, found_in = (p.sem(x) for x in ("first_ready", "pivots_ready", "chunks_ready", "found_in"))
        diag_ready, piv_done = p.sem("diag_ready"), p.sem("piv_done")
        start_ready, next_done, hot_ready, counts_done, counts_out = (p.sem(x) for x in ("start_ready", "next_done", "hot_ready", "counts_done", "counts_out"))
        rank_ready, scattered, rec_in = p.sem("rank_ready"), p.sem("scattered"), p.sem("rec_in")
        key_ready, wide_key, wide_wgt, wide_out = p.sem("key_ready"), p.sem("wide_key"), p.sem("wide_wgt"), [p.sem(f"wide_out{i}") for i in range(2)]
        wa_ready, h_psum, h_ready = (p.sem(x) for x in ("wa_ready", "h_psum", "h_ready"))
        h_stored = [p.sem(f"h_stored{i}") for i in range(U)]
        steps_v, steps_g = p.sem("steps_v"), p.sem("steps_g")
        zero_out = p.sem("zero_out")
        halves = [(0, 4), (4, 7)]
        block = ctx.enter_context(nc.Block())

        @block.sync
        def _(sp):
            sp.dma_start(dst_rows[:], a["dst"].rearrange("(g c e) -> c g e", c=P, e=P)).then_inc(dst_in, 16)
            for s, v in ((s_src, a["src"]), (s_typ, a["edge_type_16"]), (s_wgt, a["edge_weight1"])):
                strips = bass.AP(tensor=v.tensor, offset=0, ap=[[STRIP, P], [1, STRIP + WIN]])
                sp.dma_start(s[:], strips).then_inc(edge_in, 16)
            for i, n in enumerate(("L0_gnn_att_src", "L0_gnn_att_dst")):
                flat = a[n].rearrange("h d -> (h d)")
                sp.dma_start(att[:, i, :], bass.AP(tensor=flat.tensor, offset=0, ap=[[0, P], [1, D]])).then_inc(att_in, 16)
            for k in range(KD):
                sp.dma_start(wa[:, k, 0:HROW].rearrange("p (h c) -> p h c", c=HW)[:, :, 0:HEAD_DIM],
                             a["L0_gnn_W"][k * P:(k + 1) * P]).then_inc(w_in, 16)
            sp.dma_start(xa[:, :, 0:D], a["x"].rearrange("(t q) d -> q t d", q=P)).then_inc(x_in, 16)
            for q in range(SLICES):
                sp.wait_ge(wide_key, q + 1)
                sp.wait_ge(wide_wgt, q + 1)
                sp.dma_start(p.windows.rearrange("(q e) w -> q e w", q=P)[:, q * SLICE:(q + 1) * SLICE, :],
                             wide[q % 2]).then_inc(wide_out[q % 2], 16)
            rows = p.h_table.rearrange("(t q) c -> t q c", q=P)
            for u in range(U):
                sp.sem_inc(h_stored[u], 16)
            with sp.Fori(0, U) as i:
                for u in range(U):
                    sp.wait_ge(h_ready, done(i * U + u))
                    sp.dma_start(rows[bass.ds(i * U + u, 1)].rearrange("o q c -> (o q) c"), hrow[u][:]).then_inc(h_stored[u], 16)
            for u in range(U):
                sp.wait_ge(h_stored[u], 16 * (U + 1))
            for i in range(2):
                sp.wait_ge(wide_out[i], 16 * ((SLICES + 1 - i) // 2))
            sp.wait_ge(scattered, 16 * NT)
            sp.dma_start(p.rec[:], p.records.rearrange("(t q) c -> q t c", q=P)).then_inc(rec_in, 16)
            sp.wait_ge(rec_in, 16)

        @block.gpsimd
        def _(pool):
            chain = Chain(p, pool, steps_g)
            chain(pool.memset(p.ident[:], 0.0))
            chain(pool.memset(p.ones[:], 1.0))
            chain(pool.memset(p.onesb[:], 1.0))
            chain(pool.memset(shift[:], 0.0))
            chain(pool.memset(p.eps[:], EPS))
            chain(pool.memset(p.earlier[:], 1.0))
            chain(pool.affine_select(out=p.ident[:], in_=p.ident[:], compare_op=ALU.not_equal, fill=1.0, base=0,
                                     pattern=[[-1, P]], channel_multiplier=1))
            chain(pool.affine_select(out=p.earlier[:], in_=p.earlier[:], compare_op=ALU.is_ge, fill=0.0, base=-1,
                                     pattern=[[1, P]], channel_multiplier=-1))
            chain(pool.affine_select(out=shift[:, 0, :], in_=shift[:, 0, :], compare_op=ALU.not_equal, fill=1.0, base=-1,
                                     pattern=[[-1, P]], channel_multiplier=1))
            chain(pool.affine_select(out=shift[:, 1, :], in_=shift[:, 1, :], compare_op=ALU.not_equal, fill=1.0, base=P - 1,
                                     pattern=[[-1, P]], channel_multiplier=P))
            chain(pool.iota(p.count[:], pattern=[[1, DBINS]], base=0, channel_multiplier=0,
                            allow_small_or_imprecise_dtypes=True))
            chain(pool.iota(p.node[:], pattern=[[P, NT + 1]], base=0, channel_multiplier=1,
                            allow_small_or_imprecise_dtypes=True))
            pool.memset(xa[:, :, D:REC], 0.0).then_inc(p.ready, 1)
            pool.wait_ge(p.ready, 1)
            pool.wait_ge(edge_in, 48)
            pool.wait_ge(chunks_ready, 1)
            table = a["dst"].rearrange("(c e) -> c e", e=P)
            for t in range(NT + 1):
                pool.indirect_dma_start(out=found[:, t, :], out_offset=None, in_=table,
                                        in_offset=bass.IndirectOffsetOnAxis(ap=chunk_i[:, t:t + 1], axis=0)).then_inc(found_in, 16)
            for q in range(SLICES):
                if q >= 2:
                    pool.wait_ge(wide_out[q % 2], 16 * (q // 2))
                over = bass.AP(tensor=s_wgt[:].tensor, offset=q * SLICE, ap=[[STRIP + WIN, P], [1, SLICE], [1, WIN]])
                pool.tensor_copy(wide[q % 2][:, :, WIN:2 * WIN], over).then_inc(wide_wgt, 1)
            pool.wait_ge(rank_ready, 1)
            pool.wait_ge(h_ready, done(NT - 1))
            for t in range(NT):
                pool.indirect_dma_start(out=p.records[:], out_offset=bass.IndirectOffsetOnAxis(ap=rank_i[:, t:t + 1], axis=0),
                                        in_=xa[:, t, :], in_offset=None).then_inc(scattered, 16)

        @block.vector
        def _(dve):
            chain = Chain(p, dve, steps_v)
            dve.wait_ge(dst_in, 16)
            dve.wait_ge(p.ready, 1)
            chain(dve.tensor_copy(first[:], dst_rows[:, :, 0]))
            for g in range(CG):
                if g >= 2:
                    dve.wait_ge(piv_done, g - 1)
                dve.tensor_scalar(diag[:, g % 2, :], p.ident[:], first[:, g:g + 1], None, ALU.mult).then_inc(diag_ready, 1)
            for h in range(2):
                lo, hi = h * 4, min(4 * h + 4, CG)
                dve.wait_ge(piv_done, hi)
                chain(dve.tensor_copy(pivots[:, lo * P:hi * P], p.bank[h][:, 0:(hi - lo) * P]))
            before = chain.total()
            with dve.Fori(0, NT + 1) as t:
                chain.at(before + t)
                chain(dve.tensor_scalar(less[:], pivots[:], p.node[:, bass.ds(t, 1)], 0.0, ALU.is_lt, ALU.add,
                                        accum_out=chunks_below[:, bass.ds(t, 1)]))
            chain.at(before + NT + 1)
            chain(dve.tensor_scalar(chunk[:], chunks_below[:], -1.0, 0.0, ALU.add, ALU.max))
            dve.tensor_copy(chunk_i[:], chunk[:]).then_inc(chunks_ready, 1)
            dve.wait_ge(att_in, 32)
            dve.wait_ge(w_in, 16 * KD)
            for k in range(KD):
                heads = wa[:, k, 0:HROW].rearrange("q (h c) -> q h c", c=HW)
                for i, out in enumerate((heads[:, :, HEAD_DIM], wa[:, k, HROW:HROW + HEADS])):
                    chain(dve.tensor_tensor(prod[:].rearrange("q (h c) -> q h c", h=HEADS), heads[:, :, 0:HEAD_DIM],
                                            att[:, i, :].rearrange("q (h c) -> q h c", h=HEADS), ALU.mult))
                    chain(dve.tensor_reduce(out, prod[:].rearrange("q (h c) -> q h c", h=HEADS), AX, ALU.add))
            dve.tensor_copy(prod[:, 0:1], wa[:, 0, 0:1]).then_inc(wa_ready, 1)
            dve.wait_ge(found_in, 16 * (NT + 1))
            chain(dve.tensor_tensor(cmp, found[:], spread(p.node[:], 2, [P, NT + 1, P]), ALU.is_lt))
            chain(dve.tensor_reduce(start[:], cmp, AX, ALU.add))
            chain(dve.scalar_tensor_tensor(start[:], chunk[:], float(P), start[:], ALU.mult, ALU.add))
            dve.tensor_copy(xa[:, :, C_START], start[:, 0:NT]).then_inc(start_ready, 1)
            dve.wait_ge(next_done, 1)
            chain(dve.tensor_tensor(xa[:, :, C_DEG], p.bank[0][:, 0:NT], start[:, 0:NT], ALU.subtract))
            chain(dve.tensor_copy(xa[:, :, C_ID], p.node[:, 0:NT]))
            chain(dve.tensor_scalar(bin_[:], xa[:, :, C_DEG], -1.0, float(DBINS - 1), ALU.mult, ALU.add))
            chain(dve.tensor_scalar(bin_[:], bin_[:], 0.0, None, ALU.max))
            dve.tensor_tensor(hot[:], spread(bin_[:], 2, [P, NT, DBINS]), spread(p.count[:], 1, [P, NT, DBINS]),
                              ALU.is_equal).then_inc(hot_ready, 1)
            dve.wait_ge(edge_in, 48)
            chain(dve.scalar_tensor_tensor(s_key[:], s_src[:], float(RELS), s_typ[:], ALU.mult, ALU.add))
            for q in range(SLICES):
                if q >= 2:
                    dve.wait_ge(wide_out[q % 2], 16 * (q // 2))
                over = bass.AP(tensor=s_key[:].tensor, offset=q * SLICE, ap=[[STRIP + WIN, P], [1, SLICE], [1, WIN]])
                dve.tensor_copy(wide[q % 2][:, :, 0:WIN], over).then_inc(wide_key, 1)
            for lo, hi in halves:
                for g in range(lo, hi):
                    dve.wait_ge(counts_done, g + 1)
                    for n, to in enumerate((within, total)):
                        dve.tensor_copy(to[:, g * U:(g + 1) * U, :].rearrange("q t b -> q (t b)"),
                                        p.bank[2 * (g - lo) + n][:, 0:U * DBINS]).then_inc(counts_out, 1)
            dve.wait_ge(counts_out, 2 * U)
            rank_steps(dve, chain, hot[:], within, total, cum, base, within, rank[:], DBINS)
            dve.tensor_copy(rank_i[:], rank[:]).then_inc(rank_ready, 1)
            dve.wait_ge(x_in, 16)
            front.start(dve, front.varied, front.normed, h_ready)
            before = chain.total()

            def row(g):
                return xa[:, bass.ds(g, 1), 0:D].rearrange("q o d -> q (o d)")

            def result(g, u, i):
                dve.wait_ge(h_psum, done(g))
                dve.wait_ge(h_stored[u], 16 * (i + 1))
                p.alone(dve)
                ps = p.bank[4 + u % 4]
                dve.tensor_copy(hrow[u][:], ps[:, 0:HROW])
                dve.tensor_copy(xa[:, bass.ds(g, 1), C_ADST:C_ADST + HEADS].rearrange("q o d -> q (o d)"),
                                ps[:, HROW:HROW + HEADS]).then_inc(h_ready, 1)

            with dve.Fori(0, U) as i:
                chain.at(i * (front.STEPS * U) + before)
                front.moments(dve, chain, row(i * U), i * U, 0)
                for u in range(U + 1):
                    if u + 1 < U:
                        front.moments(dve, chain, row(i * U + (u + 1)), i * U + (u + 1), u + 1)
                    if u < U:
                        front.norm(dve, chain, row(i * U + u), i * U + u, u)
                    if u >= 1:
                        result(i * U + (u - 1), u - 1, i)
                assert chain.n == front.STEPS * U

        @block.tensor
        def _(pe):
            pe.wait_ge(p.ready, 1)
            for g in range(CG):
                pe.wait_ge(diag_ready, g + 1)
                pe.matmul(p.bank[g // 4][:, (g % 4) * P:(g % 4 + 1) * P], p.ones[:], diag[:, g % 2, :],
                          start=True, stop=True).then_inc(piv_done, 1)
            pe.wait_ge(start_ready, 1)
            pe.matmul(p.bank[0][:, 0:NT], shift[:, 0, :], start[:, 0:NT], start=True, stop=False)
            pe.matmul(p.bank[0][:, 0:NT], shift[:, 1, :], start[:, 1:NT + 1], start=False, stop=True).then_inc(next_done, 1)
            pe.wait_ge(hot_ready, 1)
            for lo, hi in halves:
                if lo:
                    pe.wait_ge(counts_out, 2 * lo)
                for g in range(lo, hi):
                    rows = hot[:, g * U:(g + 1) * U, :].rearrange("q t b -> q (t b)")
                    pe.matmul(p.bank[2 * (g - lo)][:, 0:U * DBINS], p.earlier[:], rows, start=True, stop=True)
                    pe.matmul(p.bank[2 * (g - lo) + 1][:, 0:U * DBINS], p.onesb[:], rows, start=True, stop=True)\
                      .then_inc(counts_done, 1)
            pe.wait_ge(wa_ready, 1)
            pe.wait_ge(counts_out, 2 * U)
            front.start(pe, front.turned, h_psum)

            def project(g, u):
                pe.wait_ge(front.copied, done(g))
                pe.wait_ge(h_ready, done(g - 3))
                for k in range(KD):
                    ins = pe.matmul(p.bank[4 + u % 4][:, 0:HROW + HEADS], front.xt[u][:, k * P:(k + 1) * P], wa[:, k, :],
                                    start=(k == 0), stop=(k == KD - 1))
                ins.then_inc(h_psum, 1)

            with pe.Fori(0, U) as i:
                for u in range(U):
                    front.turn(pe, i * U + u, u)
                    if u >= 1:
                        project(i * U + (u - 1), u - 1)
                project(i * U + (U - 1), U - 1)

        @block.scalar
        def _(act):
            act.wait_ge(p.ready, 1)
            front.scalar_loop(act, h_psum)


def load_windows(p, pool, landed):
    for t in range(NT):
        pool.indirect_dma_start(out=p.win[:, t, :], out_offset=None, in_=p.windows[:],
                                in_offset=bass.IndirectOffsetOnAxis(ap=p.start_i[:, t:t + 1], axis=0)).then_inc(landed, 16)


def attention(p: Program):
    nc, a = p.nc, p.a
    with p.phase() as ctx:
        def sb(n, s, d):
            return ctx.enter_context(nc.sbuf_tensor(n, s, d))

        most = sb("most", [NT, 2], F32)
        most_i = sb("most_i", [NT, 2], I32)
        row = sb("row", [1, 3, NT], F32)
        key_i = sb("key_i", [P, NT, WIN], I32)
        src_i = sb("src_i", [P, NT + 1, WIN], I32)
        mask = sb("mask", [P, NT, WIN], F32)
        ZEROS = 16
        zeros = sb("zeros", [P, XCH // ZEROS * REC], F32)
        bias = sb("gat_bias", [P, D], F32)
        idx = [sb(f"gat_idx{s}", [P, JCOL], I32) for s in range(SLOTS)]
        rows = [sb(f"gat_rows{s}", [P, JCOL, HROW], F32) for s in range(SLOTS)]
        msg = [sb(f"gat_msg{s}", [P, JCOL, HROW], F32) for s in range(SLOTS)]
        NS = JCOL * HEADS
        score = [sb(f"gat_score{s}", [P, NS + HEADS], F32) for s in range(SLOTS)]
        item_max = sb("item_max", [P, SLOTS, HEADS], F32)
        top = sb("top", [P, SLOTS + 1, HEADS], F32)
        fade = [sb(f"gat_fade{s}", [P, HEADS], F32) for s in range(SLOTS)]
        acc = sb("gat_acc", [P, HROW], F32)
        inv = sb("gat_inv", [P, 2, HEADS], F32)
        o = sb("gat_o", [P, D], F32)
        t_pos = sb("t_pos", [P, 3], F32)
        t_at_i = sb("t_at_i", [P, 1], I32)
        t_win = sb("t_win", [P, 2 * WIN], F32)
        t_key = sb("t_key", [P, JCOL], I32)
        t_idx_i = sb("t_idx_i", [P, JCOL], I32)
        t_mask = sb("t_mask", [P, JCOL], F32)

        bias_in, start_ready, wins_in = (p.sem(x) for x in ("gat_bias_in", "gat_start_ready", "gat_wins_in"))
        zeros_ready, zeroed = p.sem("zeros_ready"), p.sem("zeroed")
        turned, most_ready, row_done, tables = (p.sem(x) for x in ("deg_turned", "most_ready", "row_done", "tables"))
        per_slot = lambda name: [p.sem(f"{name}{s}") for s in range(SLOTS)]
        idx_ready, gathered, scores_ready, p_ready, msg_ready, sum_ready, acc_done = (
            per_slot(f"gat_{x}") for x in ("idx_ready", "gathered", "scores", "p_ready", "msg_ready", "sum_ready", "acc_done"))
        step, steps_s, steps_a, steps_t = p.sem("gat_step"), per_slot("gat_steps_s"), per_slot("gat_steps_a"), p.sem("gat_steps_t")
        t_at, t_window, t_idx, t_rows, t_scores, t_p, t_msg, t_sum, t_done, t_steps, t_begin = (
            p.sem(f"gat_t_{x}") for x in ("at", "window", "idx", "rows", "scores", "p", "msg", "sum", "done", "steps", "begin"))
        block = ctx.enter_context(nc.Block())

        def items(eng, t):
            return eng.value_load(p.items[0:1, bass.ds(t, 1)], min_val=1, max_val=-(-N_EDGES // JCOL))

        def tail_base(eng, t):
            return eng.value_load(p.tails[0:1, bass.ds(t, 1)], min_val=0, max_val=N_EDGES)

        @block.sync
        def _(sp):
            flat = a["L0_gnn_bias"]
            sp.dma_start(bias[:], bass.AP(tensor=flat.tensor, offset=0, ap=[[0, P], [1, D]])).then_inc(bias_in, 16)
            sp.wait_ge(bias_in, 16)
            sp.wait_ge(zeros_ready, 1)
            for z in range(ZEROS):
                sp.dma_start(p.x_grouped.rearrange("(z q e) c -> z q (e c)", z=ZEROS, q=P)[z], zeros[:]).then_inc(zeroed, 16)
            sp.wait_ge(zeroed, 16 * ZEROS)

        @block.gpsimd
        def _(pool):
            pool.memset(zeros[:], 0.0).then_inc(zeros_ready, 1)
            pool.wait_ge(start_ready, 1)
            load_windows(p, pool, wins_in)
            pool.wait_ge(tables, 1)
            with pool.Fori(0, NT) as t:
                n = items(pool, t)

                def gather(s):
                    pool.wait_ge(idx_ready[s], t + 1)
                    pool.wait_ge(msg_ready[s], t + 1)
                    p.alone(pool)
                    for j in range(JCOL):
                        pool.indirect_dma_start(out=rows[s][:, j, :], out_offset=None, in_=p.h_table[:],
                                                in_offset=bass.IndirectOffsetOnAxis(ap=idx[s][:, j:j + 1], axis=0))\
                            .then_inc(gathered[s], 16)

                gather(0)
                for s in range(1, SLOTS):
                    with pool.If(n > s):
                        gather(s)
                with pool.If(n > SLOTS):
                    c0 = tail_base(pool, t)
                    with pool.Fori(SLOTS, n) as k:
                        c = c0 + k - SLOTS
                        pool.wait_ge(t_at, c + 1)
                        p.alone(pool)
                        pool.indirect_dma_start(out=t_win[:], out_offset=None, in_=p.windows[:],
                                                in_offset=bass.IndirectOffsetOnAxis(ap=t_at_i[:, 0:1], axis=0)).then_inc(t_window, 16)
                        pool.wait_ge(t_idx, c + 1)
                        p.alone(pool)
                        for j in range(JCOL):
                            pool.indirect_dma_start(out=rows[0][:, j, :], out_offset=None, in_=p.h_table[:],
                                                    in_offset=bass.IndirectOffsetOnAxis(ap=t_idx_i[:, j:j + 1], axis=0))\
                                .then_inc(t_rows, 16)
                        pool.wait_ge(t_done, c + 1)
                        p.alone(pool)

        @block.scalar
        def _(act):
            act.wait_ge(tables, 1)
            for s in range(SLOTS):
                act.activation(idx[s][:], src_i[:, 0, s * JCOL:(s + 1) * JCOL], ACT.Copy).then_inc(idx_ready[s], 1)

            def exps(s):
                act.activation(msg[s][:].rearrange("q j c -> q (j c)")[:, HEAD_DIM::HW], score[s][:, 0:NS], ACT.Exp)
                return act.activation(fade[s][:], score[s][:, NS:], ACT.Exp)

            with act.Fori(0, NT) as t:
                n = items(act, t)

                def item(s):
                    act.wait_ge(sum_ready[s], t + 1)
                    act.wait_ge(acc_done[s], t + 1)
                    act.wait_ge(scores_ready[s], t + 1)
                    exps(s).then_inc(p_ready[s], 1)
                    act.wait_ge(gathered[s], 16 * JCOL * (t + 1))
                    p.alone(act)
                    act.activation(idx[s][:], src_i[:, bass.ds(t + 1, 1), s * JCOL:(s + 1) * JCOL].rearrange("q o j -> q (o j)"),
                                   ACT.Copy).then_inc(idx_ready[s], 1)

                item(0)
                for s in range(1, SLOTS):
                    with act.If(n > s):
                        item(s)
                with act.If(n > SLOTS):
                    c0 = tail_base(act, t)
                    with act.Fori(SLOTS, n) as k:
                        act.wait_ge(t_scores, c0 + k - SLOTS + 1)
                        exps(0).then_inc(t_p, 1)

        @block.tensor
        def _(pe):
            pe.transpose(p.bank[0][0:NT, 0:P], p.rec[:, :, C_DEG], p.ident[:]).then_inc(turned, 1)
            pe.wait_ge(most_ready, 1)
            pe.matmul(p.bank[1][0:1, 0:NT], most[:, 1:2], p.ident[0:NT, 0:NT], start=True, stop=True).then_inc(row_done, 1)
            pe.wait_ge(tables, 1)

            for s in range(SLOTS):
                pe.sem_inc(sum_ready[s], 1)

            def total(s):
                for j in range(JCOL):
                    ins = pe.matmul(p.bank[s][:, 0:HROW], p.ident[:], msg[s][:, j, :], start=(j == 0), stop=(j == JCOL - 1))
                return ins

            with pe.Fori(0, NT) as t:
                n = items(pe, t)

                def item(s):
                    pe.wait_ge(acc_done[s], t + 1)
                    pe.wait_ge(msg_ready[s], t + 2)
                    total(s).then_inc(sum_ready[s], 1)

                item(0)
                for s in range(1, SLOTS):
                    with pe.If(n > s):
                        item(s)
                with pe.If(n > SLOTS):
                    c0 = tail_base(pe, t)
                    with pe.Fori(SLOTS, n) as k:
                        pe.wait_ge(t_msg, c0 + k - SLOTS + 1)
                        total(0).then_inc(t_sum, 1)

        @block.vector
        def _(dve):
            chain = Chain(p, dve, step)
            chain(dve.tensor_copy(p.id_i[:], p.rec[:, :, C_ID]))
            dve.tensor_copy(p.start_i[:], p.rec[:, :, C_START]).then_inc(start_ready, 1)
            dve.wait_ge(turned, 1)
            chain(dve.tensor_reduce(most[:, 0:1], p.bank[0][0:NT, 0:P], AX, ALU.max))
            chain(dve.tensor_scalar(most_i[:, 0:1], most[:, 0:1], float(JCOL - 1), None, ALU.add))
            chain(dve.tensor_scalar(most_i[:, 1:2], most_i[:, 0:1], JCOL.bit_length() - 1, None, ALU.arith_shift_right))
            dve.tensor_scalar(most[:, 1:2], most_i[:, 1:2], 1.0, None, ALU.max).then_inc(most_ready, 1)
            dve.wait_ge(row_done, 1)
            chain(dve.tensor_copy(row[:, 0, :], p.bank[1][0:1, 0:NT]))
            chain(dve.tensor_copy(p.items[:], row[:, 0, :]))
            chain(dve.tensor_scalar(row[:, 0, :], row[:, 0, :], -float(SLOTS), 0.0, ALU.add, ALU.max))
            chain(dve.memset(row[:, 1, :], 0.0))
            chain(dve.tensor_tensor_scan(row[:, 2, :], row[:, 0, :], row[:, 1, :], 0.0, ALU.add, ALU.add))
            chain(dve.tensor_tensor(row[:, 2, :], row[:, 2, :], row[:, 0, :], ALU.subtract))
            chain(dve.tensor_copy(p.tails[:], row[:, 2, :]))
            chain(dve.tensor_tensor(mask[:], spread(p.count[:, 0:WIN], 1, [P, NT, WIN]),
                                    p.rec[:, :, C_DEG:C_DEG + 1].broadcast_to([P, NT, WIN]), ALU.is_ge))
            chain(dve.tensor_scalar(mask[:], mask[:], NEVER, None, ALU.mult))
            chain(dve.memset(src_i[:, NT, :], 0))
            dve.wait_ge(wins_in, 16 * NT)
            chain(dve.tensor_copy(key_i[:], p.win[:, :, 0:WIN]))
            dve.tensor_scalar(src_i[:, 0:NT, :], key_i[:], RELS.bit_length() - 1, None, ALU.arith_shift_right).then_inc(tables, 1)
            dve.wait_ge(tables, 1)
            dve.wait_ge(bias_in, 16)

            def heads(ap):
                return ap.rearrange("q (h c) -> q h c", h=HEADS)

            def scores(chain, s, t, masked, old, new, biggest, ready):
                sc = score[s][:, 0:NS].rearrange("q (j h) -> q j h", h=HEADS)
                g = rows[s][:].rearrange("q j (h c) -> q j h c", c=HW)
                chain(dve.tensor_tensor(sc, g[:, :, :, HEAD_DIM],
                                        p.rec[:, bass.ds(t, 1), C_ADST:C_ADST + HEADS].broadcast_to([P, JCOL, HEADS]), ALU.add))
                chain(dve.scalar_tensor_tensor(sc, sc, 0.2, sc, ALU.mult, ALU.max))
                chain(dve.tensor_tensor(sc, sc, masked, ALU.add))
                chain(dve.tensor_reduce(biggest, score[s][:, 0:NS].rearrange("q (j h) -> q h j", h=HEADS), AX, ALU.max))
                chain(dve.tensor_tensor(new, old, biggest, ALU.max))
                dve.tensor_tensor(sc, sc, spread(new, 1, [P, JCOL, HEADS]), ALU.subtract)
                dve.tensor_tensor(score[s][:, NS:], old, new, ALU.subtract).then_inc(ready, 1)

            def messages(s, ready):
                g = rows[s][:].rearrange("q j (h c) -> q (j h) c", c=HW)
                m = msg[s][:].rearrange("q j (h c) -> q (j h) c", c=HW)
                dve.tensor_tensor(m[:, :, 0:HEAD_DIM], g[:, :, 0:HEAD_DIM],
                                  m[:, :, HEAD_DIM:HW].broadcast_to([P, NS, HEAD_DIM]), ALU.mult).then_inc(ready, 1)

            def accumulate(chain, s, finished):
                chain(dve.tensor_tensor(heads(acc[:]), heads(acc[:]), spread(fade[s][:], 2, [P, HEADS, HW]), ALU.mult))
                dve.tensor_tensor(acc[:], acc[:], p.bank[s][:, 0:HROW], ALU.add).then_inc(finished, 1)

            for s in range(SLOTS):
                dve.sem_inc(msg_ready[s], 1)
                dve.sem_inc(acc_done[s], 1)
            chain_s = [Chain(p, dve, x) for x in steps_s]
            chain_a = [Chain(p, dve, x) for x in steps_a]
            chain_t, chain_k = Chain(p, dve, steps_t), Chain(p, dve, t_steps)
            TAIL_STEPS = 11
            with dve.Fori(0, NT) as t:
                n = items(dve, t)
                chain_t.at(t * 6)
                dve.memset(top[:, 0, :], LOWEST)
                chain_t(dve.memset(acc[:], 0.0))

                def front_of(s):
                    chain_s[s].at(t * 5)
                    dve.wait_ge(gathered[s], 16 * JCOL * (t + 1))
                    scores(chain_s[s], s, t, mask[:, bass.ds(t, 1), s * JCOL:(s + 1) * JCOL].rearrange("q o j -> q j o")
                           .broadcast_to([P, JCOL, HEADS]), top[:, s, :], top[:, s + 1, :], item_max[:, s, :], scores_ready[s])
                    assert chain_s[s].n == 5
                    dve.wait_ge(p_ready[s], t + 1)
                    messages(s, msg_ready[s])

                def back_of(s):
                    chain_a[s].at(t)
                    dve.wait_ge(sum_ready[s], t + 2)
                    accumulate(chain_a[s], s, acc_done[s])
                    dve.wait_ge(acc_done[s], t + 2)
                    p.alone(dve)

                front_of(0)
                for s in range(1, SLOTS):
                    with dve.If(n > s):
                        front_of(s)
                        back_of(s - 1)
                for s in range(SLOTS):
                    with dve.If(n == s + 1 if s + 1 < SLOTS else n > s):
                        back_of(s)
                with dve.If(n > SLOTS):
                    c0 = tail_base(dve, t)
                    dve.tensor_scalar(t_pos[:, 0:1], p.rec[:, bass.ds(t, 1), C_START:C_START + 1].rearrange("q o c -> q (o c)"),
                                      float(WIN), None, ALU.add)
                    dve.tensor_scalar(t_pos[:, 1:2], p.rec[:, bass.ds(t, 1), C_DEG:C_DEG + 1].rearrange("q o c -> q (o c)"),
                                      -float(WIN), None, ALU.add).then_inc(t_begin, 1)
                    dve.wait_ge(t_begin, t + 1)
                    p.alone(dve)
                    with dve.Fori(SLOTS, n) as k:
                        c = c0 + k - SLOTS
                        chain_k.at(c * TAIL_STEPS)
                        dve.tensor_scalar(t_at_i[:], t_pos[:, 0:1], float(N_EDGES), None, ALU.min).then_inc(t_at, 1)
                        dve.wait_ge(t_window, 16 * (c + 1))
                        chain_k(dve.tensor_copy(t_key[:], t_win[:, 0:JCOL]))
                        dve.tensor_scalar(t_idx_i[:], t_key[:], RELS.bit_length() - 1, None, ALU.arith_shift_right).then_inc(t_idx, 1)
                        chain_k(dve.tensor_scalar(t_mask[:], p.count[:, 0:JCOL], t_pos[:, 1:2], NEVER, ALU.is_ge, ALU.mult))
                        dve.wait_ge(t_rows, 16 * JCOL * (c + 1))
                        scores(chain_k, 0, t, spread(t_mask[:], 2, [P, JCOL, HEADS]), top[:, SLOTS, :], top[:, 0, :],
                               item_max[:, 0, :], t_scores)
                        dve.wait_ge(t_p, c + 1)
                        messages(0, t_msg)
                        dve.wait_ge(t_msg, c + 1)
                        p.alone(dve)
                        chain_k(dve.tensor_copy(top[:, SLOTS, :], top[:, 0, :]))
                        dve.wait_ge(t_sum, c + 1)
                        accumulate(chain_k, 0, t_done)
                        dve.wait_ge(t_done, c + 1)
                        p.alone(dve)
                        chain_k(dve.tensor_scalar(t_pos[:, 0:1], t_pos[:, 0:1], float(JCOL), None, ALU.add))
                        chain_k(dve.tensor_scalar(t_pos[:, 1:2], t_pos[:, 1:2], -float(JCOL), None, ALU.add))
                        assert chain_k.n == TAIL_STEPS, chain_k.n
                chain_t(dve.tensor_scalar(inv[:, 0, :], heads(acc[:])[:, :, HEAD_DIM], 1e-16, None, ALU.add))
                chain_t(dve.reciprocal(inv[:, 1, :], inv[:, 0, :]))
                chain_t(dve.tensor_tensor(heads(o[:]), heads(acc[:])[:, :, 0:HEAD_DIM], spread(inv[:, 1, :], 2, [P, HEADS, HEAD_DIM]), ALU.mult))
                chain_t(dve.tensor_tensor(o[:], o[:], bias[:], ALU.add))
                x = p.rec[:, bass.ds(t, 1), 0:D].rearrange("q o d -> q (o d)")
                chain_t(dve.scalar_tensor_tensor(x, o[:], 0.0, x, ALU.max, ALU.add))
                assert chain_t.n == 6


def tile_row(p, g, lo=0, hi=D):
    return p.rec[:, bass.ds(g, 1), lo:hi].rearrange("q o d -> q (o d)")


def route(p: Program):
    nc, a = p.nc, p.a
    with p.phase() as ctx:
        def sb(n, s, d):
            return ctx.enter_context(nc.sbuf_tensor(n, s, d))

        front = Front(p, ctx, "route")
        rw = sb("rw", [E0, D], F32)
        rwt = sb("rwt", [P, KD, E0], F32)
        rb = sb("rb", [P, E0], F32)
        logits = sb("logits", [P, U, E0], F32)
        best = sb("best", [P, U, 8], F32)
        best_i = sb("best_i", [P, U, 8], U32)
        expert = sb("expert", [P, NT], F32)
        hot = sb("hot0", [P, NT, E0], BF16)
        within = sb("within0", [P, NT, E0], F32)
        total = sb("total0", [P, NT, E0], F32)
        cum = sb("cum0", [P, NT + 1, E0], F32)
        base = sb("base0", [P, 3, E0], F32)
        align = sb("align0", [P, E0], I32)
        place = sb("place", [P, NT], F32)
        begins = sb("begins", [1, XCH], F32)
        past = sb("past", [1, XCH, E0], F32)
        chunk_e = sb("chunk_e", [1, XCH], F32)

        rw_in, rb_in, rw_turned, rwt_ready, logits_done, chosen = (
            p.sem(f"route_{x}") for x in ("rw_in", "rb_in", "rw_turned", "rwt_ready", "logits_done", "chosen"))
        hot_ready, counts_done, counts_out, place_ready, scattered, begins_ready, steps = (
            p.sem(f"route_{x}") for x in ("hot_ready", "counts_done", "counts_out", "place_ready", "scattered", "begins_ready", "steps"))
        block = ctx.enter_context(nc.Block())

        @block.sync
        def _(sp):
            sp.dma_start(rw[:], a["L0_ffn_router_w"]).then_inc(rw_in, 16)
            sp.dma_start(rb[:], bass.AP(tensor=a["L0_ffn_router_b"].tensor, offset=0, ap=[[0, P], [1, E0]])).then_inc(rb_in, 16)

        @block.gpsimd
        def _(pool):
            pool.iota(begins[:], pattern=[[P, XCH]], base=0, channel_multiplier=0,
                      allow_small_or_imprecise_dtypes=True).then_inc(begins_ready, 1)
            pool.wait_ge(place_ready, 1)
            for t in range(NT):
                pool.indirect_dma_start(out=p.x_grouped[:], out_offset=bass.IndirectOffsetOnAxis(ap=p.place_i[:, t:t + 1], axis=0),
                                        in_=p.rec[:, t, :], in_offset=None).then_inc(scattered, 16)
            pool.wait_ge(scattered, 16 * NT)

        @block.scalar
        def _(act):
            front.scalar_loop(act, logits_done)

        @block.tensor
        def _(pe):
            pe.wait_ge(rw_in, 16)
            for k in range(KD):
                ins = pe.transpose(p.bank[7][:, k * E0:(k + 1) * E0], rw[:, k * P:(k + 1) * P], p.ident[0:E0, 0:E0])
            ins.then_inc(rw_turned, 1)
            pe.wait_ge(rwt_ready, 1)
            front.start(pe, front.turned, logits_done)

            def product(g, u):
                pe.wait_ge(front.copied, done(g))
                pe.wait_ge(chosen, done(g - 3))
                for k in range(KD):
                    ins = pe.matmul(p.bank[4 + u % 4][:, 0:E0], front.xt[u][:, k * P:(k + 1) * P], rwt[:, k, :],
                                    start=(k == 0), stop=(k == KD - 1))
                ins.then_inc(logits_done, 1)

            with pe.Fori(0, U) as i:
                for u in range(U):
                    front.turn(pe, i * U + u, u)
                    if u >= 1:
                        product(i * U + (u - 1), u - 1)
                product(i * U + (U - 1), U - 1)
            pe.wait_ge(hot_ready, 1)
            for g in range(U):
                rows = hot[:, g * U:(g + 1) * U, :].rearrange("q t b -> q (t b)")
                pe.matmul(p.bank[g][:, 0:U * E0], p.earlier[:], rows, start=True, stop=True)
                pe.matmul(p.bank[g][:, U * E0:2 * U * E0], p.onesb[:], rows, start=True, stop=True).then_inc(counts_done, 1)

        @block.vector
        def _(dve):
            chain = Chain(p, dve, steps)
            dve.wait_ge(rw_turned, 1)
            dve.tensor_copy(rwt[:].rearrange("q k e -> q (k e)"), p.bank[7][:, 0:KD * E0]).then_inc(rwt_ready, 1)
            dve.wait_ge(rb_in, 16)
            front.start(dve, front.varied, front.normed, chosen)
            K = front.STEPS + 4

            def choose(g, u):
                dve.wait_ge(logits_done, done(g))
                chain(dve.tensor_tensor(logits[:, u, :], p.bank[4 + u % 4][:, 0:E0], rb[:], ALU.add), True)
                chain(dve.max(best[:, u, :], logits[:, u, :]), True)
                chain(dve.max_index(best_i[:, u, :], best[:, u, :], logits[:, u, :]), True)
                dve.tensor_copy(expert[:, bass.ds(g, 1)], best_i[:, u, 0:1])
                chain(dve.tensor_copy(tile_row(p, g, D, D + 4), front.ms[:, u, :]))
                dve.sem_inc(chosen, 1)

            with dve.Fori(0, U) as i:
                chain.at(i * (K * U))
                front.moments(dve, chain, tile_row(p, i * U), i * U, 0)
                for u in range(U + 1):
                    if u + 1 < U:
                        front.moments(dve, chain, tile_row(p, i * U + (u + 1)), i * U + (u + 1), u + 1)
                    if u < U:
                        front.norm(dve, chain, tile_row(p, i * U + u), i * U + u, u)
                    if u >= 1:
                        choose(i * U + (u - 1), u - 1)
                assert chain.n == K * U
            chain.at(K * NT)
            dve.tensor_tensor(hot[:], spread(expert[:], 2, [P, NT, E0]), spread(p.count[:, 0:E0], 1, [P, NT, E0]),
                              ALU.is_equal).then_inc(hot_ready, 1)
            for g in range(U):
                dve.wait_ge(counts_done, g + 1)
                for n, to in enumerate((within, total)):
                    dve.tensor_copy(to[:, g * U:(g + 1) * U, :].rearrange("q t b -> q (t b)"),
                                    p.bank[g][:, n * U * E0:(n + 1) * U * E0]).then_inc(counts_out, 1)
            dve.wait_ge(counts_out, 2 * U)
            rank_steps(dve, chain, hot[:], within[:], total[:], cum, base, within[:], place[:], E0, align[:])
            dve.tensor_copy(p.place_i[:], place[:]).then_inc(place_ready, 1)
            dve.wait_ge(begins_ready, 1)
            chain(dve.tensor_tensor(past[:], spread(base[0:1, 1, :], 1, [1, XCH, E0]), spread(begins[:], 2, [1, XCH, E0]), ALU.is_le))
            chain(dve.tensor_reduce(chunk_e[:], past[:], AX, ALU.add))
            chain(dve.tensor_scalar(p.chunk_e_i[:], chunk_e[:], float(E0 - 1), None, ALU.min))


def experts(p: Program):
    nc, a = p.nc, p.a
    V = 8
    assert XCH % V == 0
    with p.phase() as ctx:
        def sb(n, s, d):
            return ctx.enter_context(nc.sbuf_tensor(n, s, d))

        def slots(n, s, d):
            return [sb(f"{n}{v}", s, d) for v in range(V)]

        x, w1, w2 = slots("ex_x", [P, REC], F32), slots("ex_w1_", [P, KD, H0], F32), slots("ex_w2_", [H0, D], F32)
        b1, b2 = slots("ex_b1_", [H0, 1], F32), slots("ex_b2_", [1, D], F32)
        xn, xt, hid, y = slots("ex_xn", [P, D], F32), slots("ex_xt", [P, D], F32), slots("ex_h", [H0, P], F32), slots("ex_y", [P, D], F32)
        back = sb("back", [P, NT, D], F32)
        x_in, w_in, y_out = ([p.sem(f"ex_{n}{v}") for v in range(V)] for n in ("x_in", "w_in", "y_out"))
        normed, turned, copied, hid_done, hid_ready, y_done, y_ready = (
            p.sem(f"ex_{n}") for n in ("normed", "turned", "copied", "hid_done", "hid_ready", "y_done", "y_ready"))
        fetched = [p.sem(f"fetched{g}") for g in range(U)]
        block = ctx.enter_context(nc.Block())

        @block.sync
        def _(sp):
            rows = p.x_grouped.rearrange("(g q) c -> g q c", q=P)
            with sp.Fori(0, XCH // V) as i:
                for v in range(V):
                    g = i * V + v
                    e = sp.value_load(p.chunk_e_i[0:1, bass.ds(g, 1)], min_val=0, max_val=E0 - 1)
                    sp.wait_ge(y_done, done(g - V))
                    sp.dma_start(x[v][:], rows[bass.ds(g, 1)].rearrange("o q c -> (o q) c")).then_inc(x_in[v], 16)
                    sp.dma_start(w1[v][:], a["L0_ffn_W1"][bass.ds(e, 1)].rearrange("o (k q) h -> q (o k) h", q=P)).then_inc(w_in[v], 16)
                    sp.dma_start(w2[v][:], a["L0_ffn_W2"][bass.ds(e, 1)].rearrange("o h d -> (o h) d")).then_inc(w_in[v], 16)
                    sp.dma_start(b1[v][:], a["L0_ffn_b1"][bass.ds(e, 1)].rearrange("o (h z) -> (o h) z", z=1)).then_inc(w_in[v], 16)
                    sp.dma_start(b2[v][:], a["L0_ffn_b2"][bass.ds(e, 1)]).then_inc(w_in[v], 16)

        @block.vector
        def _(dve):
            dve.sem_inc(normed, U)
            with dve.Fori(0, XCH // V) as i:
                for v in range(V):
                    g = i * V + v
                    dve.wait_ge(turned, done(g - V))
                    dve.wait_ge(x_in[v], 16 * (i + 1))
                    dve.tensor_scalar(xn[v][:], x[v][:, 0:D], x[v][:, D:D + 1], x[v][:, D + 3:D + 4],
                                      ALU.subtract, ALU.mult).then_inc(normed, 1)
            for g in range(U):
                dve.wait_ge(fetched[g], 16 * U)
                rows = p.rec[:, g * U:(g + 1) * U, 0:D]
                dve.tensor_tensor(rows, rows, back[:, g * U:(g + 1) * U, :], ALU.add)

        @block.tensor
        def _(pe):
            for s in (turned, hid_done, y_done):
                pe.sem_inc(s, U)

            def turn(g, v):
                pe.wait_ge(normed, done(g))
                pe.wait_ge(hid_ready, done(g - 4))
                for k in range(KD):
                    ins = pe.transpose(p.bank[v % 4][:, k * P:(k + 1) * P], xn[v][:, k * P:(k + 1) * P], p.ident[:])
                ins.then_inc(turned, 1)

            def hidden(g, v, i):
                pe.wait_ge(w_in[v], 64 * (i + 1))
                pe.wait_ge(copied, done(g))
                for k in range(KD):
                    ins = pe.matmul(p.bank[v % 4][0:H0, D:D + P], w1[v][:, k, :], xt[v][:, k * P:(k + 1) * P],
                                    start=(k == 0), stop=(k == KD - 1))
                ins.then_inc(hid_done, 1)

            def output(g, v):
                pe.wait_ge(y_ready, done(g - 4))
                pe.wait_ge(hid_ready, done(g))
                pe.matmul(p.bank[4 + v % 4][:, 0:D], hid[v][:], w2[v][:], start=True, stop=False)
                pe.matmul(p.bank[4 + v % 4][:, 0:D], p.ones[0:1, :], b2[v][:], start=False, stop=True).then_inc(y_done, 1)

            with pe.Fori(0, XCH // V) as i:
                for v in range(V + 2):
                    if v < V:
                        turn(i * V + v, v)
                    if 1 <= v <= V:
                        hidden(i * V + (v - 1), v - 1, i)
                    if v >= 2:
                        output(i * V + (v - 2), v - 2)

        @block.scalar
        def _(act):
            for s in (copied, hid_ready, y_ready):
                act.sem_inc(s, U)

            def to_xt(g, v):
                act.wait_ge(hid_done, done(g - V))
                act.wait_ge(turned, done(g))
                act.activation(xt[v][:], p.bank[v % 4][:, 0:D], ACT.Copy).then_inc(copied, 1)

            def to_hidden(g, v):
                act.wait_ge(y_done, done(g - V))
                act.wait_ge(hid_done, done(g))
                act.activation(hid[v][:], p.bank[v % 4][0:H0, D:D + P], ACT.Relu, bias=b1[v][:, 0:1]).then_inc(hid_ready, 1)

            def to_y(g, v, i):
                act.wait_ge(y_out[v], 16 * (i + 1))
                act.wait_ge(y_done, done(g))
                act.activation(y[v][:], p.bank[4 + v % 4][:, 0:D], ACT.Relu).then_inc(y_ready, 1)

            with act.Fori(0, XCH // V) as i:
                for v in range(V + 2):
                    if v < V:
                        to_xt(i * V + v, v)
                    if 1 <= v <= V:
                        to_hidden(i * V + (v - 1), v - 1)
                    if v >= 2:
                        to_y(i * V + (v - 2), v - 2, i)

        @block.gpsimd
        def _(pool):
            rows = p.y_grouped.rearrange("(g q) c -> g q c", q=P)
            for v in range(V):
                pool.dma_start(y[v][:], a["x"][0:P]).then_inc(y_out[v], 16)
            with pool.Fori(0, XCH // V) as i:
                for v in range(V):
                    g = i * V + v
                    pool.wait_ge(y_ready, done(g))
                    p.alone(pool)
                    pool.dma_start(rows[bass.ds(g, 1)].rearrange("o q c -> (o q) c"), y[v][:]).then_inc(y_out[v], 16)
            for v in range(V):
                pool.wait_ge(y_out[v], 16 * (XCH // V + 1))
            for t in range(NT):
                pool.indirect_dma_start(out=back[:, t, :], out_offset=None, in_=p.y_grouped[:],
                                        in_offset=bass.IndirectOffsetOnAxis(ap=p.place_i[:, t:t + 1], axis=0)).then_inc(fetched[t // U], 16)


def transform(p: Program):
    nc, a = p.nc, p.a
    GROUPS, QUARTERS, SLOTS_T = RELS // 2, RELS // 4, 7
    QW = 4 * D
    with p.phase() as ctx:
        def sb(n, s, d):
            return ctx.enter_context(nc.sbuf_tensor(n, s, d))

        front = Front(p, ctx, "rel")
        wr = sb("wr", [P, KD, RELS * D], F32)
        quarter_i = sb("quarter_i", [P, NT, QUARTERS], I32)
        trow = [sb(f"trow{s}", [P, QW], F32) for s in range(SLOTS_T)]
        row_i = [sb(f"trow_i{s}", [P, 1], I32) for s in range(SLOTS_T)]
        w_in, indices, product_done, evac_v, evac_a, steps = (
            p.sem(f"rel_{x}") for x in ("w_in", "indices", "product_done", "evac_v", "evac_a", "steps"))
        scattered = [p.sem(f"rel_scattered{s}") for s in range(SLOTS_T)]
        block = ctx.enter_context(nc.Block())

        @block.sync
        def _(sp):
            for k in range(KD):
                sp.dma_start(wr[:, k, :].rearrange("q (r o) -> q r o", o=D),
                             a["L1_gnn_weight"][:, k * P:(k + 1) * P, :].rearrange("r q o -> q r o")).then_inc(w_in, 16)

        @block.gpsimd
        def _(pool):
            table = p.transformed.rearrange("(n r) d -> n (r d)", r=4)
            for s in range(SLOTS_T):
                pool.dma_start(row_i[s][:], a["src"][0:P].rearrange("(q o) -> q o", o=1)).then_inc(scattered[s], 16)
            with pool.Fori(0, U) as i:
                for w in range(U * QUARTERS):
                    s = w % SLOTS_T
                    pool.wait_ge(evac_v, done(i * (U * QUARTERS) + w))
                    pool.wait_ge(evac_a, done(i * (U * QUARTERS) + w))
                    p.alone(pool)
                    pool.indirect_dma_start(out=table, out_offset=bass.IndirectOffsetOnAxis(ap=row_i[s][:, 0:1], axis=0),
                                            in_=trow[s][:], in_offset=None).then_inc(scattered[s], 16)
            for s in range(SLOTS_T):
                pool.wait_ge(scattered[s], 16 * (NT * QUARTERS // SLOTS_T + 1))

        @block.vector
        def _(dve):
            chain = Chain(p, dve, steps)
            for q in range(QUARTERS):
                ins = dve.tensor_scalar(quarter_i[:, :, q], p.rec[:, :, C_ID], float(QUARTERS), float(q), ALU.mult, ALU.add)
            ins.then_inc(indices, 1)
            front.start(dve, front.varied, front.normed, evac_v)

            def results(i, u):
                for q in range(QUARTERS):
                    w = u * QUARTERS + q
                    dve.wait_ge(product_done, done((i * U + u) * GROUPS + 2 * q))
                    dve.wait_ge(scattered[w % SLOTS_T], 16 * (4 * i + (w // SLOTS_T + 1)))
                    p.alone(dve)
                    dve.tensor_copy(trow[w % SLOTS_T][:, 0:QW // 2], p.bank[4 + (2 * q) % 4][:]).then_inc(evac_v, 1)

            with dve.Fori(0, U) as i:
                chain.at(i * (front.STEPS * U))
                front.moments(dve, chain, tile_row(p, i * U), i * U, 0)
                for u in range(U + 1):
                    if u + 1 < U:
                        front.moments(dve, chain, tile_row(p, i * U + (u + 1)), i * U + (u + 1), u + 1)
                    if u < U:
                        front.norm(dve, chain, tile_row(p, i * U + u), i * U + u, u)
                    if u >= 1:
                        results(i, u - 1)
                assert chain.n == front.STEPS * U

        @block.scalar
        def _(act):
            act.wait_ge(indices, 1)
            front.start(act, front.rooted, front.copied, evac_a)

            def results(i, u):
                for q in range(QUARTERS):
                    w = u * QUARTERS + q
                    act.wait_ge(product_done, done((i * U + u) * GROUPS + 2 * q + 1))
                    act.wait_ge(scattered[w % SLOTS_T], 16 * (4 * i + (w // SLOTS_T + 1)))
                    p.alone(act)
                    act.activation(trow[w % SLOTS_T][:, QW // 2:], p.bank[4 + (2 * q + 1) % 4][:], ACT.Copy)
                    act.activation(row_i[w % SLOTS_T][:], quarter_i[:, bass.ds(i * U + u, 1), q:q + 1].rearrange("q o c -> q (o c)"),
                                   ACT.Copy).then_inc(evac_a, 1)

            with act.Fori(0, U) as i:
                front.root(act, i * U, 0)
                for u in range(U + 1):
                    if u + 1 < U:
                        front.root(act, i * U + (u + 1), u + 1)
                    if u < U:
                        front.copy(act, i * U + u, u, None)
                    if u >= 1:
                        results(i, u - 1)

        @block.tensor
        def _(pe):
            pe.wait_ge(w_in, 16 * KD)
            front.start(pe, front.turned, product_done)

            def products(g, u):
                pe.wait_ge(front.copied, done(g))
                for m in range(GROUPS):
                    pe.wait_ge(evac_a if m % 2 else evac_v, done(g * QUARTERS + m // 2 - 2))
                    for k in range(KD):
                        ins = pe.matmul(p.bank[4 + m % 4][:], front.xt[u][:, k * P:(k + 1) * P],
                                        wr[:, k, m * 2 * D:(m + 1) * 2 * D], start=(k == 0), stop=(k == KD - 1))
                    ins.then_inc(product_done, 1)

            with pe.Fori(0, U) as i:
                for u in range(U):
                    front.turn(pe, i * U + u, u)
                    if u >= 1:
                        products(i * U + (u - 1), u - 1)
                products(i * U + (U - 1), U - 1)


def relations(p: Program):
    nc, a = p.nc, p.a
    with p.phase() as ctx:
        def sb(n, s, d):
            return ctx.enter_context(nc.sbuf_tensor(n, s, d))

        key_i = sb("rel_key_i", [P, NT + 1, WIN], I32)
        weight = sb("rel_weight", [P, NT, WIN], F32)
        idx = [sb(f"rel_idx{s}", [P, JCOL], I32) for s in range(SLOTS)]
        rows = [sb(f"rel_rows{s}", [P, JCOL, D], F32) for s in range(SLOTS)]
        t_pos = sb("rt_pos", [P, 3], F32)
        t_at_i = sb("rt_at_i", [P, 1], I32)
        t_win = sb("rt_win", [P, 2 * WIN], F32)
        t_idx_i = sb("rt_idx_i", [P, JCOL], I32)
        t_w = sb("rt_w", [P, JCOL], F32)
        tables, step = p.sem("rel_tables"), p.sem("rel_step")
        per_slot = lambda name: [p.sem(f"rel_{name}{s}") for s in range(SLOTS)]
        idx_ready, gathered, used, steps_s = (per_slot(x) for x in ("idx_ready", "gathered", "used", "steps_s"))
        t_at, t_window, t_idx, t_rows, t_done, t_steps, t_begin = (
            p.sem(f"rel_t_{x}") for x in ("at", "window", "idx", "rows", "done", "steps", "begin"))
        block = ctx.enter_context(nc.Block())

        def items(eng, t):
            return eng.value_load(p.items[0:1, bass.ds(t, 1)], min_val=1, max_val=-(-N_EDGES // JCOL))

        def tail_base(eng, t):
            return eng.value_load(p.tails[0:1, bass.ds(t, 1)], min_val=0, max_val=N_EDGES)

        @block.gpsimd
        def _(pool):
            pool.wait_ge(tables, 1)
            with pool.Fori(0, NT) as t:
                n = items(pool, t)

                def gather(s):
                    pool.wait_ge(idx_ready[s], t + 1)
                    pool.wait_ge(used[s], t + 1)
                    p.alone(pool)
                    for j in range(JCOL):
                        pool.indirect_dma_start(out=rows[s][:, j, :], out_offset=None, in_=p.transformed[:],
                                                in_offset=bass.IndirectOffsetOnAxis(ap=idx[s][:, j:j + 1], axis=0))\
                            .then_inc(gathered[s], 16)

                gather(0)
                for s in range(1, SLOTS):
                    with pool.If(n > s):
                        gather(s)
                with pool.If(n > SLOTS):
                    c0 = tail_base(pool, t)
                    with pool.Fori(SLOTS, n) as k:
                        c = c0 + k - SLOTS
                        pool.wait_ge(t_at, c + 1)
                        p.alone(pool)
                        pool.indirect_dma_start(out=t_win[:], out_offset=None, in_=p.windows[:],
                                                in_offset=bass.IndirectOffsetOnAxis(ap=t_at_i[:, 0:1], axis=0)).then_inc(t_window, 16)
                        pool.wait_ge(t_idx, c + 1)
                        p.alone(pool)
                        for j in range(JCOL):
                            pool.indirect_dma_start(out=rows[0][:, j, :], out_offset=None, in_=p.transformed[:],
                                                    in_offset=bass.IndirectOffsetOnAxis(ap=t_idx_i[:, j:j + 1], axis=0))\
                                .then_inc(t_rows, 16)
                        pool.wait_ge(t_done, c + 1)
                        p.alone(pool)

        @block.scalar
        def _(act):
            act.wait_ge(tables, 1)
            for s in range(SLOTS):
                act.activation(idx[s][:], key_i[:, 0, s * JCOL:(s + 1) * JCOL], ACT.Copy).then_inc(idx_ready[s], 1)
            with act.Fori(0, NT) as t:
                n = items(act, t)

                def item(s):
                    act.wait_ge(gathered[s], 16 * JCOL * (t + 1))
                    p.alone(act)
                    act.activation(idx[s][:], key_i[:, bass.ds(t + 1, 1), s * JCOL:(s + 1) * JCOL].rearrange("q o j -> q (o j)"),
                                   ACT.Copy).then_inc(idx_ready[s], 1)

                item(0)
                for s in range(1, SLOTS):
                    with act.If(n > s):
                        item(s)

        @block.vector
        def _(dve):
            chain = Chain(p, dve, step)
            chain(dve.tensor_copy(key_i[:, 0:NT, :], p.win[:, :, 0:WIN]))
            chain(dve.memset(key_i[:, NT, :], 0))
            chain(dve.tensor_tensor(weight[:], spread(p.count[:, 0:WIN], 1, [P, NT, WIN]),
                                    p.rec[:, :, C_DEG:C_DEG + 1].broadcast_to([P, NT, WIN]), ALU.is_lt))
            dve.tensor_tensor(weight[:], weight[:], p.win[:, :, WIN:2 * WIN], ALU.mult).then_inc(tables, 1)
            dve.wait_ge(tables, 1)
            for s in range(SLOTS):
                dve.sem_inc(used[s], 1)
            chain_s = [Chain(p, dve, x) for x in steps_s]
            chain_k = Chain(p, dve, t_steps)
            TAIL_STEPS = 7

            def add(t, s, w, chain, finished):
                x = p.rec[:, bass.ds(t, 1), 0:D].rearrange("q o d -> q (o d)")
                for j in range(JCOL):
                    ins = dve.scalar_tensor_tensor(x, rows[s][:, j, :], w(j), x, ALU.mult, ALU.add)
                    if j < JCOL - 1:
                        chain(ins)
                    else:
                        ins.then_inc(finished, 1)

            with dve.Fori(0, NT) as t:
                n = items(dve, t)

                def item(s):
                    chain_s[s].at(t * (JCOL - 1))
                    dve.wait_ge(gathered[s], 16 * JCOL * (t + 1))
                    add(t, s, lambda j: weight[:, bass.ds(t, 1), s * JCOL + j:s * JCOL + j + 1].rearrange("q o c -> q (o c)"),
                        chain_s[s], used[s])
                    dve.wait_ge(used[s], t + 2)
                    p.alone(dve)

                item(0)
                for s in range(1, SLOTS):
                    with dve.If(n > s):
                        item(s)
                with dve.If(n > SLOTS):
                    c0 = tail_base(dve, t)
                    dve.tensor_scalar(t_pos[:, 0:1], tile_row(p, t, C_START, C_START + 1), float(WIN), None, ALU.add)
                    dve.tensor_scalar(t_pos[:, 1:2], tile_row(p, t, C_DEG, C_DEG + 1), -float(WIN), None, ALU.add).then_inc(t_begin, 1)
                    dve.wait_ge(t_begin, t + 1)
                    p.alone(dve)
                    with dve.Fori(SLOTS, n) as k:
                        c = c0 + k - SLOTS
                        chain_k.at(c * TAIL_STEPS)
                        dve.tensor_scalar(t_at_i[:], t_pos[:, 0:1], float(N_EDGES), None, ALU.min).then_inc(t_at, 1)
                        dve.wait_ge(t_window, 16 * (c + 1))
                        p.alone(dve)
                        dve.tensor_copy(t_idx_i[:], t_win[:, 0:JCOL]).then_inc(t_idx, 1)
                        chain_k(dve.tensor_scalar(t_w[:], p.count[:, 0:JCOL], t_pos[:, 1:2], None, ALU.is_lt))
                        chain_k(dve.tensor_tensor(t_w[:], t_w[:], t_win[:, WIN:WIN + JCOL], ALU.mult))
                        dve.wait_ge(t_rows, 16 * JCOL * (c + 1))
                        add(t, 0, lambda j: t_w[:, j:j + 1], chain_k, t_done)
                        dve.wait_ge(t_done, c + 1)
                        p.alone(dve)
                        chain_k(dve.tensor_scalar(t_pos[:, 0:1], t_pos[:, 0:1], float(JCOL), None, ALU.add))
                        chain_k(dve.tensor_scalar(t_pos[:, 1:2], t_pos[:, 1:2], -float(JCOL), None, ALU.add))
                        assert chain_k.n == TAIL_STEPS, chain_k.n


def choose_two(p: Program):
    nc, a = p.nc, p.a
    with p.phase() as ctx:
        def sb(n, s, d):
            return ctx.enter_context(nc.sbuf_tensor(n, s, d))

        front = Front(p, ctx, "two")
        real = sb("real", [P, NT], F32)
        sums = sb("col_sums", [P, KD], F32)
        wr = sb("wr1", [P, KD, E1], F32)
        br = sb("br1", [1, E1], F32)
        row = sb("row1", [1, 10, E1], F32)
        one = sb("one1", [1, 12], F32)
        real_ready, w_in, taken, mean_ready, logits_done, steps, exp_ready, exp_done, pair_ready, spread_done = (
            p.sem(f"two_{x}") for x in ("real_ready", "w_in", "taken", "mean_ready", "logits_done", "steps",
                                        "exp_ready", "exp_done", "pair_ready", "spread_done"))
        block = ctx.enter_context(nc.Block())
        logit, e, rw, s, eq, rev, s2, q = (row[:, n, :] for n in range(8))
        pair = one[:, 10:12]

        @block.sync
        def _(sp):
            sp.dma_start(wr[:], a["L1_ffn_Wr"].rearrange("(k q) e -> q k e", q=P)).then_inc(w_in, 16)
            sp.dma_start(br[:], a["L1_ffn_br"].rearrange("(o e) -> o e", o=1)).then_inc(w_in, 16)

        @block.tensor
        def _(pe):
            pe.wait_ge(real_ready, 1)
            front.start(pe, front.turned)

            with pe.Fori(0, U) as i:
                pe.wait_ge(taken, i + 1)
                p.alone(pe)
                for u in range(U):
                    g = i * U + u
                    pe.wait_ge(front.normed, done(g))
                    p.alone(pe)
                    for k in range(KD):
                        ins = pe.matmul(p.bank[k][:, 0:1], front.xn[u][:, k * P:(k + 1) * P], real[:, bass.ds(g, 1)],
                                        start=(u == 0), stop=(u == U - 1))
                    ins.then_inc(front.turned, 1)
            pe.wait_ge(w_in, 32)
            pe.wait_ge(mean_ready, 1)
            for k in range(KD):
                ins = pe.matmul(p.bank[2][0:1, 0:E1], sums[:, k:k + 1], wr[:, k, :], start=(k == 0), stop=(k == KD - 1))
            ins.then_inc(logits_done, 1)
            pe.wait_ge(pair_ready, 1)
            pe.matmul(p.bank[3][:, 0:2], p.ones[0:1, :], pair, start=True, stop=True).then_inc(spread_done, 1)

        @block.scalar
        def _(act):
            front.start(act, front.rooted)
            with act.Fori(0, U) as i:
                for u in range(U):
                    front.root(act, i * U + u, u)
            for n, (out, in_) in enumerate(((e, logit), (s, q), (one[:, 6:7], one[:, 5:6]))):
                act.wait_ge(exp_ready, n + 1)
                act.activation(out, in_, ACT.Exp).then_inc(exp_done, 1)

        @block.vector
        def _(dve):
            chain = Chain(p, dve, steps)
            dve.memset(sums[:], 0.0)
            dve.tensor_scalar(real[:], p.rec[:, :, C_ID], float(N_NODES), None, ALU.is_lt).then_inc(real_ready, 1)
            dve.wait_ge(real_ready, 1)
            front.start(dve, front.varied, front.normed)
            dve.sem_inc(taken, 1)
            K = front.STEPS + 1
            with dve.Fori(0, U) as i:
                chain.at(i * (K * U + KD))
                front.moments(dve, chain, tile_row(p, i * U), i * U, 0)
                for u in range(U):
                    g = i * U + u
                    if u + 1 < U:
                        front.moments(dve, chain, tile_row(p, g + 1), g + 1, u + 1)
                    front.norm(dve, chain, tile_row(p, g), g, u)
                    p.alone(dve)
                    chain(dve.tensor_copy(tile_row(p, g, D, D + 4), front.ms[:, u, :]))
                dve.wait_ge(front.turned, done(i * U + (U - 1)))
                p.alone(dve)
                for k in range(KD):
                    chain(dve.tensor_tensor(sums[:, k:k + 1], sums[:, k:k + 1], p.bank[k][:, 0:1], ALU.add))
                dve.sem_inc(taken, 1)
                assert chain.n == K * U + KD
            chain.at((K * U + KD) * U)
            dve.tensor_scalar(sums[:], sums[:], 1.0 / N_NODES, None, ALU.mult).then_inc(mean_ready, 1)
            dve.wait_ge(w_in, 32)
            dve.wait_ge(logits_done, 1)

            def softmax(n, x, out):
                chain(dve.tensor_reduce(one[:, 0:1], x, AX, ALU.max))
                dve.tensor_scalar(x, x, one[:, 0:1], None, ALU.subtract).then_inc(exp_ready, 1)
                dve.wait_ge(exp_done, n)
                chain(dve.tensor_reduce(one[:, 1:2], out, AX, ALU.add))
                chain(dve.reciprocal(one[:, 2:3], one[:, 1:2]))

            chain(dve.tensor_tensor(logit, p.bank[2][0:1, 0:E1], br[:], ALU.add))
            softmax(1, logit, e)
            chain(dve.tensor_scalar(rw, e, one[:, 2:3], None, ALU.mult))
            chain(dve.tensor_scalar(q, rw, CAPACITY / N_NODES, None, ALU.min))
            softmax(2, q, s)
            chain(dve.tensor_scalar(s, s, one[:, 2:3], None, ALU.mult))
            chain(dve.tensor_scalar(rev, p.count[0:1, 0:E1], -1.0, float(E1), ALU.mult, ALU.add))

            def largest(x, value, at):
                chain(dve.tensor_reduce(value, x, AX, ALU.max))
                chain(dve.tensor_scalar(eq, x, value, None, ALU.is_ge))
                chain(dve.tensor_tensor(eq, eq, rev, ALU.mult))
                chain(dve.tensor_reduce(at, eq, AX, ALU.max))

            largest(s, one[:, 3:4], one[:, 8:9])
            chain(dve.tensor_scalar(s2, rev, one[:, 8:9], -2.0, ALU.is_equal, ALU.mult))
            chain(dve.tensor_tensor(s2, s2, s, ALU.add))
            largest(s2, one[:, 4:5], one[:, 9:10])
            chain(dve.tensor_scalar(one[:, 8:10], one[:, 8:10], -1.0, float(E1), ALU.mult, ALU.add))
            chain(dve.tensor_copy(p.two_i[:], one[:, 8:10]))
            dve.tensor_tensor(one[:, 5:6], one[:, 4:5], one[:, 3:4], ALU.subtract).then_inc(exp_ready, 1)
            dve.wait_ge(exp_done, 3)
            chain(dve.tensor_scalar(one[:, 7:8], one[:, 6:7], 1.0, None, ALU.add))
            chain(dve.reciprocal(pair[:, 0:1], one[:, 7:8]))
            dve.tensor_tensor(pair[:, 1:2], pair[:, 0:1], one[:, 6:7], ALU.mult).then_inc(pair_ready, 1)
            dve.wait_ge(spread_done, 1)
            chain(dve.tensor_copy(p.two_w[:], p.bank[3][:, 0:2]))


def feed_forward(p: Program):
    nc, a = p.nc, p.a
    G, PAIRS = 4, NT // 8
    assert PAIRS * 2 * G + 1 == NT
    F = H1 // P
    EF = 2 * F
    with p.phase() as ctx:
        def sb(n, s, d):
            return ctx.enter_context(nc.sbuf_tensor(n, s, d))

        w1 = sb("ff_w1", [P, 2, KD, H1], F32)
        w2 = sb("ff_w2", [P, EF, D], F32)
        b1_rows = sb("ff_b1_rows", [EF, P], F32)
        b1 = sb("ff_b1", [P, EF], F32)
        b2 = sb("ff_b2", [P, 2, D], F32)
        gb = sb("ff_gb", [P, 2, D], F32)
        xg = [sb(f"ff_xg{s}", [P, G, D], F32) for s in range(2)]
        xt = [sb(f"ff_xt{s}", [P, KD, G * P], F32) for s in range(2)]
        gt = [sb(f"ff_gt{s}", [P, EF, G * P], F32) for s in range(2)]
        y = [sb(f"ff_y{j}", [P, D], F32) for j in range(G)]
        z = [sb(f"ff_z{j}", [P, D], F32) for j in range(G)]
        stats = sb("ff_stats", [P, G, 6], F32)
        ms = sb("ff_ms", [P, G, 4], F32)
        at = [sb(f"ff_at{j}", [P, 1], I32) for j in range(G)]
        w_in, scaled, normed, turned, copied, hidden, gelued, out_done, taken, varied, rooted, finished, steps, setup = (
            p.sem(f"ff_{x}") for x in ("w_in", "scaled", "normed", "turned", "copied", "hidden", "gelued",
                                       "out_done", "taken", "varied", "rooted", "finished", "steps", "setup"))
        b1_turned, b1_ready = p.sem("ff_b1_turned"), p.sem("ff_b1_ready")
        stored = [p.sem(f"ff_stored{j}") for j in range(G)]
        block = ctx.enter_context(nc.Block())

        LAST = 2 * PAIRS

        @block.sync
        def _(sp):
            for n in range(2):
                e = sp.value_load(p.two_i[0:1, n:n + 1], min_val=0, max_val=E1 - 1)
                sp.dma_start(w1[:, n], a["L1_ffn_W1"][bass.ds(e, 1)].rearrange("o (k q) f -> q (o k) f", q=P)).then_inc(w_in, 16)
                sp.dma_start(w2[:, n * F:(n + 1) * F], a["L1_ffn_W2"][bass.ds(e, 1)].rearrange("o (f q) d -> q (o f) d", q=P)).then_inc(w_in, 16)
                sp.dma_start(b1_rows[n * F:(n + 1) * F, :], a["L1_ffn_b1"][bass.ds(e, 1)].rearrange("o (f q) -> (o f) q", q=P)).then_inc(w_in, 16)
                sp.dma_start(b2[:, n], a["L1_ffn_b2"][bass.ds(e, 1)].broadcast_to([P, D])).then_inc(w_in, 16)
            for n, name in enumerate(("L1_ffn_gamma", "L1_ffn_beta")):
                sp.dma_start(gb[:, n], bass.AP(tensor=a[name].tensor, offset=0, ap=[[0, P], [1, D]])).then_inc(w_in, 16)

        @block.tensor
        def _(pe):
            for s in (turned, hidden, out_done):
                pe.sem_inc(s, U)
            pe.wait_ge(w_in, 16 * 10)
            pe.transpose(p.bank[6][:, 0:EF], b1_rows[:], p.ident[0:EF, 0:EF]).then_inc(b1_turned, 1)

            def into(g, slot, tiles):
                pe.wait_ge(normed, done(g))
                for j in range(tiles):
                    c = g * G + j
                    pe.wait_ge(copied, done(c - 2))
                    for k in range(KD):
                        ins = pe.transpose(p.bank[j % 2][:, k * P:(k + 1) * P], xg[slot][:, j, k * P:(k + 1) * P], p.ident[:])
                    ins.then_inc(turned, 1)
                pe.wait_ge(copied, done(g * G + (tiles - 1)))
                for ef in range(EF):
                    pe.wait_ge(gelued, done(g * EF + ef - 4))
                    for k in range(KD):
                        ins = pe.matmul(p.bank[2 + ef % 4][:, 0:tiles * P], w1[:, ef // F, k, (ef % F) * P:(ef % F + 1) * P],
                                        xt[slot][:, k, 0:tiles * P], start=(k == 0), stop=(k == KD - 1))
                    ins.then_inc(hidden, 1)

            def outof(g, slot, tiles):
                pe.wait_ge(gelued, done(g * EF + (EF - 1)))
                for j in range(tiles):
                    pe.wait_ge(taken, done(g * G + j - 2))
                    for ef in range(EF):
                        ins = pe.matmul(p.bank[6 + j % 2][:, 0:D], gt[slot][:, ef, j * P:(j + 1) * P], w2[:, ef, :],
                                        start=(ef == 0), stop=(ef == EF - 1))
                    ins.then_inc(out_done, 1)

            pe.wait_ge(scaled, EF)
            pe.wait_ge(b1_ready, 1)
            with pe.Fori(0, PAIRS) as i:
                into(i * 2, 0, G)
                into(i * 2 + 1, 1, G)
                outof(i * 2, 0, G)
                outof(i * 2 + 1, 1, G)
            into(LAST, 0, 1)
            outof(LAST, 0, 1)

        @block.scalar
        def _(act):
            for s in (copied, gelued, rooted):
                act.sem_inc(s, U)
            act.wait_ge(b1_ready, 1)

            def group(g, slot, tiles):
                for j in range(tiles):
                    act.wait_ge(turned, done(g * G + j))
                    act.activation(xt[slot][:, :, j * P:(j + 1) * P], p.bank[j % 2][:, 0:D].rearrange("q (k c) -> q k c", c=P),
                                   ACT.Copy).then_inc(copied, 1)
                act.wait_ge(out_done, done(g * G - 2 * G + (G - 1)))
                p.alone(act)
                for ef in range(EF):
                    act.wait_ge(hidden, done(g * EF + ef))
                    act.activation(gt[slot][:, ef, 0:tiles * P], p.bank[2 + ef % 4][:, 0:tiles * P], ACT.Gelu,
                                   bias=b1[:, ef:ef + 1]).then_inc(gelued, 1)

            def roots(g, tiles):
                act.wait_ge(varied, done(g))
                act.activation(ms[:, 0:tiles, 2], ms[:, 0:tiles, 1], ACT.Sqrt, bias=p.eps[:, 0:1]).then_inc(rooted, 1)

            with act.Fori(0, PAIRS) as i:
                group(i * 2, 0, G)
                group(i * 2 + 1, 1, G)
                roots(i * 2, G)
                roots(i * 2 + 1, G)
            group(LAST, 0, 1)
            roots(LAST, 1)

        @block.gpsimd
        def _(pool):
            def group(g, tiles):
                for j in range(tiles):
                    pool.wait_ge(finished, done(g * G + j))
                    p.alone(pool)
                    pool.indirect_dma_start(out=p.a["out"], out_offset=bass.IndirectOffsetOnAxis(ap=at[j][:, 0:1], axis=0),
                                            in_=z[j][:], in_offset=None).then_inc(stored[j], 16)

            for j in range(G):
                pool.dma_start(at[j][:], a["src"][0:P].rearrange("(q o) -> q o", o=1)).then_inc(stored[j], 16)
            with pool.Fori(0, PAIRS) as i:
                group(i * 2, G)
                group(i * 2 + 1, G)
            group(LAST, 1)
            for j in range(G):
                pool.wait_ge(stored[j], 16 * (1 + 2 * PAIRS + (j == 0)))

        @block.vector
        def _(dve):
            chain, first = Chain(p, dve, steps), Chain(p, dve, setup)
            for s in (normed, taken, varied, finished):
                dve.sem_inc(s, U)
            dve.wait_ge(w_in, 16 * 10)
            dve.wait_ge(b1_turned, 1)
            dve.tensor_copy(b1[:], p.bank[6][:, 0:EF]).then_inc(b1_ready, 1)
            for ef in range(EF):
                dve.tensor_scalar(w2[:, ef, :], w2[:, ef, :], p.two_w[:, ef // F:ef // F + 1], None, ALU.mult).then_inc(scaled, 1)
            first(dve.tensor_scalar(b2[:, 0, :], b2[:, 0, :], p.two_w[:, 0:1], None, ALU.mult))
            first(dve.scalar_tensor_tensor(b2[:, 0, :], b2[:, 1, :], p.two_w[:, 1:2], b2[:, 0, :], ALU.mult, ALU.add))

            def norm(g, slot, tiles):
                dve.wait_ge(turned, done(g * G - 2 * G + (G - 1)))
                dve.wait_ge(finished, done(g * G - 2 * G + (G - 1)))
                p.alone(dve)
                for j in range(tiles):
                    c = g * G + j
                    ins = dve.tensor_scalar(xg[slot][:, j, :], tile_row(p, c), tile_row(p, c, D, D + 1), tile_row(p, c, D + 3, D + 4),
                                            ALU.subtract, ALU.mult)
                ins.then_inc(normed, 1)
                dve.wait_ge(normed, done(g))

            def final(g, slot, tiles, before):
                chain.at(before)
                dve.wait_ge(finished, done(g * G - 1))
                for j in range(tiles):
                    dve.wait_ge(out_done, done(g * G + j))
                    p.alone(dve)
                    dve.tensor_tensor(y[j][:], p.bank[6 + j % 2][:, 0:D], xg[slot][:, j, :], ALU.add).then_inc(taken, 1)
                    dve.wait_ge(taken, done(g * G + j))
                    p.alone(dve)
                    chain(dve.tensor_tensor(y[j][:], y[j][:], b2[:, 0, :], ALU.add), True)
                    chain(dve.bn_stats(stats[:, j, :], y[j][:]), True)
                    ins = dve.bn_aggr(ms[:, j, 0:2], stats[:, j, :])
                ins.then_inc(varied, 1)
                for j in range(tiles):
                    dve.wait_ge(stored[j], 16 * (g + 1))
                    p.alone(dve)
                    dve.tensor_copy(at[j][:], p.id_i[:, bass.ds(g * G + j, 1)])
                dve.wait_ge(rooted, done(g))
                chain(dve.reciprocal(ms[:, 0:tiles, 3], ms[:, 0:tiles, 2]), True)
                for op in range(3):
                    for j in range(tiles):
                        ins = (lambda: dve.tensor_scalar(y[j][:], y[j][:], ms[:, j, 0:1], ms[:, j, 3:4], ALU.subtract, ALU.mult),
                               lambda: dve.tensor_tensor(y[j][:], y[j][:], gb[:, 0, :], ALU.mult),
                               lambda: dve.tensor_tensor(y[j][:], y[j][:], gb[:, 1, :], ALU.add))[op]()
                    chain(ins, True)
                for j in range(tiles):
                    dve.tensor_tensor(z[j][:], y[j][:], tile_row(p, g * G + j), ALU.add).then_inc(finished, 1)
                return chain.n

            K = 2 * G + 4
            with dve.Fori(0, PAIRS) as i:
                norm(i * 2, 0, G)
                norm(i * 2 + 1, 1, G)
                assert final(i * 2, 0, G, i * (2 * K)) == K
                assert final(i * 2 + 1, 1, G, i * (2 * K) + K) == K
            norm(LAST, 0, 1)
            final(LAST, 0, 1, PAIRS * 2 * K)


def build(nc, a):
    with ExitStack() as ctx:
        p = Program(nc, ctx, a)
        search_and_project(p)
        attention(p)
        route(p)
        experts(p)
        transform(p)
        relations(p)
        choose_two(p)
        feed_forward(p)



_INS = ["x", "src", "dst", "edge_type_16", "edge_weight1", "L0_gnn_W", "L0_gnn_att_src", "L0_gnn_att_dst", "L0_gnn_bias",
        "L0_ffn_router_w", "L0_ffn_router_b", "L0_ffn_W1", "L0_ffn_b1", "L0_ffn_W2", "L0_ffn_b2", "L1_gnn_weight",
        "L1_ffn_Wr", "L1_ffn_br", "L1_ffn_W1", "L1_ffn_b1", "L1_ffn_W2", "L1_ffn_b2", "L1_ffn_gamma", "L1_ffn_beta"]


def layout(inputs):
    import numpy as np
    arrays = {n: np.ascontiguousarray(inputs[n]) for n in _INS}
    arrays["x"] = np.pad(arrays["x"], ((0, NP - N_NODES), (0, 0)))
    arrays["dst"] = np.pad(arrays["dst"], (0, CG * P * P - N_EDGES), constant_values=2 * NP)
    for n in ("src", "edge_type_16"):
        arrays[n] = np.pad(arrays[n], (0, EP + WIN - N_EDGES))
    arrays["edge_weight1"] = np.pad(arrays["edge_weight1"].reshape(-1), (0, EP + WIN - N_EDGES))
    return arrays


def kernel(**inputs):
    import numpy as np
    import concourse.bacc as bacc
    from concourse.bass_utils import run_bass_kernel_spmd

    arrays = layout(inputs)
    nc = bacc.Bacc("TRN2", target_bir_lowering=False, num_devices=1)
    aps = {n: nc.dram_tensor(n, v.shape, mybir.dt.from_np(v.dtype), kind="ExternalInput").ap() for n, v in arrays.items()}
    aps["out"] = nc.dram_tensor("out", (NP, D), F32, kind="ExternalOutput").ap()
    build(nc, aps)
    r = run_bass_kernel_spmd(nc, [arrays], core_ids=[0])
    return r.results[0]["out"][:N_NODES]
```

```python
from contextlib import ExitStack, contextmanager

import concourse.bass as bass
import concourse.mybir as mybir

F32 = mybir.dt.float32
BF16 = mybir.dt.bfloat16
I32 = mybir.dt.int32
U32 = mybir.dt.uint32
ALU = mybir.AluOpType
ACT = mybir.ActivationFunctionType
AX = mybir.AxisListType.X

P = 128
N_NODES, N_EDGES, D = 6250, 100000, 256
NT = -(-N_NODES // P)
NP = NT * P
HEADS, HEAD_DIM = 8, 32
HW = HEAD_DIM + 1
HROW = HEADS * HW
RELS = 16
KD = D // P
EPS = 1e-5
C_ADST, C_START, C_DEG, C_ID, REC = D, D + HEADS, D + HEADS + 1, D + HEADS + 2, D + HEADS + 4
CHUNKS = -(-N_EDGES // P)
CG = -(-CHUNKS // P)
STRIP = CHUNKS
EP = P * STRIP
WIN = 32
SLICE = 23
SLICES = STRIP // SLICE
JCOL = 4
COLS = [2 * JCOL] + [JCOL] * (WIN // JCOL - 2)
SLOTS = len(COLS)
AT = [sum(COLS[:s]) for s in range(SLOTS)]
LAST = SLOTS - 1
assert sum(COLS) == WIN and COLS[LAST] == JCOL
DBINS = 64
E0, H0 = 32, 64
XCH = NT + E0 - 1
E1, H1 = 8, 512
CAPACITY = float(-(-N_NODES * 5 // (4 * E1)))
NEVER = -3e38
LOWEST = -1e38
U = 7
assert U * U == NT and SLICES * SLICE == STRIP


class Chain:

    def __init__(self, p, eng, sem):
        self.p, self.eng, self.sem, self.base, self.n = p, eng, sem, 0, 0

    def at(self, base):
        self.base, self.n = base, 0

    def total(self):
        return self.base + self.n

    def __call__(self, ins, alone=False):
        ins.then_inc(self.sem, 1)
        self.n += 1
        self.eng.wait_ge(self.sem, self.base + self.n)
        if alone:
            self.p.alone(self.eng)


def spread(ap, axis, shape):
    return ap.unsqueeze(axis).broadcast_to(shape)


class Program:
    def __init__(self, nc, ctx, a):
        self.nc, self.ctx, self.a = nc, ctx, a
        self.in_use = []
        self.bank = [ctx.enter_context(nc.psum_tensor(f"bank{i}", [P, 512], F32)) for i in range(8)]
        self.ident = self.keep("ident", [P, P], F32)
        self.ones = self.keep("ones", [P, P], F32)
        self.earlier = self.keep("earlier", [P, P], BF16)
        self.onesb = self.keep("onesb", [P, P], BF16)
        self.count = self.keep("count", [P, DBINS], F32)
        self.node = self.keep("node", [P, NT + 1], F32)
        self.rec = self.keep("rec", [P, NT, REC], F32)
        self.eps = self.keep("eps", [P, 1], F32)
        self.win = self.keep("win", [P, NT, 2 * WIN], F32)
        self.start_i = self.keep("start_i", [P, NT], I32)
        self.id_i = self.keep("id_i", [P, NT], I32)
        self.items = self.keep("items", [1, NT], I32)
        self.tails = self.keep("tails", [1, NT], I32)
        self.place_i = self.keep("place_i", [P, NT], I32)
        self.chunk_e_i = self.keep("chunk_e_i", [1, XCH], I32)
        self.two_i = self.keep("two_i", [1, 2], I32)
        self.two_w = self.keep("two_w", [P, 2], F32)
        self.ms = self.keep("ms", [P, NT, 4], F32)
        self.passed = self.sem("passed")
        self.ready = self.sem("ready")
        self.h_table = nc.dram_tensor("h_table", (NP, HROW), F32, kind="Internal").ap()
        self.windows = nc.dram_tensor("windows", (EP, 2 * WIN), F32, kind="Internal").ap()
        self.records = nc.dram_tensor("records", (NP, REC), F32, kind="Internal").ap()
        self.x_grouped = nc.dram_tensor("x_grouped", (XCH * P, REC), F32, kind="Internal").ap()
        self.y_grouped = nc.dram_tensor("y_grouped", (XCH * P, D), F32, kind="Internal").ap()
        self.transformed = nc.dram_tensor("transformed", (NP * RELS, D), F32, kind="Internal").ap()

    def alone(self, eng):
        eng.sem_inc(self.passed, 1)

    def keep(self, name, shape, dt):
        return self.ctx.enter_context(self.nc.sbuf_tensor(name, shape, dt))

    def sem(self, name):
        self.in_use.append(self.nc.alloc_semaphore(name))
        return self.in_use[-1]

    @contextmanager
    def phase(self):
        kept, self.in_use = self.in_use, []
        with ExitStack() as ctx:
            yield ctx
        self.nc.all_engine_barrier()
        self.nc.clear_and_free_semaphores(self.in_use)
        self.nc.all_engine_barrier()
        self.in_use = kept


class Front:

    LAG = 2

    def __init__(self, p, ctx, name):
        nc = p.nc
        self.p = p
        self.xn = [ctx.enter_context(nc.sbuf_tensor(f"{name}_xn{u}", [P, D], F32)) for u in range(U)]
        self.xt = [ctx.enter_context(nc.sbuf_tensor(f"{name}_xt{u}", [P, D], F32)) for u in range(U)]
        self.stats = ctx.enter_context(nc.sbuf_tensor(f"{name}_stats", [P, NT, 6], F32))
        self.varied, self.rooted, self.normed, self.turned, self.copied = (
            p.sem(f"{name}_{x}") for x in ("varied", "rooted", "normed", "turned", "copied"))

    def moments(self, dve, chain, row):
        ms = self.p.ms
        for t in range(NT):
            ins = dve.bn_stats(self.stats[:, t, :], row(t))
        chain(ins)
        for t in range(NT):
            ins = dve.bn_aggr(ms[:, t, 0:2], self.stats[:, t, :])
        ins.then_inc(self.varied, 1)
        dve.wait_ge(self.rooted, 1)
        chain(dve.reciprocal(ms[:, :, 3], ms[:, :, 2]))

    def root(self, act):
        ms = self.p.ms
        act.wait_ge(self.varied, 1)
        act.activation(ms[:, :, 2], ms[:, :, 1], ACT.Sqrt, bias=self.p.eps[:, 0:1]).then_inc(self.rooted, 1)

    def norm(self, dve, x, g, u):
        ms = self.p.ms
        dve.wait_ge(self.turned, done(g - U))
        dve.tensor_scalar(self.xn[u][:], x, ms[:, bass.ds(g, 1), 0:1].rearrange("q o c -> q (o c)"),
                          ms[:, bass.ds(g, 1), 3:4].rearrange("q o c -> q (o c)"),
                          ALU.subtract, ALU.mult).then_inc(self.normed, 1)

    def turn(self, pe, g, u):
        pe.wait_ge(self.normed, done(g))
        pe.wait_ge(self.copied, done(g - 3))
        for k in range(KD):
            ins = pe.transpose(self.p.bank[u % 4][:, k * P:(k + 1) * P], self.xn[u][:, k * P:(k + 1) * P], self.p.ident[:])
        ins.then_inc(self.turned, 1)

    def copy(self, act, g, u, used):
        if used is not None:
            act.wait_ge(used, done(g - U))
        act.wait_ge(self.turned, done(g))
        act.activation(self.xt[u][:], self.p.bank[u % 4][:, 0:D], ACT.Copy).then_inc(self.copied, 1)

    def start(self, eng, *sems):
        for s in sems:
            eng.sem_inc(s, U)

    def scalar_loop(self, act, used, store=None):
        self.root(act)
        self.start(act, self.copied)
        with act.Fori(0, U) as i:
            for u in range(U if store is None else U + self.LAG):
                if u < U:
                    self.copy(act, i * U + u, u, used)
                if store is not None and u >= self.LAG:
                    store(i * U + (u - self.LAG), u - self.LAG)


def done(g):
    return g + (1 + U)


def rank_steps(dve, chain, hot, within, total, cum, base, tmp, rank, nb, align=None):
    chain(dve.memset(cum[:, 0, :], 0.0))
    for t in range(NT):
        chain(dve.tensor_tensor(cum[:, t + 1, :], cum[:, t, :], total[:, t, :], ALU.add))
    size, ends, part = base[:, 0, :], base[:, 1, :], base[:, 2, :]
    if align is not None:
        bits = P.bit_length() - 1
        chain(dve.tensor_scalar(align, cum[:, NT, :], float(P - 1), None, ALU.add))
        chain(dve.tensor_scalar(align, align, bits, bits, ALU.arith_shift_right, ALU.logical_shift_left))
        chain(dve.tensor_copy(size, align))
    else:
        chain(dve.tensor_copy(size, cum[:, NT, :]))
    chain(dve.memset(part, 0.0))
    chain(dve.tensor_tensor_scan(ends, size, part, 0.0, ALU.add, ALU.add))
    chain(dve.tensor_tensor(part, ends, size, ALU.subtract))
    chain(dve.tensor_tensor(tmp, within, cum[:, 0:NT, :], ALU.add))
    chain(dve.tensor_tensor(tmp, tmp, spread(part, 1, [P, NT, nb]), ALU.add))
    chain(dve.tensor_tensor(tmp, tmp, hot, ALU.mult))
    chain(dve.tensor_reduce(rank, tmp, AX, ALU.add))


def search_and_project(p: Program):
    nc, a = p.nc, p.a
    with p.phase() as ctx:
        def sb(n, s, d):
            return ctx.enter_context(nc.sbuf_tensor(n, s, d))

        xa = sb("xa", [P, NT, REC], F32)
        dst_rows = sb("dst_rows", [P, CG, P], I32)
        first = sb("first", [P, CG], F32)
        diag = sb("diag", [P, 2, P], F32)
        pivots = sb("pivots", [P, CG * P], F32)
        less = sb("less", [P, CG * P], BF16)
        chunks_below = sb("chunks_below", [P, NT + 1], F32)
        chunk = sb("chunk", [P, NT + 1], F32)
        chunk_i = sb("chunk_i", [P, NT + 1], I32)
        found = sb("found", [P, NT + 1, P], I32)
        start = sb("start", [P, NT + 1], F32)
        bin_ = sb("bin_", [P, NT], F32)
        hot = sb("hot", [P, NT, DBINS], BF16)
        scratch = p.rec[:].rearrange("q t c -> q (t c)")
        within, total, cum = (scratch[:, n * NT * DBINS:(n * NT + m) * DBINS].rearrange("q (t b) -> q t b", b=DBINS)
                              for n, m in ((0, NT), (1, NT), (2, NT + 1)))
        cmp = scratch[:, (3 * NT + 1) * DBINS:(3 * NT + 1) * DBINS + (NT + 1) * P // 2].bitcast(BF16)\
            .rearrange("q (t e) -> q t e", e=P)
        base = sb("base", [P, 3, DBINS], F32)
        rank = sb("rank", [P, NT], F32)
        rank_i = sb("rank_i", [P, NT], I32)
        shift = sb("shift", [P, 2, P], F32)
        s_src = sb("s_src", [P, STRIP + WIN], I32)
        s_typ = sb("s_typ", [P, STRIP + WIN], I32)
        s_key = sb("s_key", [P, STRIP + WIN], F32)
        s_wgt = sb("s_wgt", [P, STRIP + WIN], F32)
        w = SLICE * 2 * WIN
        wide = [p.win[:].rearrange("q t c -> q (t c)")[:, i * w:(i + 1) * w].rearrange("q (e c) -> q e c", c=2 * WIN) for i in range(2)]
        wa = sb("wa", [P, KD, HROW + HEADS], F32)
        att = sb("att", [P, 2, D], F32)
        prod = sb("prod", [P, D], F32)
        front = Front(p, ctx, "gat")
        hrow = [sb(f"hrow{i}", [P, HROW], F32) for i in range(U)]

        dst_in, x_in, w_in, att_in, edge_in = (p.sem(x) for x in ("dst_in", "x_in", "w_in", "att_in", "edge_in"))
        first_ready, pivots_ready, chunks_ready, found_in = (p.sem(x) for x in ("first_ready", "pivots_ready", "chunks_ready", "found_in"))
        diag_ready, piv_done = p.sem("diag_ready"), p.sem("piv_done")
        start_ready, next_done, hot_ready, counts_done, counts_out = (p.sem(x) for x in ("start_ready", "next_done", "hot_ready", "counts_done", "counts_out"))
        rank_ready, scattered, rec_in = p.sem("rank_ready"), p.sem("scattered"), p.sem("rec_in")
        key_ready, wide_ready, wide_out = p.sem("key_ready"), p.sem("wide_ready"), [p.sem(f"wide_out{i}") for i in range(2)]
        wa_ready, h_psum, h_ready = (p.sem(x) for x in ("wa_ready", "h_psum", "h_ready"))
        h_stored = [p.sem(f"h_stored{i}") for i in range(U)]
        steps_v, steps_g = p.sem("steps_v"), p.sem("steps_g")
        zero_out = p.sem("zero_out")
        EARLY = 11
        halves = [(0, 4), (4, 7)]
        block = ctx.enter_context(nc.Block())

        @block.sync
        def _(sp):
            sp.dma_start(dst_rows[:], a["dst"].rearrange("(g c e) -> c g e", c=P, e=P)).then_inc(dst_in, 16)
            for s, v in ((s_src, a["src"]), (s_typ, a["edge_type_16"]), (s_wgt, a["edge_weight1"])):
                strips = bass.AP(tensor=v.tensor, offset=0, ap=[[STRIP, P], [1, STRIP + WIN]])
                sp.dma_start(s[:], strips).then_inc(edge_in, 16)
            for i, n in enumerate(("L0_gnn_att_src", "L0_gnn_att_dst")):
                flat = a[n].rearrange("h d -> (h d)")
                sp.dma_start(att[:, i, :], bass.AP(tensor=flat.tensor, offset=0, ap=[[0, P], [1, D]])).then_inc(att_in, 16)
            for k in range(KD):
                sp.dma_start(wa[:, k, 0:HROW].rearrange("p (h c) -> p h c", c=HW)[:, :, 0:HEAD_DIM],
                             a["L0_gnn_W"][k * P:(k + 1) * P]).then_inc(w_in, 16)
            sp.dma_start(xa[:, :, 0:D], a["x"].rearrange("(t q) d -> q t d", q=P)).then_inc(x_in, 16)
            for q in range(SLICES):
                sp.wait_ge(wide_ready, q + 1)
                sp.dma_start(p.windows.rearrange("(q e) w -> q e w", q=P)[:, q * SLICE:(q + 1) * SLICE, :],
                             wide[q % 2]).then_inc(wide_out[q % 2], 16)
            for u in range(U):
                sp.wait_ge(h_stored[u], 16 * (U + 1))
            for i in range(2):
                sp.wait_ge(wide_out[i], 16 * ((SLICES + 1 - i) // 2))
            sp.wait_ge(scattered, 16 * NT)
            sp.dma_start(p.rec[:], p.records.rearrange("(t q) c -> q t c", q=P)).then_inc(rec_in, 16)
            sp.wait_ge(rec_in, 16)

        @block.gpsimd
        def _(pool):
            chain = Chain(p, pool, steps_g)
            chain(pool.memset(p.ident[:], 0.0))
            chain(pool.memset(p.ones[:], 1.0))
            chain(pool.memset(p.onesb[:], 1.0))
            chain(pool.memset(shift[:], 0.0))
            chain(pool.memset(p.eps[:], EPS))
            chain(pool.memset(p.earlier[:], 1.0))
            chain(pool.affine_select(out=p.ident[:], in_=p.ident[:], compare_op=ALU.not_equal, fill=1.0, base=0,
                                     pattern=[[-1, P]], channel_multiplier=1))
            chain(pool.affine_select(out=p.earlier[:], in_=p.earlier[:], compare_op=ALU.is_ge, fill=0.0, base=-1,
                                     pattern=[[1, P]], channel_multiplier=-1))
            chain(pool.affine_select(out=shift[:, 0, :], in_=shift[:, 0, :], compare_op=ALU.not_equal, fill=1.0, base=-1,
                                     pattern=[[-1, P]], channel_multiplier=1))
            chain(pool.affine_select(out=shift[:, 1, :], in_=shift[:, 1, :], compare_op=ALU.not_equal, fill=1.0, base=P - 1,
                                     pattern=[[-1, P]], channel_multiplier=P))
            chain(pool.iota(p.count[:], pattern=[[1, DBINS]], base=0, channel_multiplier=0,
                            allow_small_or_imprecise_dtypes=True))
            chain(pool.iota(p.node[:], pattern=[[P, NT + 1]], base=0, channel_multiplier=1,
                            allow_small_or_imprecise_dtypes=True))
            pool.memset(xa[:, :, D:REC], 0.0).then_inc(p.ready, 1)
            pool.wait_ge(p.ready, 1)
            pool.wait_ge(edge_in, 48)
            pool.wait_ge(key_ready, 1)

            def slices(lo, hi):
                for q in range(lo, hi):
                    if q >= 2:
                        pool.wait_ge(wide_out[q % 2], 16 * (q // 2))
                    for n, strip in enumerate((s_key, s_wgt)):
                        over = bass.AP(tensor=strip[:].tensor, offset=q * SLICE, ap=[[STRIP + WIN, P], [1, SLICE], [1, WIN]])
                        ins = pool.tensor_copy(wide[q % 2][:, :, n * WIN:(n + 1) * WIN], over)
                    ins.then_inc(wide_ready, 1)

            slices(0, EARLY)
            pool.wait_ge(chunks_ready, 1)
            table = a["dst"].rearrange("(c e) -> c e", e=P)
            for t in range(NT + 1):
                pool.indirect_dma_start(out=found[:, t, :], out_offset=None, in_=table,
                                        in_offset=bass.IndirectOffsetOnAxis(ap=chunk_i[:, t:t + 1], axis=0)).then_inc(found_in, 16)
            slices(EARLY, SLICES)
            pool.wait_ge(rank_ready, 1)
            pool.wait_ge(h_ready, done(NT - 1))
            for t in range(NT):
                pool.indirect_dma_start(out=p.records[:], out_offset=bass.IndirectOffsetOnAxis(ap=rank_i[:, t:t + 1], axis=0),
                                        in_=xa[:, t, :], in_offset=None).then_inc(scattered, 16)

        @block.vector
        def _(dve):
            chain = Chain(p, dve, steps_v)
            dve.wait_ge(edge_in, 48)
            dve.scalar_tensor_tensor(s_key[:], s_src[:], float(RELS), s_typ[:], ALU.mult, ALU.add).then_inc(key_ready, 1)
            dve.wait_ge(dst_in, 16)
            dve.wait_ge(p.ready, 1)
            chain(dve.tensor_copy(first[:], dst_rows[:, :, 0]))
            for g in range(CG):
                if g >= 2:
                    dve.wait_ge(piv_done, g - 1)
                dve.tensor_scalar(diag[:, g % 2, :], p.ident[:], first[:, g:g + 1], None, ALU.mult).then_inc(diag_ready, 1)
            for h in range(2):
                lo, hi = h * 4, min(4 * h + 4, CG)
                dve.wait_ge(piv_done, hi)
                chain(dve.tensor_copy(pivots[:, lo * P:hi * P], p.bank[h][:, 0:(hi - lo) * P]))
            before = chain.total()
            with dve.Fori(0, NT + 1) as t:
                chain.at(before + t)
                chain(dve.tensor_scalar(less[:], pivots[:], p.node[:, bass.ds(t, 1)], 0.0, ALU.is_lt, ALU.add,
                                        accum_out=chunks_below[:, bass.ds(t, 1)]))
            chain.at(before + NT + 1)
            chain(dve.tensor_scalar(chunk[:], chunks_below[:], -1.0, 0.0, ALU.add, ALU.max))
            dve.tensor_copy(chunk_i[:], chunk[:]).then_inc(chunks_ready, 1)
            dve.wait_ge(x_in, 16)
            front.moments(dve, chain, lambda t: xa[:, t, 0:D])
            dve.wait_ge(att_in, 32)
            dve.wait_ge(w_in, 16 * KD)
            for k in range(KD):
                heads = wa[:, k, 0:HROW].rearrange("q (h c) -> q h c", c=HW)
                for i, out in enumerate((heads[:, :, HEAD_DIM], wa[:, k, HROW:HROW + HEADS])):
                    chain(dve.tensor_tensor(prod[:].rearrange("q (h c) -> q h c", h=HEADS), heads[:, :, 0:HEAD_DIM],
                                            att[:, i, :].rearrange("q (h c) -> q h c", h=HEADS), ALU.mult))
                    chain(dve.tensor_reduce(out, prod[:].rearrange("q (h c) -> q h c", h=HEADS), AX, ALU.add))
            dve.tensor_copy(prod[:, 0:1], wa[:, 0, 0:1]).then_inc(wa_ready, 1)
            dve.wait_ge(found_in, 16 * (NT + 1))
            chain(dve.tensor_tensor(cmp, found[:], spread(p.node[:], 2, [P, NT + 1, P]), ALU.is_lt))
            chain(dve.tensor_reduce(start[:], cmp, AX, ALU.add))
            chain(dve.scalar_tensor_tensor(start[:], chunk[:], float(P), start[:], ALU.mult, ALU.add))
            dve.tensor_copy(xa[:, :, C_START], start[:, 0:NT]).then_inc(start_ready, 1)
            dve.wait_ge(next_done, 1)
            chain(dve.tensor_tensor(xa[:, :, C_DEG], p.bank[0][:, 0:NT], start[:, 0:NT], ALU.subtract))
            chain(dve.tensor_copy(xa[:, :, C_ID], p.node[:, 0:NT]))
            chain(dve.tensor_scalar(bin_[:], xa[:, :, C_DEG], -1.0, float(DBINS - 1), ALU.mult, ALU.add))
            chain(dve.tensor_scalar(bin_[:], bin_[:], 0.0, None, ALU.max))
            dve.tensor_tensor(hot[:], spread(bin_[:], 2, [P, NT, DBINS]), spread(p.count[:], 1, [P, NT, DBINS]),
                              ALU.is_equal).then_inc(hot_ready, 1)
            for lo, hi in halves:
                for g in range(lo, hi):
                    dve.wait_ge(counts_done, g + 1)
                    for n, to in enumerate((within, total)):
                        dve.tensor_copy(to[:, g * U:(g + 1) * U, :].rearrange("q t b -> q (t b)"),
                                        p.bank[2 * (g - lo) + n][:, 0:U * DBINS]).then_inc(counts_out, 1)
            dve.wait_ge(counts_out, 2 * U)
            rank_steps(dve, chain, hot[:], within, total, cum, base, within, rank[:], DBINS)
            dve.tensor_copy(rank_i[:], rank[:]).then_inc(rank_ready, 1)
            front.start(dve, front.normed, h_ready)

            def row(g):
                return xa[:, bass.ds(g, 1), 0:D].rearrange("q o d -> q (o d)")

            def result(g, u, i):
                dve.wait_ge(h_psum, done(g))
                dve.wait_ge(h_stored[u], 16 * (i + 1))
                p.alone(dve)
                ps = p.bank[4 + u % 4]
                dve.tensor_copy(hrow[u][:], ps[:, 0:HROW])
                dve.tensor_copy(xa[:, bass.ds(g, 1), C_ADST:C_ADST + HEADS].rearrange("q o d -> q (o d)"),
                                ps[:, HROW:HROW + HEADS]).then_inc(h_ready, 1)

            with dve.Fori(0, U) as i:
                for u in range(U + front.LAG):
                    if u < U:
                        front.norm(dve, row(i * U + u), i * U + u, u)
                    if u >= front.LAG:
                        result(i * U + (u - front.LAG), u - front.LAG, i)

        @block.tensor
        def _(pe):
            pe.wait_ge(p.ready, 1)
            for g in range(CG):
                pe.wait_ge(diag_ready, g + 1)
                pe.matmul(p.bank[g // 4][:, (g % 4) * P:(g % 4 + 1) * P], p.ones[:], diag[:, g % 2, :],
                          start=True, stop=True).then_inc(piv_done, 1)
            pe.wait_ge(start_ready, 1)
            pe.matmul(p.bank[0][:, 0:NT], shift[:, 0, :], start[:, 0:NT], start=True, stop=False)
            pe.matmul(p.bank[0][:, 0:NT], shift[:, 1, :], start[:, 1:NT + 1], start=False, stop=True).then_inc(next_done, 1)
            pe.wait_ge(hot_ready, 1)
            for lo, hi in halves:
                if lo:
                    pe.wait_ge(counts_out, 2 * lo)
                for g in range(lo, hi):
                    rows = hot[:, g * U:(g + 1) * U, :].rearrange("q t b -> q (t b)")
                    pe.matmul(p.bank[2 * (g - lo)][:, 0:U * DBINS], p.earlier[:], rows, start=True, stop=True)
                    pe.matmul(p.bank[2 * (g - lo) + 1][:, 0:U * DBINS], p.onesb[:], rows, start=True, stop=True)\
                      .then_inc(counts_done, 1)
            pe.wait_ge(wa_ready, 1)
            pe.wait_ge(counts_out, 2 * U)
            front.start(pe, front.turned, h_psum)

            def project(g, u):
                pe.wait_ge(front.copied, done(g))
                pe.wait_ge(h_ready, done(g - 3))
                for k in range(KD):
                    ins = pe.matmul(p.bank[4 + u % 4][:, 0:HROW + HEADS], front.xt[u][:, k * P:(k + 1) * P], wa[:, k, :],
                                    start=(k == 0), stop=(k == KD - 1))
                ins.then_inc(h_psum, 1)

            with pe.Fori(0, U) as i:
                for u in range(U):
                    front.turn(pe, i * U + u, u)
                    if u >= 1:
                        project(i * U + (u - 1), u - 1)
                project(i * U + (U - 1), U - 1)

        @block.scalar
        def _(act):
            act.wait_ge(p.ready, 1)
            rows = p.h_table.rearrange("(t q) c -> t q c", q=P)
            for u in range(U):
                act.sem_inc(h_stored[u], 16)

            def store(g, u):
                act.wait_ge(h_ready, done(g))
                act.dma_start(rows[bass.ds(g, 1)].rearrange("o q c -> (o q) c"), hrow[u][:]).then_inc(h_stored[u], 16)

            front.scalar_loop(act, h_psum, store)


def load_windows(p, pool, landed):
    for t in range(NT):
        pool.indirect_dma_start(out=p.win[:, t, :], out_offset=None, in_=p.windows[:],
                                in_offset=bass.IndirectOffsetOnAxis(ap=p.start_i[:, t:t + 1], axis=0)).then_inc(landed, 16)


def in_order(eng, n, item, last=None, s=0):
    item(s)
    if s + 1 < SLOTS:
        with eng.If(n > s + 1):
            in_order(eng, n, item, last, s + 1)
        if last is not None:
            with eng.Else():
                last(s)
    elif last is not None:
        last(s)


def attention(p: Program):
    nc, a = p.nc, p.a
    with p.phase() as ctx:
        def sb(n, s, d):
            return ctx.enter_context(nc.sbuf_tensor(n, s, d))

        most = sb("most", [NT, 2], F32)
        most_i = sb("most_i", [NT, 2], I32)
        row = sb("row", [1, 3, NT], F32)
        key_i = sb("key_i", [P, NT, WIN], I32)
        src_i = sb("src_i", [P, NT + 1, WIN], I32)
        mask = sb("mask", [P, NT, WIN], F32)
        ZEROS = 16
        zeros = sb("zeros", [P, XCH // ZEROS * REC], F32)
        bias = sb("gat_bias", [P, D], F32)
        idx = [sb(f"gat_idx{s}", [P, COLS[s]], I32) for s in range(SLOTS)]
        rows = [sb(f"gat_rows{s}", [P, COLS[s], HROW], F32) for s in range(SLOTS)]
        msg = [sb(f"gat_msg{s}", [P, COLS[s], HROW], F32) for s in range(SLOTS)]
        NS = [c * HEADS for c in COLS]
        score = [sb(f"gat_score{s}", [P, NS[s] + HEADS], F32) for s in range(SLOTS)]
        item_max = sb("item_max", [P, SLOTS, HEADS], F32)
        top = sb("top", [P, SLOTS + 1, HEADS], F32)
        fade = [sb(f"gat_fade{s}", [P, HEADS], F32) for s in range(SLOTS)]
        warm = sb("gat_warm", [P, 1], F32)
        acc = sb("gat_acc", [P, HROW], F32)
        inv = sb("gat_inv", [P, 2, HEADS], F32)
        o = sb("gat_o", [P, D], F32)
        t_pos = sb("t_pos", [P, 3], F32)
        t_at_i = sb("t_at_i", [P, 1], I32)
        t_win = sb("t_win", [P, 2 * WIN], F32)
        t_key = sb("t_key", [P, JCOL], I32)
        t_idx_i = sb("t_idx_i", [P, JCOL], I32)
        t_mask = sb("t_mask", [P, JCOL], F32)

        bias_in, start_ready, wins_in = (p.sem(x) for x in ("gat_bias_in", "gat_start_ready", "gat_wins_in"))
        warmed = p.sem("gat_warmed")
        zeros_ready, zeroed = p.sem("zeros_ready"), p.sem("zeroed")
        turned, most_ready, row_done, tables = (p.sem(x) for x in ("deg_turned", "most_ready", "row_done", "tables"))
        per_slot = lambda name: [p.sem(f"{name}{s}") for s in range(SLOTS)]
        idx_ready, gathered, scores_ready, p_ready, msg_ready, sum_ready, acc_done = (
            per_slot(f"gat_{x}") for x in ("idx_ready", "gathered", "scores", "p_ready", "msg_ready", "sum_ready", "acc_done"))
        step, steps_s, steps_a, steps_t = p.sem("gat_step"), per_slot("gat_steps_s"), per_slot("gat_steps_a"), p.sem("gat_steps_t")
        t_at, t_window, t_idx, t_rows, t_scores, t_p, t_msg, t_sum, t_done, t_steps, t_begin = (
            p.sem(f"gat_t_{x}") for x in ("at", "window", "idx", "rows", "scores", "p", "msg", "sum", "done", "steps", "begin"))
        block = ctx.enter_context(nc.Block())

        def items(eng, t):
            return eng.value_load(p.items[0:1, bass.ds(t, 1)], min_val=1, max_val=-(-N_EDGES // JCOL))

        def tail_base(eng, t):
            return eng.value_load(p.tails[0:1, bass.ds(t, 1)], min_val=0, max_val=N_EDGES)

        @block.sync
        def _(sp):
            flat = a["L0_gnn_bias"]
            sp.dma_start(bias[:], bass.AP(tensor=flat.tensor, offset=0, ap=[[0, P], [1, D]])).then_inc(bias_in, 16)
            sp.wait_ge(bias_in, 16)
            sp.wait_ge(zeros_ready, 1)
            for z in range(ZEROS):
                sp.dma_start(p.x_grouped.rearrange("(z q e) c -> z q (e c)", z=ZEROS, q=P)[z], zeros[:]).then_inc(zeroed, 16)
            sp.wait_ge(zeroed, 16 * ZEROS)

        @block.gpsimd
        def _(pool):
            pool.memset(zeros[:], 0.0).then_inc(zeros_ready, 1)
            pool.wait_ge(start_ready, 1)
            load_windows(p, pool, wins_in)
            pool.wait_ge(tables, 1)
            with pool.Fori(0, NT) as t:
                n = items(pool, t)

                def gather(s):
                    pool.wait_ge(idx_ready[s], t + 1)
                    pool.wait_ge(msg_ready[s], t + 1)
                    p.alone(pool)
                    for j in range(COLS[s]):
                        pool.indirect_dma_start(out=rows[s][:, j, :], out_offset=None, in_=p.h_table[:],
                                                in_offset=bass.IndirectOffsetOnAxis(ap=idx[s][:, j:j + 1], axis=0))\
                            .then_inc(gathered[s], 16)

                in_order(pool, n, gather)
                with pool.If(n > SLOTS):
                    c0 = tail_base(pool, t)
                    with pool.Fori(SLOTS, n) as k:
                        c = c0 + k - SLOTS
                        pool.wait_ge(t_at, c + 1)
                        p.alone(pool)
                        pool.indirect_dma_start(out=t_win[:], out_offset=None, in_=p.windows[:],
                                                in_offset=bass.IndirectOffsetOnAxis(ap=t_at_i[:, 0:1], axis=0)).then_inc(t_window, 16)
                        pool.wait_ge(t_idx, c + 1)
                        p.alone(pool)
                        for j in range(JCOL):
                            pool.indirect_dma_start(out=rows[LAST][:, j, :], out_offset=None, in_=p.h_table[:],
                                                    in_offset=bass.IndirectOffsetOnAxis(ap=t_idx_i[:, j:j + 1], axis=0))\
                                .then_inc(t_rows, 16)
                        pool.wait_ge(t_done, c + 1)
                        p.alone(pool)

        @block.scalar
        def _(act):
            act.wait_ge(tables, 1)
            for s in range(SLOTS):
                act.activation(idx[s][:], src_i[:, 0, AT[s]:AT[s] + COLS[s]], ACT.Copy).then_inc(idx_ready[s], 1)

            def exps(s):
                act.activation(msg[s][:].rearrange("q j c -> q (j c)")[:, HEAD_DIM::HW], score[s][:, 0:NS[s]], ACT.Exp)
                return act.activation(fade[s][:], score[s][:, NS[s]:], ACT.Exp)

            act.sem_inc(warmed, 1)
            with act.Fori(0, NT) as t:
                n = items(act, t)
                act.wait_ge(warmed, t + 1)
                act.activation(warm[:], p.eps[:], ACT.Exp).then_inc(warmed, 1)

                def item(s):
                    act.wait_ge(sum_ready[s], t + 1)
                    act.wait_ge(acc_done[s], t + 1)
                    act.wait_ge(scores_ready[s], t + 1)
                    exps(s).then_inc(p_ready[s], 1)
                    act.wait_ge(gathered[s], 16 * COLS[s] * (t + 1))
                    p.alone(act)
                    act.activation(idx[s][:], src_i[:, bass.ds(t + 1, 1), AT[s]:AT[s] + COLS[s]].rearrange("q o j -> q (o j)"),
                                   ACT.Copy).then_inc(idx_ready[s], 1)

                in_order(act, n, item)
                with act.If(n > SLOTS):
                    c0 = tail_base(act, t)
                    with act.Fori(SLOTS, n) as k:
                        act.wait_ge(t_scores, c0 + k - SLOTS + 1)
                        exps(LAST).then_inc(t_p, 1)

        @block.tensor
        def _(pe):
            pe.transpose(p.bank[0][0:NT, 0:P], p.rec[:, :, C_DEG], p.ident[:]).then_inc(turned, 1)
            pe.wait_ge(most_ready, 1)
            pe.matmul(p.bank[1][0:1, 0:NT], most[:, 1:2], p.ident[0:NT, 0:NT], start=True, stop=True).then_inc(row_done, 1)
            pe.wait_ge(tables, 1)

            for s in range(SLOTS):
                pe.sem_inc(sum_ready[s], 1)

            def total(s):
                for j in range(COLS[s]):
                    ins = pe.matmul(p.bank[s][:, 0:HROW], p.ident[:], msg[s][:, j, :], start=(j == 0), stop=(j == COLS[s] - 1))
                return ins

            with pe.Fori(0, NT) as t:
                n = items(pe, t)

                def item(s):
                    pe.wait_ge(acc_done[s], t + 1)
                    pe.wait_ge(msg_ready[s], t + 2)
                    total(s).then_inc(sum_ready[s], 1)

                in_order(pe, n, item)
                with pe.If(n > SLOTS):
                    c0 = tail_base(pe, t)
                    with pe.Fori(SLOTS, n) as k:
                        pe.wait_ge(t_msg, c0 + k - SLOTS + 1)
                        total(LAST).then_inc(t_sum, 1)

        @block.vector
        def _(dve):
            chain = Chain(p, dve, step)
            chain(dve.tensor_copy(p.id_i[:], p.rec[:, :, C_ID]))
            dve.tensor_copy(p.start_i[:], p.rec[:, :, C_START]).then_inc(start_ready, 1)
            dve.wait_ge(turned, 1)
            chain(dve.tensor_reduce(most[:, 0:1], p.bank[0][0:NT, 0:P], AX, ALU.max))
            chain(dve.tensor_scalar(most_i[:, 0:1], most[:, 0:1], float(JCOL - 1), None, ALU.add))
            chain(dve.tensor_scalar(most_i[:, 1:2], most_i[:, 0:1], JCOL.bit_length() - 1, None, ALU.arith_shift_right))
            dve.tensor_scalar(most[:, 1:2], most_i[:, 1:2], -1.0, 1.0, ALU.add, ALU.max).then_inc(most_ready, 1)
            dve.wait_ge(row_done, 1)
            chain(dve.tensor_copy(row[:, 0, :], p.bank[1][0:1, 0:NT]))
            chain(dve.tensor_copy(p.items[:], row[:, 0, :]))
            chain(dve.tensor_scalar(row[:, 0, :], row[:, 0, :], -float(SLOTS), 0.0, ALU.add, ALU.max))
            chain(dve.memset(row[:, 1, :], 0.0))
            chain(dve.tensor_tensor_scan(row[:, 2, :], row[:, 0, :], row[:, 1, :], 0.0, ALU.add, ALU.add))
            chain(dve.tensor_tensor(row[:, 2, :], row[:, 2, :], row[:, 0, :], ALU.subtract))
            chain(dve.tensor_copy(p.tails[:], row[:, 2, :]))
            chain(dve.tensor_tensor(mask[:], spread(p.count[:, 0:WIN], 1, [P, NT, WIN]),
                                    p.rec[:, :, C_DEG:C_DEG + 1].broadcast_to([P, NT, WIN]), ALU.is_ge))
            chain(dve.tensor_scalar(mask[:], mask[:], NEVER, None, ALU.mult))
            chain(dve.memset(src_i[:, NT, :], 0))
            dve.wait_ge(wins_in, 16 * NT)
            chain(dve.tensor_copy(key_i[:], p.win[:, :, 0:WIN]))
            dve.tensor_scalar(src_i[:, 0:NT, :], key_i[:], RELS.bit_length() - 1, None, ALU.arith_shift_right).then_inc(tables, 1)
            dve.wait_ge(tables, 1)
            dve.wait_ge(bias_in, 16)

            def heads(ap):
                return ap.rearrange("q (h c) -> q h c", h=HEADS)

            def scores(chain, s, t, masked, old, new, biggest, ready):
                sc = score[s][:, 0:NS[s]].rearrange("q (j h) -> q j h", h=HEADS)
                g = rows[s][:].rearrange("q j (h c) -> q j h c", c=HW)
                chain(dve.tensor_tensor(sc, g[:, :, :, HEAD_DIM],
                                        p.rec[:, bass.ds(t, 1), C_ADST:C_ADST + HEADS].broadcast_to([P, COLS[s], HEADS]), ALU.add))
                chain(dve.scalar_tensor_tensor(sc, sc, 0.2, sc, ALU.mult, ALU.max))
                chain(dve.tensor_tensor(sc, sc, masked, ALU.add))
                chain(dve.tensor_reduce(biggest, score[s][:, 0:NS[s]].rearrange("q (j h) -> q h j", h=HEADS), AX, ALU.max))
                chain(dve.tensor_tensor(new, old, biggest, ALU.max))
                dve.tensor_tensor(sc, sc, spread(new, 1, [P, COLS[s], HEADS]), ALU.subtract)
                dve.tensor_tensor(score[s][:, NS[s]:], old, new, ALU.subtract).then_inc(ready, 1)

            def messages(s, ready):
                g = rows[s][:].rearrange("q j (h c) -> q (j h) c", c=HW)
                m = msg[s][:].rearrange("q j (h c) -> q (j h) c", c=HW)
                dve.tensor_tensor(m[:, :, 0:HEAD_DIM], g[:, :, 0:HEAD_DIM],
                                  m[:, :, HEAD_DIM:HW].broadcast_to([P, NS[s], HEAD_DIM]), ALU.mult).then_inc(ready, 1)

            def accumulate(chain, s, finished):
                chain(dve.tensor_tensor(heads(acc[:]), heads(acc[:]), spread(fade[s][:], 2, [P, HEADS, HW]), ALU.mult))
                dve.tensor_tensor(acc[:], acc[:], p.bank[s][:, 0:HROW], ALU.add).then_inc(finished, 1)

            for s in range(SLOTS):
                dve.sem_inc(msg_ready[s], 1)
                dve.sem_inc(acc_done[s], 1)
            chain_s = [Chain(p, dve, x) for x in steps_s]
            chain_a = [Chain(p, dve, x) for x in steps_a]
            chain_t, chain_k = Chain(p, dve, steps_t), Chain(p, dve, t_steps)
            TAIL_STEPS = 11
            with dve.Fori(0, NT) as t:
                n = items(dve, t)
                chain_t.at(t * 6)
                chain_t(dve.memset(top[:, 0, :], LOWEST))

                def front_of(s):
                    chain_s[s].at(t * 5)
                    dve.wait_ge(gathered[s], 16 * COLS[s] * (t + 1))
                    scores(chain_s[s], s, t, mask[:, bass.ds(t, 1), AT[s]:AT[s] + COLS[s]].rearrange("q o j -> q j o")
                           .broadcast_to([P, COLS[s], HEADS]), top[:, s, :], top[:, s + 1, :], item_max[:, s, :], scores_ready[s])
                    assert chain_s[s].n == 5

                def middle_of(s):
                    dve.wait_ge(p_ready[s], t + 1)
                    messages(s, msg_ready[s])

                def back_of(s):
                    chain_a[s].at(t)
                    dve.wait_ge(sum_ready[s], t + 2)
                    if s == 0:
                        p.alone(dve)
                        dve.tensor_copy(acc[:], p.bank[s][:, 0:HROW]).then_inc(acc_done[s], 1)
                    else:
                        accumulate(chain_a[s], s, acc_done[s])
                    dve.wait_ge(acc_done[s], t + 2)
                    p.alone(dve)

                def item(s):
                    front_of(s)
                    if s >= 1:
                        middle_of(s - 1)
                    if s >= 2:
                        back_of(s - 2)

                def last(s):
                    middle_of(s)
                    if s >= 1:
                        back_of(s - 1)
                    back_of(s)

                in_order(dve, n, item, last)
                with dve.If(n > SLOTS):
                    c0 = tail_base(dve, t)
                    dve.tensor_scalar(t_pos[:, 0:1], p.rec[:, bass.ds(t, 1), C_START:C_START + 1].rearrange("q o c -> q (o c)"),
                                      float(WIN), None, ALU.add)
                    dve.tensor_scalar(t_pos[:, 1:2], p.rec[:, bass.ds(t, 1), C_DEG:C_DEG + 1].rearrange("q o c -> q (o c)"),
                                      -float(WIN), None, ALU.add).then_inc(t_begin, 1)
                    dve.wait_ge(t_begin, t + 1)
                    p.alone(dve)
                    with dve.Fori(SLOTS, n) as k:
                        c = c0 + k - SLOTS
                        chain_k.at(c * TAIL_STEPS)
                        dve.tensor_scalar(t_at_i[:], t_pos[:, 0:1], float(N_EDGES), None, ALU.min).then_inc(t_at, 1)
                        dve.wait_ge(t_window, 16 * (c + 1))
                        chain_k(dve.tensor_copy(t_key[:], t_win[:, 0:JCOL]))
                        dve.tensor_scalar(t_idx_i[:], t_key[:], RELS.bit_length() - 1, None, ALU.arith_shift_right).then_inc(t_idx, 1)
                        chain_k(dve.tensor_scalar(t_mask[:], p.count[:, 0:JCOL], t_pos[:, 1:2], NEVER, ALU.is_ge, ALU.mult))
                        dve.wait_ge(t_rows, 16 * JCOL * (c + 1))
                        scores(chain_k, LAST, t, spread(t_mask[:], 2, [P, JCOL, HEADS]), top[:, SLOTS, :], top[:, 0, :],
                               item_max[:, 0, :], t_scores)
                        dve.wait_ge(t_p, c + 1)
                        messages(LAST, t_msg)
                        dve.wait_ge(t_msg, c + 1)
                        p.alone(dve)
                        chain_k(dve.tensor_copy(top[:, SLOTS, :], top[:, 0, :]))
                        dve.wait_ge(t_sum, c + 1)
                        accumulate(chain_k, LAST, t_done)
                        dve.wait_ge(t_done, c + 1)
                        p.alone(dve)
                        chain_k(dve.tensor_scalar(t_pos[:, 0:1], t_pos[:, 0:1], float(JCOL), None, ALU.add))
                        chain_k(dve.tensor_scalar(t_pos[:, 1:2], t_pos[:, 1:2], -float(JCOL), None, ALU.add))
                        assert chain_k.n == TAIL_STEPS, chain_k.n
                chain_t(dve.tensor_scalar(inv[:, 0, :], heads(acc[:])[:, :, HEAD_DIM], 1e-16, None, ALU.add))
                chain_t(dve.reciprocal(inv[:, 1, :], inv[:, 0, :]))
                chain_t(dve.tensor_tensor(heads(o[:]), heads(acc[:])[:, :, 0:HEAD_DIM], spread(inv[:, 1, :], 2, [P, HEADS, HEAD_DIM]), ALU.mult))
                chain_t(dve.tensor_tensor(o[:], o[:], bias[:], ALU.add))
                x = p.rec[:, bass.ds(t, 1), 0:D].rearrange("q o d -> q (o d)")
                chain_t(dve.scalar_tensor_tensor(x, o[:], 0.0, x, ALU.max, ALU.add))
                assert chain_t.n == 6


def tile_row(p, g, lo=0, hi=D):
    return p.rec[:, bass.ds(g, 1), lo:hi].rearrange("q o d -> q (o d)")


def route(p: Program):
    nc, a = p.nc, p.a
    with p.phase() as ctx:
        def sb(n, s, d):
            return ctx.enter_context(nc.sbuf_tensor(n, s, d))

        front = Front(p, ctx, "route")
        rw = sb("rw", [E0, D], F32)
        rwt = sb("rwt", [P, KD, E0], F32)
        rb = sb("rb", [P, E0], F32)
        logits = sb("logits", [P, U, E0], F32)
        best = sb("best", [P, U, 8], F32)
        best_i = sb("best_i", [P, U, 8], U32)
        expert = sb("expert", [P, NT], F32)
        hot = sb("hot0", [P, NT, E0], BF16)
        within = sb("within0", [P, NT, E0], F32)
        total = sb("total0", [P, NT, E0], F32)
        cum = sb("cum0", [P, NT + 1, E0], F32)
        base = sb("base0", [P, 3, E0], F32)
        align = sb("align0", [P, E0], I32)
        place = sb("place", [P, NT], F32)
        begins = sb("begins", [1, XCH], F32)
        past = sb("past", [1, XCH, E0], F32)
        chunk_e = sb("chunk_e", [1, XCH], F32)

        rw_in, rb_in, rw_turned, rwt_ready, logits_done, chosen = (
            p.sem(f"route_{x}") for x in ("rw_in", "rb_in", "rw_turned", "rwt_ready", "logits_done", "chosen"))
        hot_ready, counts_done, counts_out, place_ready, scattered, begins_ready, steps = (
            p.sem(f"route_{x}") for x in ("hot_ready", "counts_done", "counts_out", "place_ready", "scattered", "begins_ready", "steps"))
        block = ctx.enter_context(nc.Block())

        @block.sync
        def _(sp):
            sp.dma_start(rw[:], a["L0_ffn_router_w"]).then_inc(rw_in, 16)
            sp.dma_start(rb[:], bass.AP(tensor=a["L0_ffn_router_b"].tensor, offset=0, ap=[[0, P], [1, E0]])).then_inc(rb_in, 16)

        @block.gpsimd
        def _(pool):
            pool.iota(begins[:], pattern=[[P, XCH]], base=0, channel_multiplier=0,
                      allow_small_or_imprecise_dtypes=True).then_inc(begins_ready, 1)
            pool.wait_ge(place_ready, 1)
            for t in range(NT):
                pool.indirect_dma_start(out=p.x_grouped[:], out_offset=bass.IndirectOffsetOnAxis(ap=p.place_i[:, t:t + 1], axis=0),
                                        in_=p.rec[:, t, :], in_offset=None).then_inc(scattered, 16)
            pool.wait_ge(scattered, 16 * NT)

        @block.scalar
        def _(act):
            front.scalar_loop(act, logits_done)

        @block.tensor
        def _(pe):
            pe.wait_ge(rw_in, 16)
            for k in range(KD):
                ins = pe.transpose(p.bank[7][:, k * E0:(k + 1) * E0], rw[:, k * P:(k + 1) * P], p.ident[0:E0, 0:E0])
            ins.then_inc(rw_turned, 1)
            pe.wait_ge(rwt_ready, 1)
            front.start(pe, front.turned, logits_done)

            def product(g, u):
                pe.wait_ge(front.copied, done(g))
                pe.wait_ge(chosen, done(g - 3))
                for k in range(KD):
                    ins = pe.matmul(p.bank[4 + u % 4][:, 0:E0], front.xt[u][:, k * P:(k + 1) * P], rwt[:, k, :],
                                    start=(k == 0), stop=(k == KD - 1))
                ins.then_inc(logits_done, 1)

            with pe.Fori(0, U) as i:
                for u in range(U):
                    front.turn(pe, i * U + u, u)
                    if u >= 1:
                        product(i * U + (u - 1), u - 1)
                product(i * U + (U - 1), U - 1)
            pe.wait_ge(hot_ready, 1)
            for g in range(U):
                rows = hot[:, g * U:(g + 1) * U, :].rearrange("q t b -> q (t b)")
                pe.matmul(p.bank[g][:, 0:U * E0], p.earlier[:], rows, start=True, stop=True)
                pe.matmul(p.bank[g][:, U * E0:2 * U * E0], p.onesb[:], rows, start=True, stop=True).then_inc(counts_done, 1)

        @block.vector
        def _(dve):
            chain = Chain(p, dve, steps)
            dve.wait_ge(rw_turned, 1)
            dve.tensor_copy(rwt[:].rearrange("q k e -> q (k e)"), p.bank[7][:, 0:KD * E0]).then_inc(rwt_ready, 1)
            dve.wait_ge(rb_in, 16)
            front.moments(dve, chain, lambda t: p.rec[:, t, 0:D])
            chain(dve.tensor_copy(p.rec[:, :, D:D + 4], p.ms[:]))
            before = chain.total()
            front.start(dve, front.normed, chosen)
            K = 3

            def choose(g, u):
                dve.wait_ge(logits_done, done(g))
                chain(dve.tensor_tensor(logits[:, u, :], p.bank[4 + u % 4][:, 0:E0], rb[:], ALU.add), True)
                chain(dve.max(best[:, u, :], logits[:, u, :]), True)
                chain(dve.max_index(best_i[:, u, :], best[:, u, :], logits[:, u, :]), True)
                dve.tensor_copy(expert[:, bass.ds(g, 1)], best_i[:, u, 0:1]).then_inc(chosen, 1)

            with dve.Fori(0, U) as i:
                chain.at(i * (K * U) + before)
                for u in range(U + front.LAG):
                    if u < U:
                        front.norm(dve, tile_row(p, i * U + u), i * U + u, u)
                    if u >= front.LAG:
                        choose(i * U + (u - front.LAG), u - front.LAG)
                assert chain.n == K * U
            chain.at(K * NT + before)
            dve.wait_ge(chosen, done(NT - 1))
            dve.tensor_tensor(hot[:], spread(expert[:], 2, [P, NT, E0]), spread(p.count[:, 0:E0], 1, [P, NT, E0]),
                              ALU.is_equal).then_inc(hot_ready, 1)
            for g in range(U):
                dve.wait_ge(counts_done, g + 1)
                for n, to in enumerate((within, total)):
                    dve.tensor_copy(to[:, g * U:(g + 1) * U, :].rearrange("q t b -> q (t b)"),
                                    p.bank[g][:, n * U * E0:(n + 1) * U * E0]).then_inc(counts_out, 1)
            dve.wait_ge(counts_out, 2 * U)
            rank_steps(dve, chain, hot[:], within[:], total[:], cum, base, within[:], place[:], E0, align[:])
            dve.tensor_copy(p.place_i[:], place[:]).then_inc(place_ready, 1)
            dve.wait_ge(begins_ready, 1)
            chain(dve.tensor_tensor(past[:], spread(base[0:1, 1, :], 1, [1, XCH, E0]), spread(begins[:], 2, [1, XCH, E0]), ALU.is_le))
            chain(dve.tensor_reduce(chunk_e[:], past[:], AX, ALU.add))
            chain(dve.tensor_scalar(p.chunk_e_i[:], chunk_e[:], float(E0 - 1), None, ALU.min))


def experts(p: Program):
    nc, a = p.nc, p.a
    V = 8
    assert XCH % V == 0

    def signalled(g):
        return g + (1 + V)

    with p.phase() as ctx:
        def sb(n, s, d):
            return ctx.enter_context(nc.sbuf_tensor(n, s, d))

        def slots(n, s, d):
            return [sb(f"{n}{v}", s, d) for v in range(V)]

        x, w1, b1 = slots("ex_x", [P, REC], F32), slots("ex_w1_", [P, KD, H0], F32), slots("ex_b1_", [H0, 1], F32)
        w2 = sb("ex_w2", [H0 + 1, E0, D], F32)
        b1_rows, b1_cols = sb("ex_b1_rows", [E0, H0], F32), sb("ex_b1_cols", [H0, E0], F32)
        xn, xt, hid, y = slots("ex_xn", [P, D], F32), slots("ex_xt", [P, D], F32), slots("ex_h", [H0 + 1, P], F32), slots("ex_y", [P, D], F32)
        back = sb("back", [P, NT, D], F32)
        x_in, w_in, y_out = ([p.sem(f"ex_{n}{v}") for v in range(V)] for n in ("x_in", "w_in", "y_out"))
        normed, turned, copied, hid_done, hid_ready, y_done, y_ready = (
            p.sem(f"ex_{n}") for n in ("normed", "turned", "copied", "hid_done", "hid_ready", "y_done", "y_ready"))
        b1_in, w2_in, b1_turned, b1_ready, ones_ready = (
            p.sem(f"ex_{n}") for n in ("b1_in", "w2_in", "b1_turned", "b1_ready", "ones_ready"))
        fetched = [p.sem(f"fetched{g}") for g in range(U)]
        block = ctx.enter_context(nc.Block())

        def expert_of(eng, g):
            return eng.value_load(p.chunk_e_i[0:1, bass.ds(g, 1)], min_val=0, max_val=E0 - 1)

        @block.sync
        def _(sp):
            sp.dma_start(b1_rows[:], a["L0_ffn_b1"]).then_inc(b1_in, 16)
            sp.dma_start(w2[0:H0], a["L0_ffn_W2"].rearrange("e h d -> h e d")).then_inc(w2_in, 16)
            sp.dma_start(w2[H0:H0 + 1], a["L0_ffn_b2"].rearrange("(o e) d -> o e d", o=1)).then_inc(w2_in, 16)
            rows = p.x_grouped.rearrange("(g q) c -> g q c", q=P)
            with sp.Fori(0, XCH // V) as i:
                for v in range(V):
                    g = i * V + v
                    e = expert_of(sp, g)
                    sp.wait_ge(y_done, signalled(g - V))
                    sp.dma_start(x[v][:], rows[bass.ds(g, 1)].rearrange("o q c -> (o q) c")).then_inc(x_in[v], 16)
                    sp.dma_start(w1[v][:], a["L0_ffn_W1"][bass.ds(e, 1)].rearrange("o (k q) h -> q (o k) h", q=P)).then_inc(w_in[v], 16)

        @block.vector
        def _(dve):
            for v in range(V):
                ins = dve.memset(hid[v][H0:H0 + 1, :], 1.0)
            ins.then_inc(ones_ready, 1)
            dve.wait_ge(b1_turned, 1)
            dve.tensor_copy(b1_cols[:], p.bank[7][0:H0, 0:E0]).then_inc(b1_ready, 1)
            dve.wait_ge(b1_ready, 1)
            dve.sem_inc(normed, V)
            with dve.Fori(0, XCH // V) as i:
                for v in range(V):
                    g = i * V + v
                    dve.wait_ge(turned, signalled(g - V))
                    dve.wait_ge(hid_ready, signalled(g - V))
                    p.alone(dve)
                    dve.tensor_copy(b1[v][:], b1_cols[:, bass.ds(expert_of(dve, g), 1)])
                    dve.wait_ge(x_in[v], 16 * (i + 1))
                    dve.tensor_scalar(xn[v][:], x[v][:, 0:D], x[v][:, D:D + 1], x[v][:, D + 3:D + 4],
                                      ALU.subtract, ALU.mult).then_inc(normed, 1)
            for g in range(U):
                dve.wait_ge(fetched[g], 16 * U)
                rows = p.rec[:, g * U:(g + 1) * U, 0:D]
                dve.tensor_tensor(rows, rows, back[:, g * U:(g + 1) * U, :], ALU.add)

        @block.tensor
        def _(pe):
            for s in (turned, hid_done, y_done):
                pe.sem_inc(s, V)
            pe.wait_ge(b1_in, 16)
            pe.transpose(p.bank[7][0:H0, 0:E0], b1_rows[:], p.ident[0:E0, 0:E0]).then_inc(b1_turned, 1)
            pe.wait_ge(w2_in, 32)
            pe.wait_ge(ones_ready, 1)
            pe.wait_ge(b1_ready, 1)

            def turn(g, v):
                pe.wait_ge(normed, signalled(g))
                pe.wait_ge(hid_ready, signalled(g - 4))
                for k in range(KD):
                    ins = pe.transpose(p.bank[v % 4][:, k * P:(k + 1) * P], xn[v][:, k * P:(k + 1) * P], p.ident[:])
                ins.then_inc(turned, 1)

            def hidden(g, v, i):
                pe.wait_ge(w_in[v], 16 * (i + 1))
                pe.wait_ge(copied, signalled(g))
                for k in range(KD):
                    ins = pe.matmul(p.bank[v % 4][0:H0, D:D + P], w1[v][:, k, :], xt[v][:, k * P:(k + 1) * P],
                                    start=(k == 0), stop=(k == KD - 1))
                ins.then_inc(hid_done, 1)

            def output(g, v):
                pe.wait_ge(y_ready, signalled(g - 4))
                pe.wait_ge(hid_ready, signalled(g))
                p.alone(pe)
                pe.matmul(p.bank[4 + v % 4][:, 0:D], hid[v][:], w2[:, bass.ds(expert_of(pe, g), 1), :].rearrange("h o d -> h (o d)"),
                          start=True, stop=True).then_inc(y_done, 1)

            with pe.Fori(0, XCH // V) as i:
                for v in range(V + 2):
                    if v < V:
                        turn(i * V + v, v)
                    if 1 <= v <= V:
                        hidden(i * V + (v - 1), v - 1, i)
                    if v >= 2:
                        output(i * V + (v - 2), v - 2)

        @block.scalar
        def _(act):
            for s in (copied, hid_ready, y_ready):
                act.sem_inc(s, V)

            def to_xt(g, v):
                act.wait_ge(hid_done, signalled(g - V))
                act.wait_ge(turned, signalled(g))
                act.activation(xt[v][:], p.bank[v % 4][:, 0:D], ACT.Copy).then_inc(copied, 1)

            def to_hidden(g, v):
                act.wait_ge(y_done, signalled(g - V))
                act.wait_ge(hid_done, signalled(g))
                act.activation(hid[v][0:H0, :], p.bank[v % 4][0:H0, D:D + P], ACT.Relu, bias=b1[v][:, 0:1]).then_inc(hid_ready, 1)

            def to_y(g, v, i):
                act.wait_ge(y_out[v], 16 * (i + 1))
                act.wait_ge(y_done, signalled(g))
                act.activation(y[v][:], p.bank[4 + v % 4][:, 0:D], ACT.Relu).then_inc(y_ready, 1)

            with act.Fori(0, XCH // V) as i:
                for v in range(V + 2):
                    if v < V:
                        to_xt(i * V + v, v)
                    if 1 <= v <= V:
                        to_hidden(i * V + (v - 1), v - 1)
                    if v >= 2:
                        to_y(i * V + (v - 2), v - 2, i)

        @block.gpsimd
        def _(pool):
            rows = p.y_grouped.rearrange("(g q) c -> g q c", q=P)
            for v in range(V):
                pool.dma_start(y[v][:], a["x"][0:P]).then_inc(y_out[v], 16)
            with pool.Fori(0, XCH // V) as i:
                for v in range(V):
                    g = i * V + v
                    pool.wait_ge(y_ready, signalled(g))
                    p.alone(pool)
                    pool.dma_start(rows[bass.ds(g, 1)].rearrange("o q c -> (o q) c"), y[v][:]).then_inc(y_out[v], 16)
            for v in range(V):
                pool.wait_ge(y_out[v], 16 * (XCH // V + 1))
            for t in range(NT):
                pool.indirect_dma_start(out=back[:, t, :], out_offset=None, in_=p.y_grouped[:],
                                        in_offset=bass.IndirectOffsetOnAxis(ap=p.place_i[:, t:t + 1], axis=0)).then_inc(fetched[t // U], 16)


def transform(p: Program):
    nc, a = p.nc, p.a
    GROUPS, QUARTERS, SLOTS_T = RELS // 2, RELS // 4, 7
    QW = 4 * D
    with p.phase() as ctx:
        def sb(n, s, d):
            return ctx.enter_context(nc.sbuf_tensor(n, s, d))

        front = Front(p, ctx, "rel")
        wr = sb("wr", [P, KD, RELS * D], F32)
        quarter_i = sb("quarter_i", [P, NT, QUARTERS], I32)
        trow = [sb(f"trow{s}", [P, QW], F32) for s in range(SLOTS_T)]
        row_i = [sb(f"trow_i{s}", [P, 1], I32) for s in range(SLOTS_T)]
        w_in, indices, product_done, evac_v, evac_a, steps = (
            p.sem(f"rel_{x}") for x in ("w_in", "indices", "product_done", "evac_v", "evac_a", "steps"))
        scattered = [p.sem(f"rel_scattered{s}") for s in range(SLOTS_T)]
        block = ctx.enter_context(nc.Block())

        @block.sync
        def _(sp):
            for k in range(KD):
                sp.dma_start(wr[:, k, :].rearrange("q (r o) -> q r o", o=D),
                             a["L1_gnn_weight"][:, k * P:(k + 1) * P, :].rearrange("r q o -> q r o")).then_inc(w_in, 16)

        @block.gpsimd
        def _(pool):
            table = p.transformed.rearrange("(n r) d -> n (r d)", r=4)
            for s in range(SLOTS_T):
                pool.dma_start(row_i[s][:], a["src"][0:P].rearrange("(q o) -> q o", o=1)).then_inc(scattered[s], 16)
            with pool.Fori(0, U) as i:
                for w in range(U * QUARTERS):
                    s = w % SLOTS_T
                    pool.wait_ge(evac_v, done(i * (U * QUARTERS) + w))
                    pool.wait_ge(evac_a, done(i * (U * QUARTERS) + w))
                    p.alone(pool)
                    pool.indirect_dma_start(out=table, out_offset=bass.IndirectOffsetOnAxis(ap=row_i[s][:, 0:1], axis=0),
                                            in_=trow[s][:], in_offset=None).then_inc(scattered[s], 16)
            for s in range(SLOTS_T):
                pool.wait_ge(scattered[s], 16 * (NT * QUARTERS // SLOTS_T + 1))

        @block.vector
        def _(dve):
            chain = Chain(p, dve, steps)
            for q in range(QUARTERS):
                ins = dve.tensor_scalar(quarter_i[:, :, q], p.rec[:, :, C_ID], float(QUARTERS), float(q), ALU.mult, ALU.add)
            ins.then_inc(indices, 1)
            front.moments(dve, chain, lambda t: p.rec[:, t, 0:D])
            front.start(dve, front.normed, evac_v)

            def results(i, u):
                for q in range(QUARTERS):
                    w = u * QUARTERS + q
                    dve.wait_ge(product_done, done((i * U + u) * GROUPS + 2 * q))
                    dve.wait_ge(scattered[w % SLOTS_T], 16 * (4 * i + (w // SLOTS_T + 1)))
                    p.alone(dve)
                    dve.tensor_copy(trow[w % SLOTS_T][:, 0:QW // 2], p.bank[4 + (2 * q) % 4][:]).then_inc(evac_v, 1)

            with dve.Fori(0, U) as i:
                for u in range(U + front.LAG):
                    if u < U:
                        front.norm(dve, tile_row(p, i * U + u), i * U + u, u)
                    if u >= front.LAG:
                        results(i, u - front.LAG)

        @block.scalar
        def _(act):
            act.wait_ge(indices, 1)
            front.root(act)
            front.start(act, front.copied, evac_a)

            def results(i, u):
                for q in range(QUARTERS):
                    w = u * QUARTERS + q
                    act.wait_ge(product_done, done((i * U + u) * GROUPS + 2 * q + 1))
                    act.wait_ge(scattered[w % SLOTS_T], 16 * (4 * i + (w // SLOTS_T + 1)))
                    p.alone(act)
                    act.activation(trow[w % SLOTS_T][:, QW // 2:], p.bank[4 + (2 * q + 1) % 4][:], ACT.Copy)
                    act.activation(row_i[w % SLOTS_T][:], quarter_i[:, bass.ds(i * U + u, 1), q:q + 1].rearrange("q o c -> q (o c)"),
                                   ACT.Copy).then_inc(evac_a, 1)

            with act.Fori(0, U) as i:
                for u in range(U + 1):
                    if u < U:
                        front.copy(act, i * U + u, u, None)
                    if u >= 1:
                        results(i, u - 1)

        @block.tensor
        def _(pe):
            pe.wait_ge(w_in, 16 * KD)
            front.start(pe, front.turned, product_done)

            def products(g, u):
                pe.wait_ge(front.copied, done(g))
                for m in range(GROUPS):
                    pe.wait_ge(evac_a if m % 2 else evac_v, done(g * QUARTERS + m // 2 - 2))
                    for k in range(KD):
                        ins = pe.matmul(p.bank[4 + m % 4][:], front.xt[u][:, k * P:(k + 1) * P],
                                        wr[:, k, m * 2 * D:(m + 1) * 2 * D], start=(k == 0), stop=(k == KD - 1))
                    ins.then_inc(product_done, 1)

            with pe.Fori(0, U) as i:
                for u in range(U):
                    front.turn(pe, i * U + u, u)
                    if u >= 1:
                        products(i * U + (u - 1), u - 1)
                products(i * U + (U - 1), U - 1)


def relations(p: Program):
    nc, a = p.nc, p.a
    with p.phase() as ctx:
        def sb(n, s, d):
            return ctx.enter_context(nc.sbuf_tensor(n, s, d))

        key_i = sb("rel_key_i", [P, NT + 1, WIN], I32)
        weight = sb("rel_weight", [P, NT, WIN], F32)
        idx = [sb(f"rel_idx{s}", [P, COLS[s]], I32) for s in range(SLOTS)]
        rows = [sb(f"rel_rows{s}", [P, COLS[s], D], F32) for s in range(SLOTS)]
        t_pos = sb("rt_pos", [P, 3], F32)
        t_at_i = sb("rt_at_i", [P, 1], I32)
        t_win = sb("rt_win", [P, 2 * WIN], F32)
        t_idx_i = sb("rt_idx_i", [P, JCOL], I32)
        t_w = sb("rt_w", [P, JCOL], F32)
        tables, step = p.sem("rel_tables"), p.sem("rel_step")
        per_slot = lambda name: [p.sem(f"rel_{name}{s}") for s in range(SLOTS)]
        idx_ready, gathered, used, steps_s = (per_slot(x) for x in ("idx_ready", "gathered", "used", "steps_s"))
        t_at, t_window, t_idx, t_rows, t_done, t_steps, t_begin = (
            p.sem(f"rel_t_{x}") for x in ("at", "window", "idx", "rows", "done", "steps", "begin"))
        block = ctx.enter_context(nc.Block())

        def items(eng, t):
            return eng.value_load(p.items[0:1, bass.ds(t, 1)], min_val=1, max_val=-(-N_EDGES // JCOL))

        def tail_base(eng, t):
            return eng.value_load(p.tails[0:1, bass.ds(t, 1)], min_val=0, max_val=N_EDGES)

        @block.gpsimd
        def _(pool):
            pool.wait_ge(tables, 1)
            with pool.Fori(0, NT) as t:
                n = items(pool, t)

                def gather(s):
                    pool.wait_ge(idx_ready[s], t + 1)
                    pool.wait_ge(used[s], t + 1)
                    p.alone(pool)
                    for j in range(COLS[s]):
                        pool.indirect_dma_start(out=rows[s][:, j, :], out_offset=None, in_=p.transformed[:],
                                                in_offset=bass.IndirectOffsetOnAxis(ap=idx[s][:, j:j + 1], axis=0))\
                            .then_inc(gathered[s], 16)

                in_order(pool, n, gather)
                with pool.If(n > SLOTS):
                    c0 = tail_base(pool, t)
                    with pool.Fori(SLOTS, n) as k:
                        c = c0 + k - SLOTS
                        pool.wait_ge(t_at, c + 1)
                        p.alone(pool)
                        pool.indirect_dma_start(out=t_win[:], out_offset=None, in_=p.windows[:],
                                                in_offset=bass.IndirectOffsetOnAxis(ap=t_at_i[:, 0:1], axis=0)).then_inc(t_window, 16)
                        pool.wait_ge(t_idx, c + 1)
                        p.alone(pool)
                        for j in range(JCOL):
                            pool.indirect_dma_start(out=rows[LAST][:, j, :], out_offset=None, in_=p.transformed[:],
                                                    in_offset=bass.IndirectOffsetOnAxis(ap=t_idx_i[:, j:j + 1], axis=0))\
                                .then_inc(t_rows, 16)
                        pool.wait_ge(t_done, c + 1)
                        p.alone(pool)

        @block.scalar
        def _(act):
            act.wait_ge(tables, 1)
            for s in range(SLOTS):
                act.activation(idx[s][:], key_i[:, 0, AT[s]:AT[s] + COLS[s]], ACT.Copy).then_inc(idx_ready[s], 1)
            with act.Fori(0, NT) as t:
                n = items(act, t)

                def item(s):
                    act.wait_ge(gathered[s], 16 * COLS[s] * (t + 1))
                    p.alone(act)
                    act.activation(idx[s][:], key_i[:, bass.ds(t + 1, 1), AT[s]:AT[s] + COLS[s]].rearrange("q o j -> q (o j)"),
                                   ACT.Copy).then_inc(idx_ready[s], 1)

                in_order(act, n, item)

        @block.vector
        def _(dve):
            chain = Chain(p, dve, step)
            chain(dve.tensor_copy(key_i[:, 0:NT, :], p.win[:, :, 0:WIN]))
            chain(dve.memset(key_i[:, NT, :], 0))
            chain(dve.tensor_tensor(weight[:], spread(p.count[:, 0:WIN], 1, [P, NT, WIN]),
                                    p.rec[:, :, C_DEG:C_DEG + 1].broadcast_to([P, NT, WIN]), ALU.is_lt))
            dve.tensor_tensor(weight[:], weight[:], p.win[:, :, WIN:2 * WIN], ALU.mult).then_inc(tables, 1)
            dve.wait_ge(tables, 1)
            for s in range(SLOTS):
                dve.sem_inc(used[s], 1)
            chain_s = [Chain(p, dve, x) for x in steps_s]
            chain_k = Chain(p, dve, t_steps)
            TAIL_STEPS = 7

            def add(t, s, w, chain, finished):
                x = p.rec[:, bass.ds(t, 1), 0:D].rearrange("q o d -> q (o d)")
                for j in range(COLS[s]):
                    ins = dve.scalar_tensor_tensor(x, rows[s][:, j, :], w(j), x, ALU.mult, ALU.add)
                    if j < COLS[s] - 1:
                        chain(ins)
                    else:
                        ins.then_inc(finished, 1)

            with dve.Fori(0, NT) as t:
                n = items(dve, t)

                def item(s):
                    chain_s[s].at(t * (COLS[s] - 1))
                    dve.wait_ge(gathered[s], 16 * COLS[s] * (t + 1))
                    add(t, s, lambda j: weight[:, bass.ds(t, 1), AT[s] + j:AT[s] + j + 1].rearrange("q o c -> q (o c)"),
                        chain_s[s], used[s])
                    dve.wait_ge(used[s], t + 2)
                    p.alone(dve)

                in_order(dve, n, item)
                with dve.If(n > SLOTS):
                    c0 = tail_base(dve, t)
                    dve.tensor_scalar(t_pos[:, 0:1], tile_row(p, t, C_START, C_START + 1), float(WIN), None, ALU.add)
                    dve.tensor_scalar(t_pos[:, 1:2], tile_row(p, t, C_DEG, C_DEG + 1), -float(WIN), None, ALU.add).then_inc(t_begin, 1)
                    dve.wait_ge(t_begin, t + 1)
                    p.alone(dve)
                    with dve.Fori(SLOTS, n) as k:
                        c = c0 + k - SLOTS
                        chain_k.at(c * TAIL_STEPS)
                        dve.tensor_scalar(t_at_i[:], t_pos[:, 0:1], float(N_EDGES), None, ALU.min).then_inc(t_at, 1)
                        dve.wait_ge(t_window, 16 * (c + 1))
                        p.alone(dve)
                        dve.tensor_copy(t_idx_i[:], t_win[:, 0:JCOL]).then_inc(t_idx, 1)
                        chain_k(dve.tensor_scalar(t_w[:], p.count[:, 0:JCOL], t_pos[:, 1:2], None, ALU.is_lt))
                        chain_k(dve.tensor_tensor(t_w[:], t_w[:], t_win[:, WIN:WIN + JCOL], ALU.mult))
                        dve.wait_ge(t_rows, 16 * JCOL * (c + 1))
                        add(t, LAST, lambda j: t_w[:, j:j + 1], chain_k, t_done)
                        dve.wait_ge(t_done, c + 1)
                        p.alone(dve)
                        chain_k(dve.tensor_scalar(t_pos[:, 0:1], t_pos[:, 0:1], float(JCOL), None, ALU.add))
                        chain_k(dve.tensor_scalar(t_pos[:, 1:2], t_pos[:, 1:2], -float(JCOL), None, ALU.add))
                        assert chain_k.n == TAIL_STEPS, chain_k.n


def choose_two(p: Program):
    nc, a = p.nc, p.a
    with p.phase() as ctx:
        def sb(n, s, d):
            return ctx.enter_context(nc.sbuf_tensor(n, s, d))

        front = Front(p, ctx, "two")
        real = sb("real", [P, NT], F32)
        sums = sb("col_sums", [P, KD], F32)
        wr = sb("wr1", [P, KD, E1], F32)
        br = sb("br1", [1, E1], F32)
        row = sb("row1", [1, 10, E1], F32)
        one = sb("one1", [1, 12], F32)
        real_ready, w_in, taken, mean_ready, logits_done, steps, exp_ready, exp_done, pair_ready, spread_done = (
            p.sem(f"two_{x}") for x in ("real_ready", "w_in", "taken", "mean_ready", "logits_done", "steps",
                                        "exp_ready", "exp_done", "pair_ready", "spread_done"))
        block = ctx.enter_context(nc.Block())
        logit, e, rw, s, eq, rev, s2, q = (row[:, n, :] for n in range(8))
        pair = one[:, 10:12]

        @block.sync
        def _(sp):
            sp.dma_start(wr[:], a["L1_ffn_Wr"].rearrange("(k q) e -> q k e", q=P)).then_inc(w_in, 16)
            sp.dma_start(br[:], a["L1_ffn_br"].rearrange("(o e) -> o e", o=1)).then_inc(w_in, 16)

        @block.tensor
        def _(pe):
            pe.wait_ge(real_ready, 1)
            front.start(pe, front.turned)

            with pe.Fori(0, U) as i:
                pe.wait_ge(taken, i + 1)
                p.alone(pe)
                for u in range(U):
                    g = i * U + u
                    pe.wait_ge(front.normed, done(g))
                    p.alone(pe)
                    for k in range(KD):
                        ins = pe.matmul(p.bank[k][:, 0:1], front.xn[u][:, k * P:(k + 1) * P], real[:, bass.ds(g, 1)],
                                        start=(u == 0), stop=(u == U - 1))
                    ins.then_inc(front.turned, 1)
            pe.wait_ge(w_in, 32)
            pe.wait_ge(mean_ready, 1)
            for k in range(KD):
                ins = pe.matmul(p.bank[2][0:1, 0:E1], sums[:, k:k + 1], wr[:, k, :], start=(k == 0), stop=(k == KD - 1))
            ins.then_inc(logits_done, 1)
            pe.wait_ge(pair_ready, 1)
            pe.matmul(p.bank[3][:, 0:2], p.ones[0:1, :], pair, start=True, stop=True).then_inc(spread_done, 1)

        @block.scalar
        def _(act):
            front.root(act)
            for n, (out, in_) in enumerate(((e, logit), (s, q), (one[:, 6:7], one[:, 5:6]))):
                act.wait_ge(exp_ready, n + 1)
                act.activation(out, in_, ACT.Exp).then_inc(exp_done, 1)

        @block.vector
        def _(dve):
            chain = Chain(p, dve, steps)
            dve.memset(sums[:], 0.0)
            dve.tensor_scalar(real[:], p.rec[:, :, C_ID], float(N_NODES), None, ALU.is_lt).then_inc(real_ready, 1)
            dve.wait_ge(real_ready, 1)
            front.moments(dve, chain, lambda t: p.rec[:, t, 0:D])
            front.start(dve, front.normed)
            dve.sem_inc(taken, 1)
            before = chain.total()
            with dve.Fori(0, U) as i:
                chain.at(i * KD + before)
                for u in range(U):
                    front.norm(dve, tile_row(p, i * U + u), i * U + u, u)
                dve.wait_ge(front.turned, done(i * U + (U - 1)))
                p.alone(dve)
                for k in range(KD):
                    chain(dve.tensor_tensor(sums[:, k:k + 1], sums[:, k:k + 1], p.bank[k][:, 0:1], ALU.add))
                dve.sem_inc(taken, 1)
                assert chain.n == KD
            chain.at(KD * U + before)
            dve.tensor_scalar(sums[:], sums[:], 1.0 / N_NODES, None, ALU.mult).then_inc(mean_ready, 1)
            dve.wait_ge(w_in, 32)
            dve.wait_ge(logits_done, 1)

            def softmax(n, x, out):
                chain(dve.tensor_reduce(one[:, 0:1], x, AX, ALU.max))
                dve.tensor_scalar(x, x, one[:, 0:1], None, ALU.subtract).then_inc(exp_ready, 1)
                dve.wait_ge(exp_done, n)
                chain(dve.tensor_reduce(one[:, 1:2], out, AX, ALU.add))
                chain(dve.reciprocal(one[:, 2:3], one[:, 1:2]))

            chain(dve.tensor_tensor(logit, p.bank[2][0:1, 0:E1], br[:], ALU.add))
            softmax(1, logit, e)
            chain(dve.tensor_scalar(rw, e, one[:, 2:3], None, ALU.mult))
            chain(dve.tensor_scalar(q, rw, CAPACITY / N_NODES, None, ALU.min))
            softmax(2, q, s)
            chain(dve.tensor_scalar(s, s, one[:, 2:3], None, ALU.mult))
            chain(dve.tensor_scalar(rev, p.count[0:1, 0:E1], -1.0, float(E1), ALU.mult, ALU.add))

            def largest(x, value, at):
                chain(dve.tensor_reduce(value, x, AX, ALU.max))
                chain(dve.tensor_scalar(eq, x, value, None, ALU.is_ge))
                chain(dve.tensor_tensor(eq, eq, rev, ALU.mult))
                chain(dve.tensor_reduce(at, eq, AX, ALU.max))

            largest(s, one[:, 3:4], one[:, 8:9])
            chain(dve.tensor_scalar(s2, rev, one[:, 8:9], -2.0, ALU.is_equal, ALU.mult))
            chain(dve.tensor_tensor(s2, s2, s, ALU.add))
            largest(s2, one[:, 4:5], one[:, 9:10])
            chain(dve.tensor_scalar(one[:, 8:10], one[:, 8:10], -1.0, float(E1), ALU.mult, ALU.add))
            chain(dve.tensor_copy(p.two_i[:], one[:, 8:10]))
            dve.tensor_tensor(one[:, 5:6], one[:, 4:5], one[:, 3:4], ALU.subtract).then_inc(exp_ready, 1)
            dve.wait_ge(exp_done, 3)
            chain(dve.tensor_scalar(one[:, 7:8], one[:, 6:7], 1.0, None, ALU.add))
            chain(dve.reciprocal(pair[:, 0:1], one[:, 7:8]))
            dve.tensor_tensor(pair[:, 1:2], pair[:, 0:1], one[:, 6:7], ALU.mult).then_inc(pair_ready, 1)
            dve.wait_ge(spread_done, 1)
            chain(dve.tensor_copy(p.two_w[:], p.bank[3][:, 0:2]))


def feed_forward(p: Program):
    nc, a = p.nc, p.a
    G, PAIRS = 4, NT // 8
    assert PAIRS * 2 * G + 1 == NT
    F = H1 // P
    EF = 2 * F
    with p.phase() as ctx:
        def sb(n, s, d):
            return ctx.enter_context(nc.sbuf_tensor(n, s, d))

        w1 = sb("ff_w1", [P, 2, KD, H1], F32)
        w2 = sb("ff_w2", [P, EF, D], F32)
        b1_rows = sb("ff_b1_rows", [EF, P], F32)
        b1 = sb("ff_b1", [P, EF], F32)
        b2 = sb("ff_b2", [P, 2, D], F32)
        gb = sb("ff_gb", [P, 2, D], F32)
        xg = [sb(f"ff_xg{s}", [P, G, D], F32) for s in range(2)]
        xt = [sb(f"ff_xt{s}", [P, KD, G * P], F32) for s in range(2)]
        gt = [sb(f"ff_gt{s}", [P, EF, G * P], F32) for s in range(2)]
        y = [sb(f"ff_y{j}", [P, D], F32) for j in range(G)]
        z = [sb(f"ff_z{j}", [P, D], F32) for j in range(G)]
        stats = sb("ff_stats", [P, G, 6], F32)
        ms = sb("ff_ms", [P, G, 4], F32)
        at = [sb(f"ff_at{j}", [P, 1], I32) for j in range(G)]
        w_in, scaled, normed, turned, copied, hidden, gelued, out_done, taken, varied, rooted, finished, steps, setup = (
            p.sem(f"ff_{x}") for x in ("w_in", "scaled", "normed", "turned", "copied", "hidden", "gelued",
                                       "out_done", "taken", "varied", "rooted", "finished", "steps", "setup"))
        b1_turned, b1_ready = p.sem("ff_b1_turned"), p.sem("ff_b1_ready")
        stored = [p.sem(f"ff_stored{j}") for j in range(G)]
        block = ctx.enter_context(nc.Block())

        END = 2 * PAIRS

        @block.sync
        def _(sp):
            for n in range(2):
                e = sp.value_load(p.two_i[0:1, n:n + 1], min_val=0, max_val=E1 - 1)
                sp.dma_start(w1[:, n], a["L1_ffn_W1"][bass.ds(e, 1)].rearrange("o (k q) f -> q (o k) f", q=P)).then_inc(w_in, 16)
                sp.dma_start(w2[:, n * F:(n + 1) * F], a["L1_ffn_W2"][bass.ds(e, 1)].rearrange("o (f q) d -> q (o f) d", q=P)).then_inc(w_in, 16)
                sp.dma_start(b1_rows[n * F:(n + 1) * F, :], a["L1_ffn_b1"][bass.ds(e, 1)].rearrange("o (f q) -> (o f) q", q=P)).then_inc(w_in, 16)
                sp.dma_start(b2[:, n], a["L1_ffn_b2"][bass.ds(e, 1)].broadcast_to([P, D])).then_inc(w_in, 16)
            for n, name in enumerate(("L1_ffn_gamma", "L1_ffn_beta")):
                sp.dma_start(gb[:, n], bass.AP(tensor=a[name].tensor, offset=0, ap=[[0, P], [1, D]])).then_inc(w_in, 16)

        @block.tensor
        def _(pe):
            for s in (turned, hidden, out_done):
                pe.sem_inc(s, U)
            pe.wait_ge(w_in, 16 * 10)
            pe.transpose(p.bank[6][:, 0:EF], b1_rows[:], p.ident[0:EF, 0:EF]).then_inc(b1_turned, 1)

            def into(g, slot, tiles):
                pe.wait_ge(normed, done(g))
                for j in range(tiles):
                    c = g * G + j
                    pe.wait_ge(copied, done(c - 2))
                    for k in range(KD):
                        ins = pe.transpose(p.bank[j % 2][:, k * P:(k + 1) * P], xg[slot][:, j, k * P:(k + 1) * P], p.ident[:])
                    ins.then_inc(turned, 1)
                pe.wait_ge(copied, done(g * G + (tiles - 1)))
                for ef in range(EF):
                    pe.wait_ge(gelued, done(g * EF + ef - 4))
                    for k in range(KD):
                        ins = pe.matmul(p.bank[2 + ef % 4][:, 0:tiles * P], w1[:, ef // F, k, (ef % F) * P:(ef % F + 1) * P],
                                        xt[slot][:, k, 0:tiles * P], start=(k == 0), stop=(k == KD - 1))
                    ins.then_inc(hidden, 1)

            def outof(g, slot, tiles):
                pe.wait_ge(gelued, done(g * EF + (EF - 1)))
                for j in range(tiles):
                    pe.wait_ge(taken, done(g * G + j - 2))
                    for ef in range(EF):
                        ins = pe.matmul(p.bank[6 + j % 2][:, 0:D], gt[slot][:, ef, j * P:(j + 1) * P], w2[:, ef, :],
                                        start=(ef == 0), stop=(ef == EF - 1))
                    ins.then_inc(out_done, 1)

            pe.wait_ge(scaled, EF)
            pe.wait_ge(b1_ready, 1)
            with pe.Fori(0, PAIRS) as i:
                into(i * 2, 0, G)
                into(i * 2 + 1, 1, G)
                outof(i * 2, 0, G)
                outof(i * 2 + 1, 1, G)
            into(END, 0, 1)
            outof(END, 0, 1)

        @block.scalar
        def _(act):
            for s in (copied, gelued, rooted):
                act.sem_inc(s, U)
            act.wait_ge(b1_ready, 1)

            def group(g, slot, tiles):
                for j in range(tiles):
                    act.wait_ge(turned, done(g * G + j))
                    act.activation(xt[slot][:, :, j * P:(j + 1) * P], p.bank[j % 2][:, 0:D].rearrange("q (k c) -> q k c", c=P),
                                   ACT.Copy).then_inc(copied, 1)
                act.wait_ge(out_done, done(g * G - 2 * G + (G - 1)))
                p.alone(act)
                for ef in range(EF):
                    act.wait_ge(hidden, done(g * EF + ef))
                    act.activation(gt[slot][:, ef, 0:tiles * P], p.bank[2 + ef % 4][:, 0:tiles * P], ACT.Gelu,
                                   bias=b1[:, ef:ef + 1]).then_inc(gelued, 1)

            def roots(g, tiles):
                act.wait_ge(varied, done(g))
                act.activation(ms[:, 0:tiles, 2], ms[:, 0:tiles, 1], ACT.Sqrt, bias=p.eps[:, 0:1]).then_inc(rooted, 1)

            with act.Fori(0, PAIRS) as i:
                group(i * 2, 0, G)
                group(i * 2 + 1, 1, G)
                roots(i * 2, G)
                roots(i * 2 + 1, G)
            group(END, 0, 1)
            roots(END, 1)

        @block.gpsimd
        def _(pool):
            def group(g, tiles):
                for j in range(tiles):
                    pool.wait_ge(finished, done(g * G + j))
                    p.alone(pool)
                    pool.indirect_dma_start(out=p.a["out"], out_offset=bass.IndirectOffsetOnAxis(ap=at[j][:, 0:1], axis=0),
                                            in_=z[j][:], in_offset=None).then_inc(stored[j], 16)

            for j in range(G):
                pool.dma_start(at[j][:], a["src"][0:P].rearrange("(q o) -> q o", o=1)).then_inc(stored[j], 16)
            with pool.Fori(0, PAIRS) as i:
                group(i * 2, G)
                group(i * 2 + 1, G)
            group(END, 1)
            for j in range(G):
                pool.wait_ge(stored[j], 16 * (1 + 2 * PAIRS + (j == 0)))

        @block.vector
        def _(dve):
            chain, first = Chain(p, dve, steps), Chain(p, dve, setup)
            for s in (normed, taken, varied, finished):
                dve.sem_inc(s, U)
            dve.wait_ge(w_in, 16 * 10)
            dve.wait_ge(b1_turned, 1)
            dve.tensor_copy(b1[:], p.bank[6][:, 0:EF]).then_inc(b1_ready, 1)
            for ef in range(EF):
                dve.tensor_scalar(w2[:, ef, :], w2[:, ef, :], p.two_w[:, ef // F:ef // F + 1], None, ALU.mult).then_inc(scaled, 1)
            first(dve.tensor_scalar(b2[:, 0, :], b2[:, 0, :], p.two_w[:, 0:1], None, ALU.mult))
            first(dve.scalar_tensor_tensor(b2[:, 0, :], b2[:, 1, :], p.two_w[:, 1:2], b2[:, 0, :], ALU.mult, ALU.add))

            def moment(c, n):
                return p.ms[:, bass.ds(c, 1), n:n + 1].rearrange("q o c -> q (o c)")

            def norm(g, slot, tiles):
                dve.wait_ge(turned, done(g * G - 2 * G + (G - 1)))
                dve.wait_ge(finished, done(g * G - 2 * G + (G - 1)))
                p.alone(dve)
                for j in range(tiles):
                    c = g * G + j
                    ins = dve.tensor_scalar(xg[slot][:, j, :], tile_row(p, c), moment(c, 0), moment(c, 3),
                                            ALU.subtract, ALU.mult)
                ins.then_inc(normed, 1)
                dve.wait_ge(normed, done(g))

            def final(g, slot, tiles, before):
                chain.at(before)
                dve.wait_ge(finished, done(g * G - 1))
                for j in range(tiles):
                    dve.wait_ge(out_done, done(g * G + j))
                    p.alone(dve)
                    dve.tensor_tensor(y[j][:], p.bank[6 + j % 2][:, 0:D], xg[slot][:, j, :], ALU.add).then_inc(taken, 1)
                    dve.wait_ge(taken, done(g * G + j))
                    p.alone(dve)
                    chain(dve.tensor_tensor(y[j][:], y[j][:], b2[:, 0, :], ALU.add), True)
                    chain(dve.bn_stats(stats[:, j, :], y[j][:]), True)
                    ins = dve.bn_aggr(ms[:, j, 0:2], stats[:, j, :])
                ins.then_inc(varied, 1)
                for j in range(tiles):
                    dve.wait_ge(stored[j], 16 * (g + 1))
                    p.alone(dve)
                    dve.tensor_copy(at[j][:], p.id_i[:, bass.ds(g * G + j, 1)])
                dve.wait_ge(rooted, done(g))
                chain(dve.reciprocal(ms[:, 0:tiles, 3], ms[:, 0:tiles, 2]), True)
                for op in range(3):
                    for j in range(tiles):
                        ins = (lambda: dve.tensor_scalar(y[j][:], y[j][:], ms[:, j, 0:1], ms[:, j, 3:4], ALU.subtract, ALU.mult),
                               lambda: dve.tensor_tensor(y[j][:], y[j][:], gb[:, 0, :], ALU.mult),
                               lambda: dve.tensor_tensor(y[j][:], y[j][:], gb[:, 1, :], ALU.add))[op]()
                    chain(ins, True)
                for j in range(tiles):
                    dve.tensor_tensor(z[j][:], y[j][:], tile_row(p, g * G + j), ALU.add).then_inc(finished, 1)
                return chain.n

            K = 2 * G + 4
            with dve.Fori(0, PAIRS) as i:
                norm(i * 2, 0, G)
                norm(i * 2 + 1, 1, G)
                assert final(i * 2, 0, G, i * (2 * K)) == K
                assert final(i * 2 + 1, 1, G, i * (2 * K) + K) == K
            norm(END, 0, 1)
            final(END, 0, 1, PAIRS * 2 * K)


def build(nc, a):
    with ExitStack() as ctx:
        p = Program(nc, ctx, a)
        search_and_project(p)
        attention(p)
        route(p)
        experts(p)
        transform(p)
        relations(p)
        choose_two(p)
        feed_forward(p)



_INS = ["x", "src", "dst", "edge_type_16", "edge_weight1", "L0_gnn_W", "L0_gnn_att_src", "L0_gnn_att_dst", "L0_gnn_bias",
        "L0_ffn_router_w", "L0_ffn_router_b", "L0_ffn_W1", "L0_ffn_b1", "L0_ffn_W2", "L0_ffn_b2", "L1_gnn_weight",
        "L1_ffn_Wr", "L1_ffn_br", "L1_ffn_W1", "L1_ffn_b1", "L1_ffn_W2", "L1_ffn_b2", "L1_ffn_gamma", "L1_ffn_beta"]


def layout(inputs):
    import numpy as np
    arrays = {n: np.ascontiguousarray(inputs[n]) for n in _INS}
    arrays["x"] = np.pad(arrays["x"], ((0, NP - N_NODES), (0, 0)))
    arrays["dst"] = np.pad(arrays["dst"], (0, CG * P * P - N_EDGES), constant_values=2 * NP)
    for n in ("src", "edge_type_16"):
        arrays[n] = np.pad(arrays[n], (0, EP + WIN - N_EDGES))
    arrays["edge_weight1"] = np.pad(arrays["edge_weight1"].reshape(-1), (0, EP + WIN - N_EDGES))
    return arrays


def kernel(**inputs):
    import numpy as np
    import concourse.bacc as bacc
    from concourse.bass_utils import run_bass_kernel_spmd

    arrays = layout(inputs)
    nc = bacc.Bacc("TRN2", target_bir_lowering=False, num_devices=1)
    aps = {n: nc.dram_tensor(n, v.shape, mybir.dt.from_np(v.dtype), kind="ExternalInput").ap() for n, v in arrays.items()}
    aps["out"] = nc.dram_tensor("out", (NP, D), F32, kind="ExternalOutput").ap()
    build(nc, aps)
    r = run_bass_kernel_spmd(nc, [arrays], core_ids=[0])
    return r.results[0]["out"][:N_NODES]
```

```python
from contextlib import ExitStack, contextmanager

import concourse.bass as bass
import concourse.mybir as mybir

F32 = mybir.dt.float32
BF16 = mybir.dt.bfloat16
I32 = mybir.dt.int32
U32 = mybir.dt.uint32
ALU = mybir.AluOpType
ACT = mybir.ActivationFunctionType
AX = mybir.AxisListType.X

P = 128
N_NODES, N_EDGES, D = 6250, 100000, 256
NT = -(-N_NODES // P)
NP = NT * P
HEADS, HEAD_DIM = 8, 32
HW = HEAD_DIM + 1
HROW = HEADS * HW
RELS = 16
KD = D // P
EPS = 1e-5
C_ADST, C_START, C_DEG, C_ID, REC = D, D + HEADS, D + HEADS + 1, D + HEADS + 2, D + HEADS + 4
CHUNKS = -(-N_EDGES // P)
CG = -(-CHUNKS // P)
STRIP = CHUNKS
EP = P * STRIP
WIN = 32
SLICE = 23
SLICES = STRIP // SLICE
JCOL = 4
COLS = [2 * JCOL] + [JCOL] * (WIN // JCOL - 2)
SLOTS = len(COLS)
AT = [sum(COLS[:s]) for s in range(SLOTS)]
COLS1 = [8] + [2] * (WIN // 2 - 4)
SLOTS1 = len(COLS1)
AT1 = [sum(COLS1[:s]) for s in range(SLOTS1)]
LAST = SLOTS - 1
assert sum(COLS) == sum(COLS1) == WIN and COLS[LAST] == JCOL
DBINS = 64
E0, H0 = 32, 64
XCH = NT + E0 - 1
E1, H1 = 8, 512
CAPACITY = float(-(-N_NODES * 5 // (4 * E1)))
NEVER = -3e38
LOWEST = -1e38
U = 7
assert U * U == NT and SLICES * SLICE == STRIP


class Chain:

    def __init__(self, p, eng, sem):
        self.p, self.eng, self.sem, self.base, self.n = p, eng, sem, 0, 0

    def at(self, base):
        self.base, self.n = base, 0

    def total(self):
        return self.base + self.n

    def __call__(self, ins, alone=False):
        ins.then_inc(self.sem, 1)
        self.n += 1
        self.eng.wait_ge(self.sem, self.base + self.n)
        if alone:
            self.p.alone(self.eng)


def spread(ap, axis, shape):
    return ap.unsqueeze(axis).broadcast_to(shape)


class Program:
    def __init__(self, nc, ctx, a):
        self.nc, self.ctx, self.a = nc, ctx, a
        self.in_use = []
        self.bank = [ctx.enter_context(nc.psum_tensor(f"bank{i}", [P, 512], F32)) for i in range(8)]
        self.ident = self.keep("ident", [P, P], F32)
        self.ones = self.keep("ones", [P, P], F32)
        self.earlier = self.keep("earlier", [P, P], BF16)
        self.onesb = self.keep("onesb", [P, P], BF16)
        self.count = self.keep("count", [P, DBINS], F32)
        self.node = self.keep("node", [P, NT + 1], F32)
        self.rec = self.keep("rec", [P, NT, REC], F32)
        self.eps = self.keep("eps", [P, 1], F32)
        self.win = self.keep("win", [P, NT, 2 * WIN], F32)
        self.start_i = self.keep("start_i", [P, NT], I32)
        self.id_i = self.keep("id_i", [P, NT], I32)
        self.items = self.keep("items", [1, NT], I32)
        self.items1 = self.keep("items1", [1, NT], I32)
        self.tails = self.keep("tails", [1, NT], I32)
        self.place_i = self.keep("place_i", [P, NT], I32)
        self.chunk_e_i = self.keep("chunk_e_i", [1, XCH], I32)
        self.two_i = self.keep("two_i", [1, 2], I32)
        self.two_w = self.keep("two_w", [P, 2], F32)
        self.ms = self.keep("ms", [P, NT, 4], F32)
        self.passed = self.sem("passed")
        self.ready = self.sem("ready")
        self.h_table = nc.dram_tensor("h_table", (NP, HROW), F32, kind="Internal").ap()
        self.windows = nc.dram_tensor("windows", (EP, 2 * WIN), F32, kind="Internal").ap()
        self.records = nc.dram_tensor("records", (NP, REC), F32, kind="Internal").ap()
        self.x_grouped = nc.dram_tensor("x_grouped", (XCH * P, REC), F32, kind="Internal").ap()
        self.y_grouped = nc.dram_tensor("y_grouped", (XCH * P, D), F32, kind="Internal").ap()
        self.transformed = nc.dram_tensor("transformed", (NP * RELS, D), F32, kind="Internal").ap()

    def alone(self, eng):
        eng.sem_inc(self.passed, 1)

    def keep(self, name, shape, dt):
        return self.ctx.enter_context(self.nc.sbuf_tensor(name, shape, dt))

    def sem(self, name):
        self.in_use.append(self.nc.alloc_semaphore(name))
        return self.in_use[-1]

    @contextmanager
    def phase(self):
        kept, self.in_use = self.in_use, []
        with ExitStack() as ctx:
            yield ctx
        self.nc.all_engine_barrier()
        self.nc.clear_and_free_semaphores(self.in_use)
        self.nc.all_engine_barrier()
        self.in_use = kept


def moments(p, dve, chain, stats, tiles, row):
    for t in tiles:
        ins = dve.bn_stats(stats[:, t, :], row(t))
    chain(ins)
    for t in tiles:
        ins = dve.bn_aggr(p.ms[:, t, 0:2], stats[:, t, :])
    return ins


class Front:

    LAG = 2

    def __init__(self, p, ctx, name):
        nc = p.nc
        self.p = p
        self.xn = [ctx.enter_context(nc.sbuf_tensor(f"{name}_xn{u}", [P, D], F32)) for u in range(U)]
        self.xt = [ctx.enter_context(nc.sbuf_tensor(f"{name}_xt{u}", [P, D], F32)) for u in range(U)]
        self.stats = ctx.enter_context(nc.sbuf_tensor(f"{name}_stats", [P, NT, 6], F32))
        self.varied, self.rooted, self.normed, self.turned, self.copied = (
            p.sem(f"{name}_{x}") for x in ("varied", "rooted", "normed", "turned", "copied"))

    def moments(self, dve, chain, row=None):
        ms = self.p.ms
        if row is not None:
            moments(self.p, dve, chain, self.stats, range(NT), row).then_inc(self.varied, 1)
        dve.wait_ge(self.rooted, 1)
        chain(dve.reciprocal(ms[:, :, 3], ms[:, :, 2]))

    def root(self, act, known=False):
        ms = self.p.ms
        if not known:
            act.wait_ge(self.varied, 1)
        act.activation(ms[:, :, 2], ms[:, :, 1], ACT.Sqrt, bias=self.p.eps[:, 0:1]).then_inc(self.rooted, 1)

    def norm(self, dve, x, g, u):
        ms = self.p.ms
        dve.wait_ge(self.turned, done(g - U))
        dve.tensor_scalar(self.xn[u][:], x, ms[:, bass.ds(g, 1), 0:1].rearrange("q o c -> q (o c)"),
                          ms[:, bass.ds(g, 1), 3:4].rearrange("q o c -> q (o c)"),
                          ALU.subtract, ALU.mult).then_inc(self.normed, 1)

    def turn(self, pe, g, u):
        pe.wait_ge(self.normed, done(g))
        pe.wait_ge(self.copied, done(g - 3))
        for k in range(KD):
            ins = pe.transpose(self.p.bank[u % 4][:, k * P:(k + 1) * P], self.xn[u][:, k * P:(k + 1) * P], self.p.ident[:])
        ins.then_inc(self.turned, 1)

    def copy(self, act, g, u, used):
        if used is not None:
            act.wait_ge(used, done(g - U))
        act.wait_ge(self.turned, done(g))
        act.activation(self.xt[u][:], self.p.bank[u % 4][:, 0:D], ACT.Copy).then_inc(self.copied, 1)

    def start(self, eng, *sems):
        for s in sems:
            eng.sem_inc(s, U)

    def scalar_loop(self, act, used, store=None):
        self.root(act)
        self.start(act, self.copied)
        with act.Fori(0, U) as i:
            for u in range(U if store is None else U + self.LAG):
                if u < U:
                    self.copy(act, i * U + u, u, used)
                if store is not None and u >= self.LAG:
                    store(i * U + (u - self.LAG), u - self.LAG)


def done(g):
    return g + (1 + U)


def rank_steps(dve, chain, hot, within, total, cum, base, tmp, rank, nb, align=None):
    chain(dve.memset(cum[:, 0, :], 0.0))
    for t in range(NT):
        chain(dve.tensor_tensor(cum[:, t + 1, :], cum[:, t, :], total[:, t, :], ALU.add))
    size, ends, part = base[:, 0, :], base[:, 1, :], base[:, 2, :]
    if align is not None:
        bits = P.bit_length() - 1
        chain(dve.tensor_scalar(align, cum[:, NT, :], float(P - 1), None, ALU.add))
        chain(dve.tensor_scalar(align, align, bits, bits, ALU.arith_shift_right, ALU.logical_shift_left))
        chain(dve.tensor_copy(size, align))
    else:
        chain(dve.tensor_copy(size, cum[:, NT, :]))
    chain(dve.memset(part, 0.0))
    chain(dve.tensor_tensor_scan(ends, size, part, 0.0, ALU.add, ALU.add))
    chain(dve.tensor_tensor(part, ends, size, ALU.subtract))
    chain(dve.tensor_tensor(tmp, within, cum[:, 0:NT, :], ALU.add))
    chain(dve.tensor_tensor(tmp, tmp, spread(part, 1, [P, NT, nb]), ALU.add))
    chain(dve.tensor_tensor(tmp, tmp, hot, ALU.mult))
    chain(dve.tensor_reduce(rank, tmp, AX, ALU.add))


def search_and_project(p: Program):
    nc, a = p.nc, p.a
    with p.phase() as ctx:
        def sb(n, s, d):
            return ctx.enter_context(nc.sbuf_tensor(n, s, d))

        xa = sb("xa", [P, NT, REC], F32)
        dst_rows = sb("dst_rows", [P, CG, P], I32)
        first = sb("first", [P, CG], F32)
        diag = sb("diag", [P, 2, P], F32)
        pivots = sb("pivots", [P, CG * P], F32)
        less = sb("less", [P, CG * P], BF16)
        chunks_below = sb("chunks_below", [P, NT + 1], F32)
        BY_VECTOR = 24
        edge_of, signs = (sb(n, [P, NT + 1 - BY_VECTOR], F32) for n in ("edge_of", "signs"))
        sign_out = sb("sign_out", [P, CG * P], BF16)
        signs_done = p.sem("signs_done")
        chunk = sb("chunk", [P, NT + 1], F32)
        chunk_i = sb("chunk_i", [P, NT + 1], I32)
        found = sb("found", [P, NT + 1, P], I32)
        start = sb("start", [P, NT + 1], F32)
        bin_ = sb("bin_", [P, NT], F32)
        hot = sb("hot", [P, NT, DBINS], BF16)
        scratch = p.rec[:].rearrange("q t c -> q (t c)")
        within, total, cum = (scratch[:, n * NT * DBINS:(n * NT + m) * DBINS].rearrange("q (t b) -> q t b", b=DBINS)
                              for n, m in ((0, NT), (1, NT), (2, NT + 1)))
        cmp = scratch[:, (3 * NT + 1) * DBINS:(3 * NT + 1) * DBINS + (NT + 1) * P // 2].bitcast(BF16)\
            .rearrange("q (t e) -> q t e", e=P)
        base = sb("base", [P, 3, DBINS], F32)
        rank = sb("rank", [P, NT], F32)
        rank_i = sb("rank_i", [P, NT], I32)
        shift = sb("shift", [P, 2, P], F32)
        s_src = sb("s_src", [P, STRIP + WIN], I32)
        s_typ = sb("s_typ", [P, STRIP + WIN], I32)
        s_key = sb("s_key", [P, STRIP + WIN], F32)
        s_wgt = sb("s_wgt", [P, STRIP + WIN], F32)
        w = SLICE * 2 * WIN
        wide = [p.win[:].rearrange("q t c -> q (t c)")[:, i * w:(i + 1) * w].rearrange("q (e c) -> q e c", c=2 * WIN) for i in range(2)]
        wa = sb("wa", [P, KD, HROW + HEADS], F32)
        att = sb("att", [P, 2, D], F32)
        prod = sb("prod", [P, D], F32)
        front = Front(p, ctx, "gat")
        hrow = [sb(f"hrow{i}", [P, HROW], F32) for i in range(U)]

        dst_in, x_in, w_in, att_in, edge_in = (p.sem(x) for x in ("dst_in", "x_in", "w_in", "att_in", "edge_in"))
        pivots_ready, chunks_ready, found_in = (p.sem(x) for x in ("pivots_ready", "chunks_ready", "found_in"))
        diag_ready, piv_done = p.sem("diag_ready"), p.sem("piv_done")
        start_ready, next_done, hot_ready, counts_done, counts_out = (p.sem(x) for x in ("start_ready", "next_done", "hot_ready", "counts_done", "counts_out"))
        rank_ready, scattered, rec_in = p.sem("rank_ready"), p.sem("scattered"), p.sem("rec_in")
        key_ready, wide_ready, wide_out = p.sem("key_ready"), p.sem("wide_ready"), [p.sem(f"wide_out{i}") for i in range(2)]
        wa_ready, h_psum, h_ready = (p.sem(x) for x in ("wa_ready", "h_psum", "h_ready"))
        h_stored = [p.sem(f"h_stored{i}") for i in range(U)]
        steps_v, steps_g = p.sem("steps_v"), p.sem("steps_g")
        zero_out = p.sem("zero_out")
        EARLY, BY_POOL = 14, 24

        def windows_of(q, n):
            strip = (s_key, s_wgt)[n]
            return bass.AP(tensor=strip[:].tensor, offset=q * SLICE, ap=[[STRIP + WIN, P], [1, SLICE], [1, WIN]])

        halves = [(0, 4), (4, 7)]
        block = ctx.enter_context(nc.Block())

        @block.sync
        def _(sp):
            sp.dma_start(dst_rows[:], a["dst"].rearrange("(g c e) -> c g e", c=P, e=P)).then_inc(dst_in, 16)
            for s, v in ((s_src, a["src"]), (s_typ, a["edge_type_16"]), (s_wgt, a["edge_weight1"])):
                strips = bass.AP(tensor=v.tensor, offset=0, ap=[[STRIP, P], [1, STRIP + WIN]])
                sp.dma_start(s[:], strips).then_inc(edge_in, 16)
            for i, n in enumerate(("L0_gnn_att_src", "L0_gnn_att_dst")):
                flat = a[n].rearrange("h d -> (h d)")
                sp.dma_start(att[:, i, :], bass.AP(tensor=flat.tensor, offset=0, ap=[[0, P], [1, D]])).then_inc(att_in, 16)
            for k in range(KD):
                sp.dma_start(wa[:, k, 0:HROW].rearrange("p (h c) -> p h c", c=HW)[:, :, 0:HEAD_DIM],
                             a["L0_gnn_W"][k * P:(k + 1) * P]).then_inc(w_in, 16)
            sp.dma_start(xa[:, :, 0:D], a["x"].rearrange("(t q) d -> q t d", q=P)).then_inc(x_in, 16)
            for q in range(SLICES):
                sp.wait_ge(wide_ready, q + 1)
                sp.dma_start(p.windows.rearrange("(q e) w -> q e w", q=P)[:, q * SLICE:(q + 1) * SLICE, :],
                             wide[q % 2]).then_inc(wide_out[q % 2], 16)
            for u in range(U):
                sp.wait_ge(h_stored[u], 16 * (U + 1))
            for i in range(2):
                sp.wait_ge(wide_out[i], 16 * ((SLICES + 1 - i) // 2))
            sp.wait_ge(scattered, 16 * NT)
            sp.dma_start(p.rec[:], p.records.rearrange("(t q) c -> q t c", q=P)).then_inc(rec_in, 16)
            sp.wait_ge(rec_in, 16)

        @block.gpsimd
        def _(pool):
            chain = Chain(p, pool, steps_g)
            chain(pool.memset(p.ident[:], 0.0))
            chain(pool.memset(p.ones[:], 1.0))
            chain(pool.memset(p.onesb[:], 1.0))
            chain(pool.memset(shift[:], 0.0))
            chain(pool.memset(p.eps[:], EPS))
            chain(pool.memset(p.earlier[:], 1.0))
            chain(pool.affine_select(out=p.ident[:], in_=p.ident[:], compare_op=ALU.not_equal, fill=1.0, base=0,
                                     pattern=[[-1, P]], channel_multiplier=1))
            chain(pool.affine_select(out=p.earlier[:], in_=p.earlier[:], compare_op=ALU.is_ge, fill=0.0, base=-1,
                                     pattern=[[1, P]], channel_multiplier=-1))
            chain(pool.affine_select(out=shift[:, 0, :], in_=shift[:, 0, :], compare_op=ALU.not_equal, fill=1.0, base=-1,
                                     pattern=[[-1, P]], channel_multiplier=1))
            chain(pool.affine_select(out=shift[:, 1, :], in_=shift[:, 1, :], compare_op=ALU.not_equal, fill=1.0, base=P - 1,
                                     pattern=[[-1, P]], channel_multiplier=P))
            chain(pool.iota(p.count[:], pattern=[[1, DBINS]], base=0, channel_multiplier=0,
                            allow_small_or_imprecise_dtypes=True))
            chain(pool.iota(p.node[:], pattern=[[P, NT + 1]], base=0, channel_multiplier=1,
                            allow_small_or_imprecise_dtypes=True))
            pool.memset(xa[:, :, D:REC], 0.0).then_inc(p.ready, 1)
            pool.wait_ge(p.ready, 1)
            pool.wait_ge(edge_in, 48)
            pool.wait_ge(key_ready, 1)

            def slices(lo, hi):
                for q in range(lo, hi):
                    if q >= 2:
                        pool.wait_ge(wide_out[q % 2], 16 * (q // 2))
                    for n in range(2):
                        ins = pool.tensor_copy(wide[q % 2][:, :, n * WIN:(n + 1) * WIN], windows_of(q, n))
                    ins.then_inc(wide_ready, 1)

            slices(0, EARLY)
            pool.wait_ge(chunks_ready, 1)
            table = a["dst"].rearrange("(c e) -> c e", e=P)
            for t in range(NT + 1):
                pool.indirect_dma_start(out=found[:, t, :], out_offset=None, in_=table,
                                        in_offset=bass.IndirectOffsetOnAxis(ap=chunk_i[:, t:t + 1], axis=0)).then_inc(found_in, 16)
            slices(EARLY, BY_POOL)
            pool.wait_ge(rank_ready, 1)
            pool.wait_ge(h_ready, done(NT - 1))
            for t in range(NT):
                pool.indirect_dma_start(out=p.records[:], out_offset=bass.IndirectOffsetOnAxis(ap=rank_i[:, t:t + 1], axis=0),
                                        in_=xa[:, t, :], in_offset=None).then_inc(scattered, 16)

        @block.vector
        def _(dve):
            chain = Chain(p, dve, steps_v)
            dve.wait_ge(edge_in, 48)
            dve.scalar_tensor_tensor(s_key[:], s_src[:], float(RELS), s_typ[:], ALU.mult, ALU.add).then_inc(key_ready, 1)
            dve.wait_ge(dst_in, 16)
            dve.wait_ge(p.ready, 1)
            chain(dve.tensor_copy(first[:], dst_rows[:, :, 0]))
            for g in range(CG):
                if g >= 2:
                    dve.wait_ge(piv_done, g - 1)
                dve.tensor_scalar(diag[:, g % 2, :], p.ident[:], first[:, g:g + 1], None, ALU.mult).then_inc(diag_ready, 1)
            for h in range(2):
                lo, hi = h * 4, min(4 * h + 4, CG)
                dve.wait_ge(piv_done, hi)
                chain(dve.tensor_copy(pivots[:, lo * P:hi * P], p.bank[h][:, 0:(hi - lo) * P]))
            chain(dve.tensor_scalar(edge_of[:], p.node[:, BY_VECTOR:], -0.5, None, ALU.add))
            dve.sem_inc(pivots_ready, 1)
            before = chain.total()
            with dve.Fori(0, BY_VECTOR) as t:
                chain.at(before + t)
                chain(dve.tensor_scalar(less[:], pivots[:], p.node[:, bass.ds(t, 1)], 0.0, ALU.is_lt, ALU.add,
                                        accum_out=chunks_below[:, bass.ds(t, 1)]))
            chain.at(before + BY_VECTOR)
            dve.wait_ge(signs_done, NT + 1 - BY_VECTOR)
            chain(dve.tensor_scalar(chunks_below[:, BY_VECTOR:], signs[:], float(CG * P), 0.5, ALU.add, ALU.mult))
            chain(dve.tensor_scalar(chunk[:], chunks_below[:], -1.0, 0.0, ALU.add, ALU.max))
            dve.tensor_copy(chunk_i[:], chunk[:]).then_inc(chunks_ready, 1)
            dve.wait_ge(x_in, 16)
            front.moments(dve, chain, lambda t: xa[:, t, 0:D])
            dve.wait_ge(att_in, 32)
            dve.wait_ge(w_in, 16 * KD)
            for k in range(KD):
                heads = wa[:, k, 0:HROW].rearrange("q (h c) -> q h c", c=HW)
                for i, out in enumerate((heads[:, :, HEAD_DIM], wa[:, k, HROW:HROW + HEADS])):
                    chain(dve.tensor_tensor(prod[:].rearrange("q (h c) -> q h c", h=HEADS), heads[:, :, 0:HEAD_DIM],
                                            att[:, i, :].rearrange("q (h c) -> q h c", h=HEADS), ALU.mult))
                    chain(dve.tensor_reduce(out, prod[:].rearrange("q (h c) -> q h c", h=HEADS), AX, ALU.add))
            dve.tensor_copy(prod[:, 0:1], wa[:, 0, 0:1]).then_inc(wa_ready, 1)
            front.start(dve, front.normed, h_ready)

            def row(g):
                return xa[:, bass.ds(g, 1), 0:D].rearrange("q o d -> q (o d)")

            def result(g, u, i):
                dve.wait_ge(h_psum, done(g))
                dve.wait_ge(h_stored[u], 16 * (i + 1))
                p.alone(dve)
                ps = p.bank[4 + u % 4]
                dve.tensor_copy(hrow[u][:], ps[:, 0:HROW])
                dve.tensor_copy(xa[:, bass.ds(g, 1), C_ADST:C_ADST + HEADS].rearrange("q o d -> q (o d)"),
                                ps[:, HROW:HROW + HEADS]).then_inc(h_ready, 1)

            with dve.Fori(0, U) as i:
                for u in range(U + front.LAG):
                    if u < U:
                        front.norm(dve, row(i * U + u), i * U + u, u)
                    if u >= front.LAG:
                        result(i * U + (u - front.LAG), u - front.LAG, i)
            dve.wait_ge(found_in, 16 * (NT + 1))
            chain(dve.tensor_tensor(cmp, found[:], spread(p.node[:], 2, [P, NT + 1, P]), ALU.is_lt))
            chain(dve.tensor_reduce(start[:], cmp, AX, ALU.add))
            chain(dve.scalar_tensor_tensor(start[:], chunk[:], float(P), start[:], ALU.mult, ALU.add))
            dve.tensor_copy(xa[:, :, C_START], start[:, 0:NT]).then_inc(start_ready, 1)
            dve.wait_ge(next_done, 1)
            chain(dve.tensor_tensor(xa[:, :, C_DEG], p.bank[0][:, 0:NT], start[:, 0:NT], ALU.subtract))
            chain(dve.tensor_copy(xa[:, :, C_ID], p.node[:, 0:NT]))
            chain(dve.tensor_scalar(bin_[:], xa[:, :, C_DEG], -1.0, float(DBINS - 1), ALU.mult, ALU.add))
            chain(dve.tensor_scalar(bin_[:], bin_[:], 0.0, None, ALU.max))
            dve.tensor_tensor(hot[:], spread(bin_[:], 2, [P, NT, DBINS]), spread(p.count[:], 1, [P, NT, DBINS]),
                              ALU.is_equal).then_inc(hot_ready, 1)
            for lo, hi in halves:
                for g in range(lo, hi):
                    dve.wait_ge(counts_done, g + 1)
                    for n, to in enumerate((within, total)):
                        dve.tensor_copy(to[:, g * U:(g + 1) * U, :].rearrange("q t b -> q (t b)"),
                                        p.bank[2 * (g - lo) + n][:, 0:U * DBINS]).then_inc(counts_out, 1)
            dve.wait_ge(counts_out, 2 * U)
            rank_steps(dve, chain, hot[:], within, total, cum, base, within, rank[:], DBINS)
            dve.tensor_copy(rank_i[:], rank[:]).then_inc(rank_ready, 1)

        @block.tensor
        def _(pe):
            pe.wait_ge(p.ready, 1)
            for g in range(CG):
                pe.wait_ge(diag_ready, g + 1)
                pe.matmul(p.bank[g // 4][:, (g % 4) * P:(g % 4 + 1) * P], p.ones[:], diag[:, g % 2, :],
                          start=True, stop=True).then_inc(piv_done, 1)
            pe.wait_ge(wa_ready, 1)
            pe.wait_ge(pivots_ready, 1)
            front.start(pe, front.turned, h_psum)

            def project(g, u):
                pe.wait_ge(front.copied, done(g))
                pe.wait_ge(h_ready, done(g - 3))
                for k in range(KD):
                    ins = pe.matmul(p.bank[4 + u % 4][:, 0:HROW + HEADS], front.xt[u][:, k * P:(k + 1) * P], wa[:, k, :],
                                    start=(k == 0), stop=(k == KD - 1))
                ins.then_inc(h_psum, 1)

            with pe.Fori(0, U) as i:
                for u in range(U):
                    front.turn(pe, i * U + u, u)
                    if u >= 1:
                        project(i * U + (u - 1), u - 1)
                project(i * U + (U - 1), U - 1)
            pe.wait_ge(front.copied, done(NT - 1))
            pe.wait_ge(h_ready, done(NT - 1))
            pe.wait_ge(start_ready, 1)
            pe.matmul(p.bank[0][:, 0:NT], shift[:, 0, :], start[:, 0:NT], start=True, stop=False)
            pe.matmul(p.bank[0][:, 0:NT], shift[:, 1, :], start[:, 1:NT + 1], start=False, stop=True).then_inc(next_done, 1)
            pe.wait_ge(hot_ready, 1)
            for lo, hi in halves:
                if lo:
                    pe.wait_ge(counts_out, 2 * lo)
                for g in range(lo, hi):
                    rows = hot[:, g * U:(g + 1) * U, :].rearrange("q t b -> q (t b)")
                    pe.matmul(p.bank[2 * (g - lo)][:, 0:U * DBINS], p.earlier[:], rows, start=True, stop=True)
                    pe.matmul(p.bank[2 * (g - lo) + 1][:, 0:U * DBINS], p.onesb[:], rows, start=True, stop=True)\
                      .then_inc(counts_done, 1)

        @block.scalar
        def _(act):
            act.wait_ge(p.ready, 1)
            act.wait_ge(pivots_ready, 1)
            for t in range(NT + 1 - BY_VECTOR):
                if t >= 1:
                    act.wait_ge(signs_done, t)
                act.activation(sign_out[:], pivots[:], ACT.Sign, scale=-1.0, bias=edge_of[:, t:t + 1],
                               accum_out=signs[:, t:t + 1]).then_inc(signs_done, 1)
            rows = p.h_table.rearrange("(t q) c -> t q c", q=P)
            for u in range(U):
                act.sem_inc(h_stored[u], 16)

            def store(g, u):
                act.wait_ge(h_ready, done(g))
                act.dma_start(rows[bass.ds(g, 1)].rearrange("o q c -> (o q) c"), hrow[u][:]).then_inc(h_stored[u], 16)

            front.scalar_loop(act, h_psum, store)
            for q in range(BY_POOL, SLICES):
                act.wait_ge(wide_ready, q)
                act.wait_ge(wide_out[q % 2], 16 * (q // 2))
                for n in range(2):
                    ins = act.activation(wide[q % 2][:, :, n * WIN:(n + 1) * WIN], windows_of(q, n), ACT.Copy)
                ins.then_inc(wide_ready, 1)


def load_windows(p, pool, landed):
    for t in range(NT):
        pool.indirect_dma_start(out=p.win[:, t, :], out_offset=None, in_=p.windows[:],
                                in_offset=bass.IndirectOffsetOnAxis(ap=p.start_i[:, t:t + 1], axis=0)).then_inc(landed, 16)


def in_order(eng, n, item, last=None, slots=SLOTS, s=0):
    item(s)
    if s + 1 < slots:
        with eng.If(n > s + 1):
            in_order(eng, n, item, last, slots, s + 1)
        if last is not None:
            with eng.Else():
                last(s)
    elif last is not None:
        last(s)


def attention(p: Program):
    nc, a = p.nc, p.a
    with p.phase() as ctx:
        def sb(n, s, d):
            return ctx.enter_context(nc.sbuf_tensor(n, s, d))

        most = sb("most", [NT, 1], F32)
        most_i = sb("most_i", [1, NT], I32)
        row = sb("row", [1, 3, NT], F32)
        key_i = sb("key_i", [P, NT, WIN], I32)
        src_i = sb("src_i", [P, NT + 1, WIN], I32)
        mask = sb("mask", [P, NT, WIN], F32)
        ZEROS = 16
        zeros = sb("zeros", [P, XCH // ZEROS * REC], F32)
        bias = sb("gat_bias", [P, D], F32)
        idx = [sb(f"gat_idx{s}", [P, COLS[s]], I32) for s in range(SLOTS)]
        rows = [sb(f"gat_rows{s}", [P, COLS[s], HROW], F32) for s in range(SLOTS)]
        msg = [sb(f"gat_msg{s}", [P, COLS[s], HROW], F32) for s in range(SLOTS)]
        NS = [c * HEADS for c in COLS]
        score = [sb(f"gat_score{s}", [P, NS[s] + HEADS], F32) for s in range(SLOTS)]
        item_max = sb("item_max", [P, SLOTS, HEADS], F32)
        top = sb("top", [P, SLOTS + 1, HEADS], F32)
        fade = [sb(f"gat_fade{s}", [P, HEADS], F32) for s in range(SLOTS)]
        warm = sb("gat_warm", [P, 1], F32)
        acc = sb("gat_acc", [P, HROW], F32)
        inv = sb("gat_inv", [P, 2, HEADS], F32)
        o = sb("gat_o", [P, D], F32)
        t_pos = sb("t_pos", [P, 3], F32)
        t_at_i = sb("t_at_i", [P, 1], I32)
        t_win = sb("t_win", [P, 2 * WIN], F32)
        t_key = sb("t_key", [P, JCOL], I32)
        t_idx_i = sb("t_idx_i", [P, JCOL], I32)
        t_mask = sb("t_mask", [P, JCOL], F32)

        bias_in, start_ready, wins_in = (p.sem(x) for x in ("gat_bias_in", "gat_start_ready", "gat_wins_in"))
        warmed = p.sem("gat_warmed")
        zeros_ready, zeroed = p.sem("zeros_ready"), p.sem("zeroed")
        turned, most_ready, row_done, tables = (p.sem(x) for x in ("deg_turned", "most_ready", "row_done", "tables"))
        per_slot = lambda name: [p.sem(f"{name}{s}") for s in range(SLOTS)]
        idx_ready, gathered, scores_ready, p_ready, msg_ready, sum_ready, acc_done = (
            per_slot(f"gat_{x}") for x in ("idx_ready", "gathered", "scores", "p_ready", "msg_ready", "sum_ready", "acc_done"))
        step, steps_s, steps_a, steps_t = p.sem("gat_step"), per_slot("gat_steps_s"), per_slot("gat_steps_a"), p.sem("gat_steps_t")
        t_at, t_window, t_idx, t_rows, t_scores, t_p, t_msg, t_sum, t_done, t_steps, t_begin = (
            p.sem(f"gat_t_{x}") for x in ("at", "window", "idx", "rows", "scores", "p", "msg", "sum", "done", "steps", "begin"))
        block = ctx.enter_context(nc.Block())

        def items(eng, t):
            return eng.value_load(p.items[0:1, bass.ds(t, 1)], min_val=1, max_val=-(-N_EDGES // JCOL))

        def tail_base(eng, t):
            return eng.value_load(p.tails[0:1, bass.ds(t, 1)], min_val=0, max_val=N_EDGES)

        @block.sync
        def _(sp):
            flat = a["L0_gnn_bias"]
            sp.dma_start(bias[:], bass.AP(tensor=flat.tensor, offset=0, ap=[[0, P], [1, D]])).then_inc(bias_in, 16)
            sp.wait_ge(bias_in, 16)
            sp.wait_ge(zeros_ready, 1)
            for z in range(ZEROS):
                sp.dma_start(p.x_grouped.rearrange("(z q e) c -> z q (e c)", z=ZEROS, q=P)[z], zeros[:]).then_inc(zeroed, 16)
            sp.wait_ge(zeroed, 16 * ZEROS)

        @block.gpsimd
        def _(pool):
            pool.memset(zeros[:], 0.0).then_inc(zeros_ready, 1)
            pool.wait_ge(start_ready, 1)
            load_windows(p, pool, wins_in)
            pool.wait_ge(tables, 1)
            with pool.Fori(0, NT) as t:
                n = items(pool, t)

                def gather(s):
                    pool.wait_ge(idx_ready[s], t + 1)
                    pool.wait_ge(msg_ready[s], t + 1)
                    p.alone(pool)
                    for j in range(COLS[s]):
                        pool.indirect_dma_start(out=rows[s][:, j, :], out_offset=None, in_=p.h_table[:],
                                                in_offset=bass.IndirectOffsetOnAxis(ap=idx[s][:, j:j + 1], axis=0))\
                            .then_inc(gathered[s], 16)

                in_order(pool, n, gather)
                with pool.If(n > SLOTS):
                    c0 = tail_base(pool, t)
                    with pool.Fori(SLOTS, n) as k:
                        c = c0 + k - SLOTS
                        pool.wait_ge(t_at, c + 1)
                        p.alone(pool)
                        pool.indirect_dma_start(out=t_win[:], out_offset=None, in_=p.windows[:],
                                                in_offset=bass.IndirectOffsetOnAxis(ap=t_at_i[:, 0:1], axis=0)).then_inc(t_window, 16)
                        pool.wait_ge(t_idx, c + 1)
                        p.alone(pool)
                        for j in range(JCOL):
                            pool.indirect_dma_start(out=rows[LAST][:, j, :], out_offset=None, in_=p.h_table[:],
                                                    in_offset=bass.IndirectOffsetOnAxis(ap=t_idx_i[:, j:j + 1], axis=0))\
                                .then_inc(t_rows, 16)
                        pool.wait_ge(t_done, c + 1)
                        p.alone(pool)

        @block.scalar
        def _(act):
            act.wait_ge(tables, 1)
            for s in range(SLOTS):
                act.activation(idx[s][:], src_i[:, 0, AT[s]:AT[s] + COLS[s]], ACT.Copy).then_inc(idx_ready[s], 1)

            def exps(s):
                act.activation(msg[s][:].rearrange("q j c -> q (j c)")[:, HEAD_DIM::HW], score[s][:, 0:NS[s]], ACT.Exp)
                return act.activation(fade[s][:], score[s][:, NS[s]:], ACT.Exp)

            act.sem_inc(warmed, 1)
            with act.Fori(0, NT) as t:
                n = items(act, t)
                act.wait_ge(warmed, t + 1)
                act.activation(warm[:], p.eps[:], ACT.Exp).then_inc(warmed, 1)

                def item(s):
                    act.wait_ge(sum_ready[s], t + 1)
                    act.wait_ge(acc_done[s], t + 1)
                    act.wait_ge(scores_ready[s], t + 1)
                    exps(s).then_inc(p_ready[s], 1)
                    act.wait_ge(gathered[s], 16 * COLS[s] * (t + 1))
                    p.alone(act)
                    act.activation(idx[s][:], src_i[:, bass.ds(t + 1, 1), AT[s]:AT[s] + COLS[s]].rearrange("q o j -> q (o j)"),
                                   ACT.Copy).then_inc(idx_ready[s], 1)

                in_order(act, n, item)
                with act.If(n > SLOTS):
                    c0 = tail_base(act, t)
                    with act.Fori(SLOTS, n) as k:
                        act.wait_ge(t_scores, c0 + k - SLOTS + 1)
                        exps(LAST).then_inc(t_p, 1)

        @block.tensor
        def _(pe):
            pe.transpose(p.bank[0][0:NT, 0:P], p.rec[:, :, C_DEG], p.ident[:]).then_inc(turned, 1)
            pe.wait_ge(most_ready, 1)
            pe.matmul(p.bank[1][0:1, 0:NT], most[:], p.ident[0:NT, 0:NT], start=True, stop=True).then_inc(row_done, 1)
            pe.wait_ge(tables, 1)

            for s in range(SLOTS):
                pe.sem_inc(sum_ready[s], 1)

            def total(s):
                for j in range(COLS[s]):
                    ins = pe.matmul(p.bank[s][:, 0:HROW], p.ident[:], msg[s][:, j, :], start=(j == 0), stop=(j == COLS[s] - 1))
                return ins

            with pe.Fori(0, NT) as t:
                n = items(pe, t)

                def item(s):
                    pe.wait_ge(acc_done[s], t + 1)
                    pe.wait_ge(msg_ready[s], t + 2)
                    total(s).then_inc(sum_ready[s], 1)

                in_order(pe, n, item)
                with pe.If(n > SLOTS):
                    c0 = tail_base(pe, t)
                    with pe.Fori(SLOTS, n) as k:
                        pe.wait_ge(t_msg, c0 + k - SLOTS + 1)
                        total(LAST).then_inc(t_sum, 1)

        @block.vector
        def _(dve):
            chain = Chain(p, dve, step)
            chain(dve.tensor_copy(p.id_i[:], p.rec[:, :, C_ID]))
            dve.tensor_copy(p.start_i[:], p.rec[:, :, C_START]).then_inc(start_ready, 1)
            dve.wait_ge(turned, 1)
            dve.tensor_reduce(most[:], p.bank[0][0:NT, 0:P], AX, ALU.max).then_inc(most_ready, 1)
            dve.wait_ge(row_done, 1)
            for cols, to in ((COLS, row[:, 0, :]), (COLS1, row[:, 1, :])):
                chain(dve.tensor_scalar(most_i[:], p.bank[1][0:1, 0:NT], float(cols[1] - 1), None, ALU.add))
                chain(dve.tensor_scalar(most_i[:], most_i[:], cols[1].bit_length() - 1, None, ALU.arith_shift_right))
                chain(dve.tensor_scalar(to, most_i[:], 1.0 - cols[0] // cols[1], 1.0, ALU.add, ALU.max))
            chain(dve.tensor_copy(p.items1[:], row[:, 1, :]))
            chain(dve.tensor_copy(p.items[:], row[:, 0, :]))
            chain(dve.tensor_scalar(row[:, 0, :], row[:, 0, :], -float(SLOTS), 0.0, ALU.add, ALU.max))
            chain(dve.memset(row[:, 1, :], 0.0))
            chain(dve.tensor_tensor_scan(row[:, 2, :], row[:, 0, :], row[:, 1, :], 0.0, ALU.add, ALU.add))
            chain(dve.tensor_tensor(row[:, 2, :], row[:, 2, :], row[:, 0, :], ALU.subtract))
            chain(dve.tensor_copy(p.tails[:], row[:, 2, :]))
            chain(dve.tensor_tensor(mask[:], spread(p.count[:, 0:WIN], 1, [P, NT, WIN]),
                                    p.rec[:, :, C_DEG:C_DEG + 1].broadcast_to([P, NT, WIN]), ALU.is_ge))
            chain(dve.tensor_scalar(mask[:], mask[:], NEVER, None, ALU.mult))
            chain(dve.memset(src_i[:, NT, :], 0))
            dve.wait_ge(wins_in, 16 * NT)
            chain(dve.tensor_copy(key_i[:], p.win[:, :, 0:WIN]))
            dve.tensor_scalar(src_i[:, 0:NT, :], key_i[:], RELS.bit_length() - 1, None, ALU.arith_shift_right).then_inc(tables, 1)
            dve.wait_ge(tables, 1)
            dve.wait_ge(bias_in, 16)

            def heads(ap):
                return ap.rearrange("q (h c) -> q h c", h=HEADS)

            def scores(chain, s, t, masked, old, new, biggest, ready):
                sc = score[s][:, 0:NS[s]].rearrange("q (j h) -> q j h", h=HEADS)
                g = rows[s][:].rearrange("q j (h c) -> q j h c", c=HW)
                chain(dve.tensor_tensor(sc, g[:, :, :, HEAD_DIM],
                                        p.rec[:, bass.ds(t, 1), C_ADST:C_ADST + HEADS].broadcast_to([P, COLS[s], HEADS]), ALU.add))
                chain(dve.scalar_tensor_tensor(sc, sc, 0.2, sc, ALU.mult, ALU.max))
                chain(dve.tensor_tensor(sc, sc, masked, ALU.add))
                chain(dve.tensor_reduce(biggest, score[s][:, 0:NS[s]].rearrange("q (j h) -> q h j", h=HEADS), AX, ALU.max))
                chain(dve.tensor_tensor(new, old, biggest, ALU.max))
                dve.tensor_tensor(sc, sc, spread(new, 1, [P, COLS[s], HEADS]), ALU.subtract)
                dve.tensor_tensor(score[s][:, NS[s]:], old, new, ALU.subtract).then_inc(ready, 1)

            def messages(s, ready):
                g = rows[s][:].rearrange("q j (h c) -> q (j h) c", c=HW)
                m = msg[s][:].rearrange("q j (h c) -> q (j h) c", c=HW)
                dve.tensor_tensor(m[:, :, 0:HEAD_DIM], g[:, :, 0:HEAD_DIM],
                                  m[:, :, HEAD_DIM:HW].broadcast_to([P, NS[s], HEAD_DIM]), ALU.mult).then_inc(ready, 1)

            def accumulate(chain, s, finished):
                chain(dve.tensor_tensor(heads(acc[:]), heads(acc[:]), spread(fade[s][:], 2, [P, HEADS, HW]), ALU.mult))
                dve.tensor_tensor(acc[:], acc[:], p.bank[s][:, 0:HROW], ALU.add).then_inc(finished, 1)

            for s in range(SLOTS):
                dve.sem_inc(msg_ready[s], 1)
                dve.sem_inc(acc_done[s], 1)
            chain_s = [Chain(p, dve, x) for x in steps_s]
            chain_a = [Chain(p, dve, x) for x in steps_a]
            chain_t, chain_k = Chain(p, dve, steps_t), Chain(p, dve, t_steps)
            TAIL_STEPS = 11
            with dve.Fori(0, NT) as t:
                n = items(dve, t)
                chain_t.at(t * 6)
                chain_t(dve.memset(top[:, 0, :], LOWEST))

                def front_of(s):
                    chain_s[s].at(t * 5)
                    dve.wait_ge(gathered[s], 16 * COLS[s] * (t + 1))
                    scores(chain_s[s], s, t, mask[:, bass.ds(t, 1), AT[s]:AT[s] + COLS[s]].rearrange("q o j -> q j o")
                           .broadcast_to([P, COLS[s], HEADS]), top[:, s, :], top[:, s + 1, :], item_max[:, s, :], scores_ready[s])
                    assert chain_s[s].n == 5

                def middle_of(s):
                    dve.wait_ge(p_ready[s], t + 1)
                    messages(s, msg_ready[s])

                def back_of(s):
                    chain_a[s].at(t)
                    dve.wait_ge(sum_ready[s], t + 2)
                    if s == 0:
                        p.alone(dve)
                        dve.tensor_copy(acc[:], p.bank[s][:, 0:HROW]).then_inc(acc_done[s], 1)
                    else:
                        accumulate(chain_a[s], s, acc_done[s])
                    dve.wait_ge(acc_done[s], t + 2)
                    p.alone(dve)

                def item(s):
                    front_of(s)
                    if s >= 1:
                        middle_of(s - 1)
                    if s >= 3:
                        back_of(s - 3)

                def last(s):
                    middle_of(s)
                    for r in range(max(0, s - 2), s + 1):
                        back_of(r)

                in_order(dve, n, item, last)
                with dve.If(n > SLOTS):
                    c0 = tail_base(dve, t)
                    dve.tensor_scalar(t_pos[:, 0:1], p.rec[:, bass.ds(t, 1), C_START:C_START + 1].rearrange("q o c -> q (o c)"),
                                      float(WIN), None, ALU.add)
                    dve.tensor_scalar(t_pos[:, 1:2], p.rec[:, bass.ds(t, 1), C_DEG:C_DEG + 1].rearrange("q o c -> q (o c)"),
                                      -float(WIN), None, ALU.add).then_inc(t_begin, 1)
                    dve.wait_ge(t_begin, t + 1)
                    p.alone(dve)
                    with dve.Fori(SLOTS, n) as k:
                        c = c0 + k - SLOTS
                        chain_k.at(c * TAIL_STEPS)
                        dve.tensor_scalar(t_at_i[:], t_pos[:, 0:1], float(N_EDGES), None, ALU.min).then_inc(t_at, 1)
                        dve.wait_ge(t_window, 16 * (c + 1))
                        chain_k(dve.tensor_copy(t_key[:], t_win[:, 0:JCOL]))
                        dve.tensor_scalar(t_idx_i[:], t_key[:], RELS.bit_length() - 1, None, ALU.arith_shift_right).then_inc(t_idx, 1)
                        chain_k(dve.tensor_scalar(t_mask[:], p.count[:, 0:JCOL], t_pos[:, 1:2], NEVER, ALU.is_ge, ALU.mult))
                        dve.wait_ge(t_rows, 16 * JCOL * (c + 1))
                        scores(chain_k, LAST, t, spread(t_mask[:], 2, [P, JCOL, HEADS]), top[:, SLOTS, :], top[:, 0, :],
                               item_max[:, 0, :], t_scores)
                        dve.wait_ge(t_p, c + 1)
                        messages(LAST, t_msg)
                        dve.wait_ge(t_msg, c + 1)
                        p.alone(dve)
                        chain_k(dve.tensor_copy(top[:, SLOTS, :], top[:, 0, :]))
                        dve.wait_ge(t_sum, c + 1)
                        accumulate(chain_k, LAST, t_done)
                        dve.wait_ge(t_done, c + 1)
                        p.alone(dve)
                        chain_k(dve.tensor_scalar(t_pos[:, 0:1], t_pos[:, 0:1], float(JCOL), None, ALU.add))
                        chain_k(dve.tensor_scalar(t_pos[:, 1:2], t_pos[:, 1:2], -float(JCOL), None, ALU.add))
                        assert chain_k.n == TAIL_STEPS, chain_k.n
                chain_t(dve.tensor_scalar(inv[:, 0, :], heads(acc[:])[:, :, HEAD_DIM], 1e-16, None, ALU.add))
                chain_t(dve.reciprocal(inv[:, 1, :], inv[:, 0, :]))
                chain_t(dve.tensor_tensor(heads(o[:]), heads(acc[:])[:, :, 0:HEAD_DIM], spread(inv[:, 1, :], 2, [P, HEADS, HEAD_DIM]), ALU.mult))
                chain_t(dve.tensor_tensor(o[:], o[:], bias[:], ALU.add))
                x = p.rec[:, bass.ds(t, 1), 0:D].rearrange("q o d -> q (o d)")
                chain_t(dve.scalar_tensor_tensor(x, o[:], 0.0, x, ALU.max, ALU.add))
                assert chain_t.n == 6


def tile_row(p, g, lo=0, hi=D):
    return p.rec[:, bass.ds(g, 1), lo:hi].rearrange("q o d -> q (o d)")


def route(p: Program):
    nc, a = p.nc, p.a
    with p.phase() as ctx:
        def sb(n, s, d):
            return ctx.enter_context(nc.sbuf_tensor(n, s, d))

        front = Front(p, ctx, "route")
        rw = sb("rw", [E0, D], F32)
        rwt = sb("rwt", [P, KD, E0], F32)
        rb = sb("rb", [P, E0], F32)
        logits = sb("logits", [P, U, E0], F32)
        best = sb("best", [P, U, 8], F32)
        best_i = sb("best_i", [P, U, 8], U32)
        expert = sb("expert", [P, NT], F32)
        hot = sb("hot0", [P, NT, E0], BF16)
        within = sb("within0", [P, NT, E0], F32)
        total = sb("total0", [P, NT, E0], F32)
        cum = sb("cum0", [P, NT + 1, E0], F32)
        base = sb("base0", [P, 3, E0], F32)
        align = sb("align0", [P, E0], I32)
        place = sb("place", [P, NT], F32)
        begins = sb("begins", [1, XCH], F32)
        past = sb("past", [1, XCH, E0], F32)
        chunk_e = sb("chunk_e", [1, XCH], F32)

        rw_in, rb_in, rw_turned, rwt_ready, logits_done, chosen = (
            p.sem(f"route_{x}") for x in ("rw_in", "rb_in", "rw_turned", "rwt_ready", "logits_done", "chosen"))
        hot_ready, counts_done, counts_out, place_ready, scattered, begins_ready, steps = (
            p.sem(f"route_{x}") for x in ("hot_ready", "counts_done", "counts_out", "place_ready", "scattered", "begins_ready", "steps"))
        block = ctx.enter_context(nc.Block())

        @block.sync
        def _(sp):
            sp.dma_start(rw[:], a["L0_ffn_router_w"]).then_inc(rw_in, 16)
            sp.dma_start(rb[:], bass.AP(tensor=a["L0_ffn_router_b"].tensor, offset=0, ap=[[0, P], [1, E0]])).then_inc(rb_in, 16)

        @block.gpsimd
        def _(pool):
            pool.iota(begins[:], pattern=[[P, XCH]], base=0, channel_multiplier=0,
                      allow_small_or_imprecise_dtypes=True).then_inc(begins_ready, 1)
            pool.wait_ge(place_ready, 1)
            for t in range(NT):
                pool.indirect_dma_start(out=p.x_grouped[:], out_offset=bass.IndirectOffsetOnAxis(ap=p.place_i[:, t:t + 1], axis=0),
                                        in_=p.rec[:, t, :], in_offset=None).then_inc(scattered, 16)
            pool.wait_ge(scattered, 16 * NT)

        @block.scalar
        def _(act):
            front.scalar_loop(act, logits_done)

        @block.tensor
        def _(pe):
            pe.wait_ge(rw_in, 16)
            for k in range(KD):
                ins = pe.transpose(p.bank[7][:, k * E0:(k + 1) * E0], rw[:, k * P:(k + 1) * P], p.ident[0:E0, 0:E0])
            ins.then_inc(rw_turned, 1)
            pe.wait_ge(rwt_ready, 1)
            front.start(pe, front.turned, logits_done)

            def product(g, u):
                pe.wait_ge(front.copied, done(g))
                pe.wait_ge(chosen, done(g - 3))
                for k in range(KD):
                    ins = pe.matmul(p.bank[4 + u % 4][:, 0:E0], front.xt[u][:, k * P:(k + 1) * P], rwt[:, k, :],
                                    start=(k == 0), stop=(k == KD - 1))
                ins.then_inc(logits_done, 1)

            with pe.Fori(0, U) as i:
                for u in range(U):
                    front.turn(pe, i * U + u, u)
                    if u >= 1:
                        product(i * U + (u - 1), u - 1)
                product(i * U + (U - 1), U - 1)
            pe.wait_ge(hot_ready, 1)
            for g in range(U):
                rows = hot[:, g * U:(g + 1) * U, :].rearrange("q t b -> q (t b)")
                pe.matmul(p.bank[g][:, 0:U * E0], p.earlier[:], rows, start=True, stop=True)
                pe.matmul(p.bank[g][:, U * E0:2 * U * E0], p.onesb[:], rows, start=True, stop=True).then_inc(counts_done, 1)

        @block.vector
        def _(dve):
            chain = Chain(p, dve, steps)
            dve.wait_ge(rw_turned, 1)
            dve.tensor_copy(rwt[:].rearrange("q k e -> q (k e)"), p.bank[7][:, 0:KD * E0]).then_inc(rwt_ready, 1)
            dve.wait_ge(rb_in, 16)
            front.moments(dve, chain, lambda t: p.rec[:, t, 0:D])
            chain(dve.tensor_copy(p.rec[:, :, D:D + 4], p.ms[:]))
            before = chain.total()
            front.start(dve, front.normed, chosen)
            K = 3

            def choose(g, u):
                dve.wait_ge(logits_done, done(g))
                chain(dve.tensor_tensor(logits[:, u, :], p.bank[4 + u % 4][:, 0:E0], rb[:], ALU.add), True)
                chain(dve.max(best[:, u, :], logits[:, u, :]), True)
                chain(dve.max_index(best_i[:, u, :], best[:, u, :], logits[:, u, :]), True)
                dve.tensor_copy(expert[:, bass.ds(g, 1)], best_i[:, u, 0:1]).then_inc(chosen, 1)

            with dve.Fori(0, U) as i:
                chain.at(i * (K * U) + before)
                for u in range(U + front.LAG):
                    if u < U:
                        front.norm(dve, tile_row(p, i * U + u), i * U + u, u)
                    if u >= front.LAG:
                        choose(i * U + (u - front.LAG), u - front.LAG)
                assert chain.n == K * U
            chain.at(K * NT + before)
            dve.wait_ge(chosen, done(NT - 1))
            dve.tensor_tensor(hot[:], spread(expert[:], 2, [P, NT, E0]), spread(p.count[:, 0:E0], 1, [P, NT, E0]),
                              ALU.is_equal).then_inc(hot_ready, 1)
            for g in range(U):
                dve.wait_ge(counts_done, g + 1)
                for n, to in enumerate((within, total)):
                    dve.tensor_copy(to[:, g * U:(g + 1) * U, :].rearrange("q t b -> q (t b)"),
                                    p.bank[g][:, n * U * E0:(n + 1) * U * E0]).then_inc(counts_out, 1)
            dve.wait_ge(counts_out, 2 * U)
            rank_steps(dve, chain, hot[:], within[:], total[:], cum, base, within[:], place[:], E0, align[:])
            dve.tensor_copy(p.place_i[:], place[:]).then_inc(place_ready, 1)
            dve.wait_ge(begins_ready, 1)
            chain(dve.tensor_tensor(past[:], spread(base[0:1, 1, :], 1, [1, XCH, E0]), spread(begins[:], 2, [1, XCH, E0]), ALU.is_le))
            chain(dve.tensor_reduce(chunk_e[:], past[:], AX, ALU.add))
            chain(dve.tensor_scalar(p.chunk_e_i[:], chunk_e[:], float(E0 - 1), None, ALU.min))


def experts(p: Program):
    nc, a = p.nc, p.a
    V = 8
    assert XCH % V == 0

    def signalled(g):
        return g + (1 + V)

    with p.phase() as ctx:
        def sb(n, s, d):
            return ctx.enter_context(nc.sbuf_tensor(n, s, d))

        def slots(n, s, d):
            return [sb(f"{n}{v}", s, d) for v in range(V)]

        x, w1, b1 = slots("ex_x", [P, REC], F32), slots("ex_w1_", [P, KD, H0], F32), slots("ex_b1_", [H0, 1], F32)
        w2 = sb("ex_w2", [H0 + 1, E0, D], F32)
        b1_rows, b1_cols = sb("ex_b1_rows", [E0, H0], F32), sb("ex_b1_cols", [H0, E0], F32)
        xn, xt, hid, y = slots("ex_xn", [P, D], F32), slots("ex_xt", [P, D], F32), slots("ex_h", [H0 + 1, P], F32), slots("ex_y", [P, D], F32)
        back = sb("back", [P, NT, D], F32)
        stats, steps = sb("ex_stats", [P, NT, 6], F32), p.sem("ex_steps")
        x_in, w_in, y_out = ([p.sem(f"ex_{n}{v}") for v in range(V)] for n in ("x_in", "w_in", "y_out"))
        normed, turned, copied, hid_done, hid_ready, y_done, y_ready = (
            p.sem(f"ex_{n}") for n in ("normed", "turned", "copied", "hid_done", "hid_ready", "y_done", "y_ready"))
        b1_in, w2_in, b1_turned, b1_ready, ones_ready = (
            p.sem(f"ex_{n}") for n in ("b1_in", "w2_in", "b1_turned", "b1_ready", "ones_ready"))
        fetched = [p.sem(f"fetched{g}") for g in range(U)]
        block = ctx.enter_context(nc.Block())

        def expert_of(eng, g):
            return eng.value_load(p.chunk_e_i[0:1, bass.ds(g, 1)], min_val=0, max_val=E0 - 1)

        @block.sync
        def _(sp):
            sp.dma_start(b1_rows[:], a["L0_ffn_b1"]).then_inc(b1_in, 16)
            sp.dma_start(w2[0:H0], a["L0_ffn_W2"].rearrange("e h d -> h e d")).then_inc(w2_in, 16)
            sp.dma_start(w2[H0:H0 + 1], a["L0_ffn_b2"].rearrange("(o e) d -> o e d", o=1)).then_inc(w2_in, 16)
            rows = p.x_grouped.rearrange("(g q) c -> g q c", q=P)
            with sp.Fori(0, XCH // V) as i:
                for v in range(V):
                    g = i * V + v
                    e = expert_of(sp, g)
                    sp.wait_ge(y_done, signalled(g - V))
                    sp.dma_start(x[v][:], rows[bass.ds(g, 1)].rearrange("o q c -> (o q) c")).then_inc(x_in[v], 16)
                    sp.dma_start(w1[v][:], a["L0_ffn_W1"][bass.ds(e, 1)].rearrange("o (k q) h -> q (o k) h", q=P)).then_inc(w_in[v], 16)

        @block.vector
        def _(dve):
            for v in range(V):
                ins = dve.memset(hid[v][H0:H0 + 1, :], 1.0)
            ins.then_inc(ones_ready, 1)
            dve.wait_ge(b1_turned, 1)
            dve.tensor_copy(b1_cols[:], p.bank[7][0:H0, 0:E0]).then_inc(b1_ready, 1)
            dve.wait_ge(b1_ready, 1)
            dve.sem_inc(normed, V)
            with dve.Fori(0, XCH // V) as i:
                for v in range(V):
                    g = i * V + v
                    dve.wait_ge(turned, signalled(g - V))
                    dve.wait_ge(hid_ready, signalled(g - V))
                    p.alone(dve)
                    dve.tensor_copy(b1[v][:], b1_cols[:, bass.ds(expert_of(dve, g), 1)])
                    dve.wait_ge(x_in[v], 16 * (i + 1))
                    dve.tensor_scalar(xn[v][:], x[v][:, 0:D], x[v][:, D:D + 1], x[v][:, D + 3:D + 4],
                                      ALU.subtract, ALU.mult).then_inc(normed, 1)
            chain = Chain(p, dve, steps)
            for g in range(U):
                dve.wait_ge(fetched[g], 16 * U)
                rows = p.rec[:, g * U:(g + 1) * U, 0:D]
                chain(dve.tensor_tensor(rows, rows, back[:, g * U:(g + 1) * U, :], ALU.add))
                chain(moments(p, dve, chain, stats, range(g * U, (g + 1) * U), lambda t: p.rec[:, t, 0:D]))

        @block.tensor
        def _(pe):
            for s in (turned, hid_done, y_done):
                pe.sem_inc(s, V)
            pe.wait_ge(b1_in, 16)
            pe.transpose(p.bank[7][0:H0, 0:E0], b1_rows[:], p.ident[0:E0, 0:E0]).then_inc(b1_turned, 1)
            pe.wait_ge(w2_in, 32)
            pe.wait_ge(ones_ready, 1)
            pe.wait_ge(b1_ready, 1)

            def turn(g, v):
                pe.wait_ge(normed, signalled(g))
                pe.wait_ge(hid_ready, signalled(g - 4))
                for k in range(KD):
                    ins = pe.transpose(p.bank[v % 4][:, k * P:(k + 1) * P], xn[v][:, k * P:(k + 1) * P], p.ident[:])
                ins.then_inc(turned, 1)

            def hidden(g, v, i):
                pe.wait_ge(w_in[v], 16 * (i + 1))
                pe.wait_ge(copied, signalled(g))
                for k in range(KD):
                    ins = pe.matmul(p.bank[v % 4][0:H0, D:D + P], w1[v][:, k, :], xt[v][:, k * P:(k + 1) * P],
                                    start=(k == 0), stop=(k == KD - 1))
                ins.then_inc(hid_done, 1)

            def output(g, v):
                pe.wait_ge(y_ready, signalled(g - 4))
                pe.wait_ge(hid_ready, signalled(g))
                p.alone(pe)
                pe.matmul(p.bank[4 + v % 4][:, 0:D], hid[v][:], w2[:, bass.ds(expert_of(pe, g), 1), :].rearrange("h o d -> h (o d)"),
                          start=True, stop=True).then_inc(y_done, 1)

            with pe.Fori(0, XCH // V) as i:
                for v in range(V + 2):
                    if v < V:
                        turn(i * V + v, v)
                    if 1 <= v <= V:
                        hidden(i * V + (v - 1), v - 1, i)
                    if v >= 2:
                        output(i * V + (v - 2), v - 2)

        @block.scalar
        def _(act):
            for s in (copied, hid_ready, y_ready):
                act.sem_inc(s, V)

            def to_xt(g, v):
                act.wait_ge(hid_done, signalled(g - V))
                act.wait_ge(turned, signalled(g))
                act.activation(xt[v][:], p.bank[v % 4][:, 0:D], ACT.Copy).then_inc(copied, 1)

            def to_hidden(g, v):
                act.wait_ge(y_done, signalled(g - V))
                act.wait_ge(hid_done, signalled(g))
                act.activation(hid[v][0:H0, :], p.bank[v % 4][0:H0, D:D + P], ACT.Relu, bias=b1[v][:, 0:1]).then_inc(hid_ready, 1)

            def to_y(g, v, i):
                act.wait_ge(y_out[v], 16 * (i + 1))
                act.wait_ge(y_done, signalled(g))
                act.activation(y[v][:], p.bank[4 + v % 4][:, 0:D], ACT.Relu).then_inc(y_ready, 1)

            with act.Fori(0, XCH // V) as i:
                for v in range(V + 2):
                    if v < V:
                        to_xt(i * V + v, v)
                    if 1 <= v <= V:
                        to_hidden(i * V + (v - 1), v - 1)
                    if v >= 2:
                        to_y(i * V + (v - 2), v - 2, i)

        @block.gpsimd
        def _(pool):
            rows = p.y_grouped.rearrange("(g q) c -> g q c", q=P)
            for v in range(V):
                pool.dma_start(y[v][:], a["x"][0:P]).then_inc(y_out[v], 16)
            with pool.Fori(0, XCH // V) as i:
                for v in range(V):
                    g = i * V + v
                    pool.wait_ge(y_ready, signalled(g))
                    p.alone(pool)
                    pool.dma_start(rows[bass.ds(g, 1)].rearrange("o q c -> (o q) c"), y[v][:]).then_inc(y_out[v], 16)
            for v in range(V):
                pool.wait_ge(y_out[v], 16 * (XCH // V + 1))
            for t in range(NT):
                pool.indirect_dma_start(out=back[:, t, :], out_offset=None, in_=p.y_grouped[:],
                                        in_offset=bass.IndirectOffsetOnAxis(ap=p.place_i[:, t:t + 1], axis=0)).then_inc(fetched[t // U], 16)


def transform(p: Program):
    nc, a = p.nc, p.a
    GROUPS, QUARTERS, SLOTS_T = RELS // 2, RELS // 4, 7
    QW = 4 * D
    with p.phase() as ctx:
        def sb(n, s, d):
            return ctx.enter_context(nc.sbuf_tensor(n, s, d))

        front = Front(p, ctx, "rel")
        wr = sb("wr", [P, KD, RELS * D], F32)
        quarter_i = sb("quarter_i", [P, NT, QUARTERS], I32)
        trow = [sb(f"trow{s}", [P, QW], F32) for s in range(SLOTS_T)]
        row_i = [sb(f"trow_i{s}", [P, 1], I32) for s in range(SLOTS_T)]
        w_in = [p.sem(f"rel_w_in{m}") for m in range(GROUPS)]
        indices, product_done, evac_v, evac_a, steps = (
            p.sem(f"rel_{x}") for x in ("indices", "product_done", "evac_v", "evac_a", "steps"))
        scattered = [p.sem(f"rel_scattered{s}") for s in range(SLOTS_T)]
        block = ctx.enter_context(nc.Block())

        @block.sync
        def _(sp):
            for m in range(GROUPS):
                for k in range(KD):
                    sp.dma_start(wr[:, k, m * 2 * D:(m + 1) * 2 * D].rearrange("q (r o) -> q r o", o=D),
                                 a["L1_gnn_weight"][2 * m:2 * m + 2, k * P:(k + 1) * P, :].rearrange("r q o -> q r o")).then_inc(w_in[m], 16)

        @block.gpsimd
        def _(pool):
            table = p.transformed.rearrange("(n r) d -> n (r d)", r=4)
            for s in range(SLOTS_T):
                pool.dma_start(row_i[s][:], a["src"][0:P].rearrange("(q o) -> q o", o=1)).then_inc(scattered[s], 16)
            with pool.Fori(0, U) as i:
                for w in range(U * QUARTERS):
                    s = w % SLOTS_T
                    pool.wait_ge(evac_v, done(i * (U * QUARTERS) + w))
                    pool.wait_ge(evac_a, done(i * (U * QUARTERS) + w))
                    p.alone(pool)
                    pool.indirect_dma_start(out=table, out_offset=bass.IndirectOffsetOnAxis(ap=row_i[s][:, 0:1], axis=0),
                                            in_=trow[s][:], in_offset=None).then_inc(scattered[s], 16)
            for s in range(SLOTS_T):
                pool.wait_ge(scattered[s], 16 * (NT * QUARTERS // SLOTS_T + 1))

        @block.vector
        def _(dve):
            chain = Chain(p, dve, steps)
            for q in range(QUARTERS):
                ins = dve.tensor_scalar(quarter_i[:, :, q], p.rec[:, :, C_ID], float(QUARTERS), float(q), ALU.mult, ALU.add)
            ins.then_inc(indices, 1)
            front.moments(dve, chain)
            front.start(dve, front.normed, evac_v)

            def results(i, u):
                for q in range(QUARTERS):
                    w = u * QUARTERS + q
                    dve.wait_ge(product_done, done((i * U + u) * GROUPS + 2 * q))
                    dve.wait_ge(scattered[w % SLOTS_T], 16 * (4 * i + (w // SLOTS_T + 1)))
                    p.alone(dve)
                    dve.tensor_copy(trow[w % SLOTS_T][:, 0:QW // 2], p.bank[4 + (2 * q) % 4][:]).then_inc(evac_v, 1)

            with dve.Fori(0, U) as i:
                for u in range(U + front.LAG):
                    if u < U:
                        front.norm(dve, tile_row(p, i * U + u), i * U + u, u)
                    if u >= front.LAG:
                        results(i, u - front.LAG)

        @block.scalar
        def _(act):
            act.wait_ge(indices, 1)
            front.root(act, known=True)
            front.start(act, front.copied, evac_a)

            def results(i, u):
                for q in range(QUARTERS):
                    w = u * QUARTERS + q
                    act.wait_ge(product_done, done((i * U + u) * GROUPS + 2 * q + 1))
                    act.wait_ge(scattered[w % SLOTS_T], 16 * (4 * i + (w // SLOTS_T + 1)))
                    p.alone(act)
                    act.activation(trow[w % SLOTS_T][:, QW // 2:], p.bank[4 + (2 * q + 1) % 4][:], ACT.Copy)
                    act.activation(row_i[w % SLOTS_T][:], quarter_i[:, bass.ds(i * U + u, 1), q:q + 1].rearrange("q o c -> q (o c)"),
                                   ACT.Copy).then_inc(evac_a, 1)

            with act.Fori(0, U) as i:
                for u in range(U + 1):
                    if u < U:
                        front.copy(act, i * U + u, u, None)
                    if u >= 1:
                        results(i, u - 1)

        @block.tensor
        def _(pe):
            front.start(pe, front.turned, product_done)

            def products(g, u):
                pe.wait_ge(front.copied, done(g))
                for m in range(GROUPS):
                    pe.wait_ge(w_in[m], 16 * KD)
                    pe.wait_ge(evac_a if m % 2 else evac_v, done(g * QUARTERS + m // 2 - 2))
                    for k in range(KD):
                        ins = pe.matmul(p.bank[4 + m % 4][:], front.xt[u][:, k * P:(k + 1) * P],
                                        wr[:, k, m * 2 * D:(m + 1) * 2 * D], start=(k == 0), stop=(k == KD - 1))
                    ins.then_inc(product_done, 1)

            with pe.Fori(0, U) as i:
                for u in range(U):
                    front.turn(pe, i * U + u, u)
                    if u >= 1:
                        products(i * U + (u - 1), u - 1)
                products(i * U + (U - 1), U - 1)


def relations(p: Program):
    nc, a = p.nc, p.a
    with p.phase() as ctx:
        def sb(n, s, d):
            return ctx.enter_context(nc.sbuf_tensor(n, s, d))

        key_i = sb("rel_key_i", [P, NT + 1, WIN], I32)
        weight = sb("rel_weight", [P, NT, WIN], F32)
        idx = [sb(f"rel_idx{s}", [P, COLS1[s]], I32) for s in range(SLOTS1)]
        rows = [sb(f"rel_rows{s}", [P, COLS1[s], D], F32) for s in range(SLOTS1)]
        t_pos = sb("rt_pos", [P, 3], F32)
        t_at_i = sb("rt_at_i", [P, 1], I32)
        t_win = sb("rt_win", [P, 2 * WIN], F32)
        t_idx_i = sb("rt_idx_i", [P, JCOL], I32)
        t_w = sb("rt_w", [P, JCOL], F32)
        stats, moments = sb("rel_stats6", [P, 6], F32), sb("rel_moments", [P, 2], F32)
        steps_m = p.sem("rel_steps_m")
        tables, step = p.sem("rel_tables"), p.sem("rel_step")
        per_slot = lambda name: [p.sem(f"rel_{name}{s}") for s in range(SLOTS1)]
        idx_ready, gathered, used, steps_s = (per_slot(x) for x in ("idx_ready", "gathered", "used", "steps_s"))
        t_at, t_window, t_idx, t_rows, t_done, t_steps, t_begin = (
            p.sem(f"rel_t_{x}") for x in ("at", "window", "idx", "rows", "done", "steps", "begin"))
        block = ctx.enter_context(nc.Block())

        def items(eng, t):
            return eng.value_load(p.items[0:1, bass.ds(t, 1)], min_val=1, max_val=-(-N_EDGES // JCOL))

        def items1(eng, t):
            return eng.value_load(p.items1[0:1, bass.ds(t, 1)], min_val=1, max_val=-(-N_EDGES // COLS1[1]))

        def tail_base(eng, t):
            return eng.value_load(p.tails[0:1, bass.ds(t, 1)], min_val=0, max_val=N_EDGES)

        @block.gpsimd
        def _(pool):
            pool.wait_ge(tables, 1)
            with pool.Fori(0, NT) as t:
                n, n1 = items(pool, t), items1(pool, t)

                def gather(s):
                    pool.wait_ge(idx_ready[s], t + 1)
                    pool.wait_ge(used[s], t + 1)
                    p.alone(pool)
                    for j in range(COLS1[s]):
                        pool.indirect_dma_start(out=rows[s][:, j, :], out_offset=None, in_=p.transformed[:],
                                                in_offset=bass.IndirectOffsetOnAxis(ap=idx[s][:, j:j + 1], axis=0))\
                            .then_inc(gathered[s], 16)

                in_order(pool, n1, gather, slots=SLOTS1)
                with pool.If(n > SLOTS):
                    c0 = tail_base(pool, t)
                    with pool.Fori(SLOTS, n) as k:
                        c = c0 + k - SLOTS
                        pool.wait_ge(t_at, c + 1)
                        p.alone(pool)
                        pool.indirect_dma_start(out=t_win[:], out_offset=None, in_=p.windows[:],
                                                in_offset=bass.IndirectOffsetOnAxis(ap=t_at_i[:, 0:1], axis=0)).then_inc(t_window, 16)
                        pool.wait_ge(t_idx, c + 1)
                        p.alone(pool)
                        for j in range(JCOL):
                            pool.indirect_dma_start(out=rows[0][:, j, :], out_offset=None, in_=p.transformed[:],
                                                    in_offset=bass.IndirectOffsetOnAxis(ap=t_idx_i[:, j:j + 1], axis=0))\
                                .then_inc(t_rows, 16)
                        pool.wait_ge(t_done, c + 1)
                        p.alone(pool)

        @block.scalar
        def _(act):
            act.wait_ge(tables, 1)
            for s in range(SLOTS1):
                act.activation(idx[s][:], key_i[:, 0, AT1[s]:AT1[s] + COLS1[s]], ACT.Copy).then_inc(idx_ready[s], 1)
            with act.Fori(0, NT) as t:
                n1 = items1(act, t)

                def item(s):
                    act.wait_ge(gathered[s], 16 * COLS1[s] * (t + 1))
                    p.alone(act)
                    act.activation(idx[s][:], key_i[:, bass.ds(t + 1, 1), AT1[s]:AT1[s] + COLS1[s]].rearrange("q o j -> q (o j)"),
                                   ACT.Copy).then_inc(idx_ready[s], 1)

                in_order(act, n1, item, slots=SLOTS1)

        @block.vector
        def _(dve):
            chain = Chain(p, dve, step)
            chain(dve.tensor_copy(key_i[:, 0:NT, :], p.win[:, :, 0:WIN]))
            chain(dve.memset(key_i[:, NT, :], 0))
            chain(dve.tensor_tensor(weight[:], spread(p.count[:, 0:WIN], 1, [P, NT, WIN]),
                                    p.rec[:, :, C_DEG:C_DEG + 1].broadcast_to([P, NT, WIN]), ALU.is_lt))
            dve.tensor_tensor(weight[:], weight[:], p.win[:, :, WIN:2 * WIN], ALU.mult).then_inc(tables, 1)
            dve.wait_ge(tables, 1)
            for s in range(SLOTS1):
                dve.sem_inc(used[s], 1)
            chain_s = [Chain(p, dve, x) for x in steps_s]
            chain_k, chain_m = Chain(p, dve, t_steps), Chain(p, dve, steps_m)
            TAIL_STEPS = 7

            def add(t, s, columns, w, chain, finished):
                x = p.rec[:, bass.ds(t, 1), 0:D].rearrange("q o d -> q (o d)")
                for j in range(columns):
                    ins = dve.scalar_tensor_tensor(x, rows[s][:, j, :], w(j), x, ALU.mult, ALU.add)
                    if j < columns - 1:
                        chain(ins)
                    else:
                        ins.then_inc(finished, 1)

            with dve.Fori(0, NT) as t:
                n, n1 = items(dve, t), items1(dve, t)

                def item(s):
                    chain_s[s].at(t * (COLS1[s] - 1))
                    dve.wait_ge(gathered[s], 16 * COLS1[s] * (t + 1))
                    add(t, s, COLS1[s], lambda j: weight[:, bass.ds(t, 1), AT1[s] + j:AT1[s] + j + 1].rearrange("q o c -> q (o c)"),
                        chain_s[s], used[s])
                    dve.wait_ge(used[s], t + 2)
                    p.alone(dve)

                in_order(dve, n1, item, slots=SLOTS1)
                with dve.If(n > SLOTS):
                    c0 = tail_base(dve, t)
                    dve.tensor_scalar(t_pos[:, 0:1], tile_row(p, t, C_START, C_START + 1), float(WIN), None, ALU.add)
                    dve.tensor_scalar(t_pos[:, 1:2], tile_row(p, t, C_DEG, C_DEG + 1), -float(WIN), None, ALU.add).then_inc(t_begin, 1)
                    dve.wait_ge(t_begin, t + 1)
                    p.alone(dve)
                    with dve.Fori(SLOTS, n) as k:
                        c = c0 + k - SLOTS
                        chain_k.at(c * TAIL_STEPS)
                        dve.tensor_scalar(t_at_i[:], t_pos[:, 0:1], float(N_EDGES), None, ALU.min).then_inc(t_at, 1)
                        dve.wait_ge(t_window, 16 * (c + 1))
                        p.alone(dve)
                        dve.tensor_copy(t_idx_i[:], t_win[:, 0:JCOL]).then_inc(t_idx, 1)
                        chain_k(dve.tensor_scalar(t_w[:], p.count[:, 0:JCOL], t_pos[:, 1:2], None, ALU.is_lt))
                        chain_k(dve.tensor_tensor(t_w[:], t_w[:], t_win[:, WIN:WIN + JCOL], ALU.mult))
                        dve.wait_ge(t_rows, 16 * JCOL * (c + 1))
                        add(t, 0, JCOL, lambda j: t_w[:, j:j + 1], chain_k, t_done)
                        dve.wait_ge(t_done, c + 1)
                        p.alone(dve)
                        chain_k(dve.tensor_scalar(t_pos[:, 0:1], t_pos[:, 0:1], float(JCOL), None, ALU.add))
                        chain_k(dve.tensor_scalar(t_pos[:, 1:2], t_pos[:, 1:2], -float(JCOL), None, ALU.add))
                        assert chain_k.n == TAIL_STEPS, chain_k.n
                chain_m.at(t * 3)
                chain_m(dve.bn_stats(stats[:], tile_row(p, t)), True)
                chain_m(dve.bn_aggr(moments[:], stats[:]), True)
                chain_m(dve.tensor_copy(p.ms[:, bass.ds(t, 1), 0:2].rearrange("q o c -> q (o c)"), moments[:]))
                assert chain_m.n == 3


def choose_two(p: Program):
    nc, a = p.nc, p.a
    with p.phase() as ctx:
        def sb(n, s, d):
            return ctx.enter_context(nc.sbuf_tensor(n, s, d))

        weight = sb("weight2", [P, NT], F32)
        scaled = sb("scaled2", [P, NT], F32)
        means = sb("means2", [P, 1], F32)
        sums = sb("col_sums", [P, KD], F32)
        wr = sb("wr1", [P, KD, E1], F32)
        br = sb("br1", [1, E1], F32)
        row = sb("row1", [1, 10, E1], F32)
        one = sb("one1", [1, 12], F32)
        rooted, weight_ready, means_ready, w_in, summed, mean_ready, logits_done, steps, exp_ready, exp_done, pair_ready, spread_done = (
            p.sem(f"two_{x}") for x in ("rooted", "weight_ready", "means_ready", "w_in", "summed", "mean_ready", "logits_done", "steps",
                                        "exp_ready", "exp_done", "pair_ready", "spread_done"))
        block = ctx.enter_context(nc.Block())
        logit, e, rw, s, eq, rev, s2, q = (row[:, n, :] for n in range(8))
        pair = one[:, 10:12]

        @block.sync
        def _(sp):
            sp.dma_start(wr[:], a["L1_ffn_Wr"].rearrange("(k q) e -> q k e", q=P)).then_inc(w_in, 16)
            sp.dma_start(br[:], a["L1_ffn_br"].rearrange("(o e) -> o e", o=1)).then_inc(w_in, 16)

        @block.tensor
        def _(pe):
            pe.wait_ge(weight_ready, 1)
            for t in range(NT):
                for k in range(KD):
                    ins = pe.matmul(p.bank[k][:, 0:1], p.rec[:, t, k * P:(k + 1) * P], weight[:, t:t + 1],
                                    start=(t == 0), stop=(t == NT - 1))
            ins.then_inc(summed, 1)
            pe.wait_ge(means_ready, 1)
            pe.matmul(p.bank[4][:, 0:1], p.ones[:], means[:], start=True, stop=True).then_inc(summed, 1)
            pe.wait_ge(w_in, 32)
            pe.wait_ge(mean_ready, 1)
            for k in range(KD):
                ins = pe.matmul(p.bank[2][0:1, 0:E1], sums[:, k:k + 1], wr[:, k, :], start=(k == 0), stop=(k == KD - 1))
            ins.then_inc(logits_done, 1)
            pe.wait_ge(pair_ready, 1)
            pe.matmul(p.bank[3][:, 0:2], p.ones[0:1, :], pair, start=True, stop=True).then_inc(spread_done, 1)

        @block.scalar
        def _(act):
            act.activation(p.ms[:, :, 2], p.ms[:, :, 1], ACT.Sqrt, bias=p.eps[:, 0:1]).then_inc(rooted, 1)
            for n, (out, in_) in enumerate(((e, logit), (s, q), (one[:, 6:7], one[:, 5:6]))):
                act.wait_ge(exp_ready, n + 1)
                act.activation(out, in_, ACT.Exp).then_inc(exp_done, 1)

        @block.vector
        def _(dve):
            chain = Chain(p, dve, steps)
            chain(dve.tensor_scalar(weight[:], p.rec[:, :, C_ID], float(N_NODES), None, ALU.is_lt))
            dve.wait_ge(rooted, 1)
            chain(dve.reciprocal(p.ms[:, :, 3], p.ms[:, :, 2]))
            dve.tensor_tensor(weight[:], weight[:], p.ms[:, :, 3], ALU.mult).then_inc(weight_ready, 1)
            dve.wait_ge(weight_ready, 1)
            chain(dve.tensor_tensor(scaled[:], weight[:], p.ms[:, :, 0], ALU.mult))
            dve.tensor_reduce(means[:], scaled[:], AX, ALU.add).then_inc(means_ready, 1)
            dve.wait_ge(summed, 2)
            chain(dve.tensor_copy(means[:], p.bank[4][:, 0:1]))
            for k in range(KD):
                ins = dve.tensor_tensor(sums[:, k:k + 1], p.bank[k][:, 0:1], means[:], ALU.subtract)
            chain(ins)
            dve.tensor_scalar(sums[:], sums[:], 1.0 / N_NODES, None, ALU.mult).then_inc(mean_ready, 1)
            dve.wait_ge(w_in, 32)
            dve.wait_ge(logits_done, 1)

            def softmax(n, x, out):
                chain(dve.tensor_reduce(one[:, 0:1], x, AX, ALU.max))
                dve.tensor_scalar(x, x, one[:, 0:1], None, ALU.subtract).then_inc(exp_ready, 1)
                dve.wait_ge(exp_done, n)
                chain(dve.tensor_reduce(one[:, 1:2], out, AX, ALU.add))
                chain(dve.reciprocal(one[:, 2:3], one[:, 1:2]))

            chain(dve.tensor_tensor(logit, p.bank[2][0:1, 0:E1], br[:], ALU.add))
            softmax(1, logit, e)
            chain(dve.tensor_scalar(rw, e, one[:, 2:3], None, ALU.mult))
            chain(dve.tensor_scalar(q, rw, CAPACITY / N_NODES, None, ALU.min))
            softmax(2, q, s)
            chain(dve.tensor_scalar(s, s, one[:, 2:3], None, ALU.mult))
            chain(dve.tensor_scalar(rev, p.count[0:1, 0:E1], -1.0, float(E1), ALU.mult, ALU.add))

            def largest(x, value, at):
                chain(dve.tensor_reduce(value, x, AX, ALU.max))
                chain(dve.tensor_scalar(eq, x, value, None, ALU.is_ge))
                chain(dve.tensor_tensor(eq, eq, rev, ALU.mult))
                chain(dve.tensor_reduce(at, eq, AX, ALU.max))

            largest(s, one[:, 3:4], one[:, 8:9])
            chain(dve.tensor_scalar(s2, rev, one[:, 8:9], -2.0, ALU.is_equal, ALU.mult))
            chain(dve.tensor_tensor(s2, s2, s, ALU.add))
            largest(s2, one[:, 4:5], one[:, 9:10])
            chain(dve.tensor_scalar(one[:, 8:10], one[:, 8:10], -1.0, float(E1), ALU.mult, ALU.add))
            chain(dve.tensor_copy(p.two_i[:], one[:, 8:10]))
            dve.tensor_tensor(one[:, 5:6], one[:, 4:5], one[:, 3:4], ALU.subtract).then_inc(exp_ready, 1)
            dve.wait_ge(exp_done, 3)
            chain(dve.tensor_scalar(one[:, 7:8], one[:, 6:7], 1.0, None, ALU.add))
            chain(dve.reciprocal(pair[:, 0:1], one[:, 7:8]))
            dve.tensor_tensor(pair[:, 1:2], pair[:, 0:1], one[:, 6:7], ALU.mult).then_inc(pair_ready, 1)
            dve.wait_ge(spread_done, 1)
            chain(dve.tensor_copy(p.two_w[:], p.bank[3][:, 0:2]))


def feed_forward(p: Program):
    nc, a = p.nc, p.a
    G, PAIRS = 4, NT // 8
    assert PAIRS * 2 * G + 1 == NT
    F = H1 // P
    EF = 2 * F
    with p.phase() as ctx:
        def sb(n, s, d):
            return ctx.enter_context(nc.sbuf_tensor(n, s, d))

        w1 = sb("ff_w1", [P, 2, KD, H1], F32)
        w2 = sb("ff_w2", [P, EF, D], F32)
        b1_rows = sb("ff_b1_rows", [EF, P], F32)
        b1 = sb("ff_b1", [P, EF], F32)
        b2 = sb("ff_b2", [P, 2, D], F32)
        gb = sb("ff_gb", [P, 2, D], F32)
        xg = [sb(f"ff_xg{s}", [P, G, D], F32) for s in range(2)]
        xt = [sb(f"ff_xt{s}", [P, KD, G * P], F32) for s in range(2)]
        gt = [sb(f"ff_gt{s}", [P, EF, G * P], F32) for s in range(2)]
        y = [[sb(f"ff_y{n}{j}", [P, D], F32) for j in range(G)] for n in range(2)]
        z = [sb(f"ff_z{j}", [P, D], F32) for j in range(G)]
        stats = sb("ff_stats", [P, G, 6], F32)
        ms = [sb(f"ff_ms{n}", [P, G, 4], F32) for n in range(2)]
        at = [sb(f"ff_at{j}", [P, 1], I32) for j in range(G)]
        w_in, scaled, normed, turned, copied, hidden, gelued, out_done, taken, varied, rooted, finished, steps, setup = (
            p.sem(f"ff_{x}") for x in ("w_in", "scaled", "normed", "turned", "copied", "hidden", "gelued",
                                       "out_done", "taken", "varied", "rooted", "finished", "steps", "setup"))
        steps_b = p.sem("ff_steps_b")
        b1_turned, b1_ready = p.sem("ff_b1_turned"), p.sem("ff_b1_ready")
        stored = [p.sem(f"ff_stored{j}") for j in range(G)]
        block = ctx.enter_context(nc.Block())

        END = 2 * PAIRS

        @block.sync
        def _(sp):
            for n in range(2):
                e = sp.value_load(p.two_i[0:1, n:n + 1], min_val=0, max_val=E1 - 1)
                sp.dma_start(w1[:, n], a["L1_ffn_W1"][bass.ds(e, 1)].rearrange("o (k q) f -> q (o k) f", q=P)).then_inc(w_in, 16)
                sp.dma_start(w2[:, n * F:(n + 1) * F], a["L1_ffn_W2"][bass.ds(e, 1)].rearrange("o (f q) d -> q (o f) d", q=P)).then_inc(w_in, 16)
                sp.dma_start(b1_rows[n * F:(n + 1) * F, :], a["L1_ffn_b1"][bass.ds(e, 1)].rearrange("o (f q) -> (o f) q", q=P)).then_inc(w_in, 16)
                sp.dma_start(b2[:, n], a["L1_ffn_b2"][bass.ds(e, 1)].broadcast_to([P, D])).then_inc(w_in, 16)
            for n, name in enumerate(("L1_ffn_gamma", "L1_ffn_beta")):
                sp.dma_start(gb[:, n], bass.AP(tensor=a[name].tensor, offset=0, ap=[[0, P], [1, D]])).then_inc(w_in, 16)

        @block.tensor
        def _(pe):
            for s in (turned, hidden, out_done):
                pe.sem_inc(s, U)
            pe.wait_ge(w_in, 16 * 10)
            pe.transpose(p.bank[6][:, 0:EF], b1_rows[:], p.ident[0:EF, 0:EF]).then_inc(b1_turned, 1)

            def into(g, slot, tiles):
                pe.wait_ge(normed, done(g))
                for j in range(tiles):
                    c = g * G + j
                    pe.wait_ge(copied, done(c - 2))
                    for k in range(KD):
                        ins = pe.transpose(p.bank[j % 2][:, k * P:(k + 1) * P], xg[slot][:, j, k * P:(k + 1) * P], p.ident[:])
                    ins.then_inc(turned, 1)
                pe.wait_ge(copied, done(g * G + (tiles - 1)))
                for ef in range(EF):
                    pe.wait_ge(gelued, done(g * EF + ef - 4))
                    for k in range(KD):
                        ins = pe.matmul(p.bank[2 + ef % 4][:, 0:tiles * P], w1[:, ef // F, k, (ef % F) * P:(ef % F + 1) * P],
                                        xt[slot][:, k, 0:tiles * P], start=(k == 0), stop=(k == KD - 1))
                    ins.then_inc(hidden, 1)

            def outof(g, slot, tiles):
                pe.wait_ge(gelued, done(g * EF + (EF - 1)))
                for j in range(tiles):
                    pe.wait_ge(taken, done(g * G + j - 2))
                    for ef in range(EF):
                        ins = pe.matmul(p.bank[6 + j % 2][:, 0:D], gt[slot][:, ef, j * P:(j + 1) * P], w2[:, ef, :],
                                        start=(ef == 0), stop=(ef == EF - 1))
                    ins.then_inc(out_done, 1)

            pe.wait_ge(scaled, EF)
            pe.wait_ge(b1_ready, 1)
            into(0, 0, G)
            with pe.Fori(0, PAIRS - 1) as i:
                for n in range(2):
                    into(i * 2 + (n + 1), 1 - n, G)
                    outof(i * 2 + n, n, G)
            into(END - 1, 1, G)
            outof(END - 2, 0, G)
            into(END, 0, 1)
            outof(END - 1, 1, G)
            outof(END, 0, 1)

        @block.scalar
        def _(act):
            for s in (copied, gelued, rooted):
                act.sem_inc(s, U)
            act.wait_ge(b1_ready, 1)

            def group(g, slot, tiles):
                for j in range(tiles):
                    act.wait_ge(turned, done(g * G + j))
                    act.activation(xt[slot][:, :, j * P:(j + 1) * P], p.bank[j % 2][:, 0:D].rearrange("q (k c) -> q k c", c=P),
                                   ACT.Copy).then_inc(copied, 1)
                act.wait_ge(out_done, done(g * G - 2 * G + (G - 1)))
                p.alone(act)
                for ef in range(EF):
                    act.wait_ge(hidden, done(g * EF + ef))
                    act.activation(gt[slot][:, ef, 0:tiles * P], p.bank[2 + ef % 4][:, 0:tiles * P], ACT.Gelu,
                                   bias=b1[:, ef:ef + 1]).then_inc(gelued, 1)

            def roots(g, n, tiles):
                act.wait_ge(varied, done(g))
                act.activation(ms[n][:, 0:tiles, 2], ms[n][:, 0:tiles, 1], ACT.Sqrt, bias=p.eps[:, 0:1]).then_inc(rooted, 1)

            group(0, 0, G)
            group(1, 1, G)
            with act.Fori(0, PAIRS - 1) as i:
                for n in range(2):
                    group(i * 2 + (n + 2), n, G)
                    roots(i * 2 + n, n, G)
            group(END, 0, 1)
            roots(END - 2, 0, G)
            roots(END - 1, 1, G)
            roots(END, 0, 1)

        @block.gpsimd
        def _(pool):
            def group(g, tiles):
                for j in range(tiles):
                    pool.wait_ge(finished, done(g * G + j))
                    p.alone(pool)
                    pool.indirect_dma_start(out=p.a["out"], out_offset=bass.IndirectOffsetOnAxis(ap=at[j][:, 0:1], axis=0),
                                            in_=z[j][:], in_offset=None).then_inc(stored[j], 16)

            for j in range(G):
                pool.dma_start(at[j][:], a["src"][0:P].rearrange("(q o) -> q o", o=1)).then_inc(stored[j], 16)
            with pool.Fori(0, PAIRS) as i:
                group(i * 2, G)
                group(i * 2 + 1, G)
            group(END, 1)
            for j in range(G):
                pool.wait_ge(stored[j], 16 * (1 + 2 * PAIRS + (j == 0)))

        @block.vector
        def _(dve):
            first = Chain(p, dve, setup)
            for s in (normed, taken, varied, finished):
                dve.sem_inc(s, U)
            dve.wait_ge(w_in, 16 * 10)
            dve.wait_ge(b1_turned, 1)
            dve.tensor_copy(b1[:], p.bank[6][:, 0:EF]).then_inc(b1_ready, 1)
            for ef in range(EF):
                dve.tensor_scalar(w2[:, ef, :], w2[:, ef, :], p.two_w[:, ef // F:ef // F + 1], None, ALU.mult).then_inc(scaled, 1)
            first(dve.tensor_scalar(b2[:, 0, :], b2[:, 0, :], p.two_w[:, 0:1], None, ALU.mult))
            first(dve.scalar_tensor_tensor(b2[:, 0, :], b2[:, 1, :], p.two_w[:, 1:2], b2[:, 0, :], ALU.mult, ALU.add))

            def moment(c, n):
                return p.ms[:, bass.ds(c, 1), n:n + 1].rearrange("q o c -> q (o c)")

            def norm(g, slot, tiles):
                dve.wait_ge(turned, done(g * G - 2 * G + (G - 1)))
                p.alone(dve)
                for j in range(tiles):
                    c = g * G + j
                    ins = dve.tensor_scalar(xg[slot][:, j, :], tile_row(p, c), moment(c, 0), moment(c, 3),
                                            ALU.subtract, ALU.mult)
                ins.then_inc(normed, 1)
                dve.wait_ge(normed, done(g))

            chain_a, chain_b = Chain(p, dve, steps), Chain(p, dve, steps_b)
            KA, KB = 1 + 2 * G, 4

            def inner(g, n, tiles):
                chain_a.at(g * KA)
                dve.wait_ge(finished, done(g * G - G - 1))
                dve.wait_ge(varied, done(g - 1))
                p.alone(dve)
                for j in range(tiles):
                    c = g * G + j
                    ins = dve.tensor_scalar(y[n][j][:], tile_row(p, c), moment(c, 0), moment(c, 3), ALU.subtract, ALU.mult)
                chain_a(ins, True)
                for j in range(tiles):
                    dve.wait_ge(out_done, done(g * G + j))
                    p.alone(dve)
                    dve.tensor_tensor(y[n][j][:], p.bank[6 + j % 2][:, 0:D], y[n][j][:], ALU.add).then_inc(taken, 1)
                    dve.wait_ge(taken, done(g * G + j))
                    p.alone(dve)
                    chain_a(dve.tensor_tensor(y[n][j][:], y[n][j][:], b2[:, 0, :], ALU.add), True)
                    chain_a(dve.bn_stats(stats[:, j, :], y[n][j][:]), True)
                    ins = dve.bn_aggr(ms[n][:, j, 0:2], stats[:, j, :])
                ins.then_inc(varied, 1)
                assert chain_a.n == 1 + 2 * tiles

            def outer(g, n, tiles):
                chain_b.at(g * KB)
                for j in range(tiles):
                    dve.wait_ge(stored[j], 16 * (g + 1))
                    p.alone(dve)
                    dve.tensor_copy(at[j][:], p.id_i[:, bass.ds(g * G + j, 1)])
                dve.wait_ge(rooted, done(g))
                chain_b(dve.reciprocal(ms[n][:, 0:tiles, 3], ms[n][:, 0:tiles, 2]), True)
                for j in range(tiles):
                    ins = dve.tensor_scalar(y[n][j][:], y[n][j][:], ms[n][:, j, 0:1], ms[n][:, j, 3:4], ALU.subtract, ALU.mult)
                chain_b(ins, True)
                for k, op in enumerate((ALU.mult, ALU.add)):
                    for j in range(tiles):
                        ins = dve.tensor_tensor(y[n][j][:], y[n][j][:], gb[:, k, :], op)
                    chain_b(ins, True)
                for j in range(tiles):
                    dve.tensor_tensor(z[j][:], y[n][j][:], tile_row(p, g * G + j), ALU.add).then_inc(finished, 1)
                assert chain_b.n == KB

            norm(0, 0, G)
            norm(1, 1, G)
            norm(2, 0, G)
            inner(0, 0, G)
            with dve.Fori(0, PAIRS - 2) as i:
                for n in (1, 2):
                    g = i * 2 + n
                    norm(g + 2, n % 2, G)
                    inner(g, n % 2, G)
                    outer(g - 1, 1 - n % 2, G)
            for g in range(END - 3, END + 1):
                if g + 2 <= END:
                    norm(g + 2, g % 2, G if g + 2 < END else 1)
                inner(g, g % 2, G if g < END else 1)
                outer(g - 1, 1 - g % 2, G)
            outer(END, END % 2, 1)


def build(nc, a):
    with ExitStack() as ctx:
        p = Program(nc, ctx, a)
        search_and_project(p)
        attention(p)
        route(p)
        experts(p)
        transform(p)
        relations(p)
        choose_two(p)
        feed_forward(p)



_INS = ["x", "src", "dst", "edge_type_16", "edge_weight1", "L0_gnn_W", "L0_gnn_att_src", "L0_gnn_att_dst", "L0_gnn_bias",
        "L0_ffn_router_w", "L0_ffn_router_b", "L0_ffn_W1", "L0_ffn_b1", "L0_ffn_W2", "L0_ffn_b2", "L1_gnn_weight",
        "L1_ffn_Wr", "L1_ffn_br", "L1_ffn_W1", "L1_ffn_b1", "L1_ffn_W2", "L1_ffn_b2", "L1_ffn_gamma", "L1_ffn_beta"]


def layout(inputs):
    import numpy as np
    arrays = {n: np.ascontiguousarray(inputs[n]) for n in _INS}
    arrays["x"] = np.pad(arrays["x"], ((0, NP - N_NODES), (0, 0)))
    arrays["dst"] = np.pad(arrays["dst"], (0, CG * P * P - N_EDGES), constant_values=2 * NP)
    for n in ("src", "edge_type_16"):
        arrays[n] = np.pad(arrays[n], (0, EP + WIN - N_EDGES))
    arrays["edge_weight1"] = np.pad(arrays["edge_weight1"].reshape(-1), (0, EP + WIN - N_EDGES))
    return arrays


def kernel(**inputs):
    import numpy as np
    import concourse.bacc as bacc
    from concourse.bass_utils import run_bass_kernel_spmd

    arrays = layout(inputs)
    nc = bacc.Bacc("TRN2", target_bir_lowering=False, num_devices=1)
    aps = {n: nc.dram_tensor(n, v.shape, mybir.dt.from_np(v.dtype), kind="ExternalInput").ap() for n, v in arrays.items()}
    aps["out"] = nc.dram_tensor("out", (NP, D), F32, kind="ExternalOutput").ap()
    build(nc, aps)
    r = run_bass_kernel_spmd(nc, [arrays], core_ids=[0])
    return r.results[0]["out"][:N_NODES]
```
